# Optimizing a Trainium2 kernel written in Bass

```python
import numpy as np
import jax
import jax.numpy as jnp

def _softmax(x, axis=-1):
    return jax.nn.softmax(x, axis=axis)

def _gelu(x):
    return jax.nn.gelu(x, approximate=True)

def _silu(x):
    return jax.nn.silu(x)

def _sigmoid(x):
    return jax.nn.sigmoid(x)

def _layernorm(x, axis=-1, eps=1e-05):
    m = jnp.mean(x, axis=axis, keepdims=True)
    v = jnp.var(x, axis=axis, keepdims=True)
    return (x - m) / jnp.sqrt(v + eps)

def _scatter_add(tgt, idx, src, axis=0):
    return tgt.at[idx].add(src)

def _segment_sum(src, seg, n):
    return jax.ops.segment_sum(src, seg, n)
kernel_name = 'mk_gnn_ffn_d2_gnn_r8_cf434e'

def setup_inputs(seed: int=0):
    np.random.seed(seed)
    _w = jnp.asarray

    def _rec_inputs():
        import jax
        import jax.numpy as jnp
        _gk = jax.random.key(seed)
        x = -0.0002117 + 1 * jax.random.normal(jax.random.fold_in(_gk, 1), (6250, 256), jnp.float32)
        _s = jax.random.randint(jax.random.fold_in(_gk, 2), (50000,), 0, 6250, jnp.int32)
        _d = jax.random.randint(jax.random.fold_in(_gk, 3), (50000,), 0, 6250, jnp.int32)
        _loop = jnp.arange(6250, dtype=jnp.int32)
        src = jnp.concatenate([_s, _d, _loop])
        dst = jnp.concatenate([_d, _s, _loop])
        _o = jnp.argsort(dst, stable=True)
        src = src[_o]
        dst = dst[_o]
        edge_attr_2 = jax.random.uniform(jax.random.fold_in(_gk, 11), (106250, 2), jnp.float32, 0.0, 1)
        return (x, src, dst, edge_attr_2)
    x, src, dst, edge_attr_2 = _rec_inputs()

    def _L0_gnn_setup():
        import jax, jax.numpy as jnp
        import numpy as np
        N_NODES = 12500
        N_EDGES = 200000
        IN_FEATS = 256
        OUT_FEATS = 64
        NUM_HEADS = 4
        key = jax.random.key(seed)
        k_h, k_adj, k_dir, k_wf, k_wr, k_af = jax.random.split(key, 6)
        h = jax.random.normal(k_h, (N_NODES, IN_FEATS), dtype=jnp.float32)
        adj = jax.random.randint(k_adj, (2, N_EDGES), 0, N_NODES, dtype=jnp.int64)
        bit = jax.random.randint(k_dir, (N_EDGES,), 0, 2).astype(jnp.float32)
        direction = jnp.stack([bit, 1.0 - bit], axis=1)
        s_w = float(np.sqrt(6.0 / (IN_FEATS + OUT_FEATS)))
        s_a = float(np.sqrt(6.0 / (NUM_HEADS + OUT_FEATS)))
        W_forward = jax.random.uniform(k_wf, (OUT_FEATS, IN_FEATS), jnp.float32, -s_w, s_w)
        W_reverse = jax.random.uniform(k_wr, (OUT_FEATS, IN_FEATS), jnp.float32, -s_w, s_w)
        attn_forward = jax.random.uniform(k_af, (1, NUM_HEADS, OUT_FEATS), jnp.float32, -s_a, s_a)
        return {'h': h, 'adj': adj, 'direction': direction, 'W_forward': W_forward, 'W_reverse': W_reverse, 'attn_forward': attn_forward}
    _L0_gnn_all = _L0_gnn_setup()
    _L0_gnn_in = {k: v for k, v in _L0_gnn_all.items() if k in ('W_forward', 'W_reverse', 'attn_forward')}
    del _L0_gnn_all

    def _L0_ffn_setup():
        import jax, jax.numpy as jnp
        import numpy as np
        B, N, D = (16, 512, 256)
        NUM_EXPERTS, TOP_K, HEADS = (4, 2, 4)
        N_EDGES = 131072
        LN_EPS = 1e-05

        def _layernorm(x, g, b):
            mu = x.mean(-1, keepdims=True)
            var = ((x - mu) ** 2).mean(-1, keepdims=True)
            return (x - mu) * jax.lax.rsqrt(var + LN_EPS) * g + b

        def _forward(x, edge_index, W_gat, att_src, att_dst, b_gat, ln_gamma, ln_beta, W1, b1, W2, b2):
            Bc, Nc, Dc = x.shape
            M = Bc * Nc
            x_flat = x.reshape(M, Dc)
            h = (x_flat @ W_gat).reshape(M, HEADS, NUM_EXPERTS)
            loops = jnp.arange(M, dtype=edge_index.dtype)
            src = jnp.concatenate([edge_index[0], loops])
            dst = jnp.concatenate([edge_index[1], loops])
            a_src = (h * att_src).sum(-1)
            a_dst = (h * att_dst).sum(-1)
            e = jax.nn.leaky_relu(a_src[src] + a_dst[dst], negative_slope=0.2)
            e_max = jax.ops.segment_max(e, dst, num_segments=M)
            ee = jnp.exp(e - e_max[dst])
            denom = jax.ops.segment_sum(ee, dst, num_segments=M)
            alpha = ee / (denom[dst] + 1e-16)
            msg = h[src] * alpha[:, :, None]
            agg = jax.ops.segment_sum(msg, dst, num_segments=M).reshape(M, HEADS * NUM_EXPERTS) + b_gat
            scores = _layernorm(agg, ln_gamma, ln_beta).reshape(M, HEADS, NUM_EXPERTS).mean(1)
            scores = scores.reshape(Bc, Nc, NUM_EXPERTS)
            topk_s, topk_i = jax.lax.top_k(scores, TOP_K)
            w = jax.nn.softmax(topk_s, axis=-1)
            out = jnp.zeros_like(x)
            for ei in range(NUM_EXPERTS):
                g = jnp.where(topk_i == ei, w, 0.0).sum(-1)
                hh = jax.nn.gelu(x @ W1[ei] + b1[ei], approximate=False)
                out = out + g[..., None] * (hh @ W2[ei] + b2[ei])
            return out
        key = jax.random.key(seed)
        ks = jax.random.split(key, 8)
        s = 0.05
        return {'x': jax.random.normal(ks[0], (B, N, D), jnp.float32), 'W_gat': jax.random.normal(ks[1], (D, HEADS * NUM_EXPERTS), jnp.float32) * s, 'att_src': jax.random.normal(ks[2], (HEADS, NUM_EXPERTS), jnp.float32) * s, 'att_dst': jax.random.normal(ks[3], (HEADS, NUM_EXPERTS), jnp.float32) * s, 'b_gat': jnp.zeros((HEADS * NUM_EXPERTS,), jnp.float32), 'ln_gamma': jnp.ones((HEADS * NUM_EXPERTS,), jnp.float32), 'ln_beta': jnp.zeros((HEADS * NUM_EXPERTS,), jnp.float32), 'W1': jax.random.normal(ks[4], (NUM_EXPERTS, D, 2 * D), jnp.float32) * s, 'b1': jnp.zeros((NUM_EXPERTS, 2 * D), jnp.float32), 'W2': jax.random.normal(ks[5], (NUM_EXPERTS, 2 * D, D), jnp.float32) * s, 'b2': jnp.zeros((NUM_EXPERTS, D), jnp.float32), 'edge_index': jax.random.randint(ks[6], (2, N_EDGES), 0, B * N, jnp.int32)}
    _L0_ffn_all = _L0_ffn_setup()
    _L0_ffn_in = {k: v for k, v in _L0_ffn_all.items() if k in ('W_gat', 'att_src', 'att_dst', 'b_gat', 'ln_gamma', 'ln_beta', 'W1', 'b1', 'W2', 'b2', 'edge_index')}
    del _L0_ffn_all

    def _L1_gnn_setup():
        import jax, jax.numpy as jnp
        import numpy as np
        BN_EPS = 1e-05
        key = jax.random.key(seed)
        k1, k2, k3 = jax.random.split(key, 3)
        N, F, H, E = (6250, 256, 256, 200000)
        x = jax.random.normal(k1, (N, F), dtype=jnp.float32)
        edge_index = jax.random.randint(k2, (2, E), 0, N, dtype=jnp.int64)
        lim = 1.0 / np.sqrt(F)
        W = jax.random.uniform(k3, (H, F), dtype=jnp.float32, minval=-lim, maxval=lim)
        b = jnp.zeros((H,), dtype=jnp.float32)
        bn_w = jnp.ones((H,), dtype=jnp.float32)
        bn_b = jnp.zeros((H,), dtype=jnp.float32)
        return {'x': x, 'edge_index': edge_index, 'W': W, 'b': b, 'bn_w': bn_w, 'bn_b': bn_b}
    _L1_gnn_all = _L1_gnn_setup()
    _L1_gnn_in = {k: v for k, v in _L1_gnn_all.items() if k in ('W', 'b', 'bn_w', 'bn_b')}
    del _L1_gnn_all

    def _L1_ffn_setup():
        import jax, jax.numpy as jnp
        import numpy as np
        E, D, H, TOP_K = (6, 256, 256, 2)
        ROUTER_H = D // 2
        key = jax.random.key(seed)
        ks = jax.random.split(key, 12)
        s = 1.0 / np.sqrt(D)
        sh = 1.0 / np.sqrt(H)
        sr = 1.0 / np.sqrt(ROUTER_H)
        return {'features': jax.random.normal(ks[0], (8, 512, D), dtype=jnp.float32), 'router_w1': jax.random.uniform(ks[1], (D, ROUTER_H), jnp.float32, -s, s), 'router_b1': jnp.zeros((ROUTER_H,), jnp.float32), 'router_w2': jax.random.uniform(ks[2], (ROUTER_H, E), jnp.float32, -sr, sr), 'router_b2': jnp.zeros((E,), jnp.float32), 'expert_w1': jax.random.uniform(ks[3], (E, D, H), jnp.float32, -s, s), 'expert_b1': jnp.zeros((E, H), jnp.float32), 'expert_w2': jax.random.uniform(ks[4], (E, H, H), jnp.float32, -sh, sh), 'expert_b2': jnp.zeros((E, H), jnp.float32), 'expert_w3': jax.random.uniform(ks[5], (E, H, D), jnp.float32, -sh, sh), 'expert_b3': jnp.zeros((E, D), jnp.float32)}
    _L1_ffn_all = _L1_ffn_setup()
    _L1_ffn_in = {k: v for k, v in _L1_ffn_all.items() if k in ('router_w1', 'router_b1', 'router_w2', 'router_b2', 'expert_w1', 'expert_b1', 'expert_w2', 'expert_b2', 'expert_w3', 'expert_b3')}
    del _L1_ffn_all
    return {'x': x, 'src': src, 'dst': dst, 'edge_attr_2': edge_attr_2, 'L0_gnn_W_forward': _L0_gnn_in['W_forward'], 'L0_gnn_W_reverse': _L0_gnn_in['W_reverse'], 'L0_gnn_attn_forward': _L0_gnn_in['attn_forward'], 'L0_ffn_W_gat': _L0_ffn_in['W_gat'], 'L0_ffn_att_src': _L0_ffn_in['att_src'], 'L0_ffn_att_dst': _L0_ffn_in['att_dst'], 'L0_ffn_b_gat': _L0_ffn_in['b_gat'], 'L0_ffn_ln_gamma': _L0_ffn_in['ln_gamma'], 'L0_ffn_ln_beta': _L0_ffn_in['ln_beta'], 'L0_ffn_W1': _L0_ffn_in['W1'], 'L0_ffn_b1': _L0_ffn_in['b1'], 'L0_ffn_W2': _L0_ffn_in['W2'], 'L0_ffn_b2': _L0_ffn_in['b2'], 'L0_ffn_edge_index': _L0_ffn_in['edge_index'], 'L1_gnn_W': _L1_gnn_in['W'], 'L1_gnn_b': _L1_gnn_in['b'], 'L1_gnn_bn_w': _L1_gnn_in['bn_w'], 'L1_gnn_bn_b': _L1_gnn_in['bn_b'], 'L1_ffn_router_w1': _L1_ffn_in['router_w1'], 'L1_ffn_router_b1': _L1_ffn_in['router_b1'], 'L1_ffn_router_w2': _L1_ffn_in['router_w2'], 'L1_ffn_router_b2': _L1_ffn_in['router_b2'], 'L1_ffn_expert_w1': _L1_ffn_in['expert_w1'], 'L1_ffn_expert_b1': _L1_ffn_in['expert_b1'], 'L1_ffn_expert_w2': _L1_ffn_in['expert_w2'], 'L1_ffn_expert_b2': _L1_ffn_in['expert_b2'], 'L1_ffn_expert_w3': _L1_ffn_in['expert_w3'], 'L1_ffn_expert_b3': _L1_ffn_in['expert_b3']}

def reference(x, src, dst, edge_attr_2, L0_gnn_W_forward, L0_gnn_W_reverse, L0_gnn_attn_forward, L0_ffn_W_gat, L0_ffn_att_src, L0_ffn_att_dst, L0_ffn_b_gat, L0_ffn_ln_gamma, L0_ffn_ln_beta, L0_ffn_W1, L0_ffn_b1, L0_ffn_W2, L0_ffn_b2, L0_ffn_edge_index, L1_gnn_W, L1_gnn_b, L1_gnn_bn_w, L1_gnn_bn_b, L1_ffn_router_w1, L1_ffn_router_b1, L1_ffn_router_w2, L1_ffn_router_b2, L1_ffn_expert_w1, L1_ffn_expert_b1, L1_ffn_expert_w2, L1_ffn_expert_b2, L1_ffn_expert_w3, L1_ffn_expert_b3):
    import jax
    import jax.numpy as jnp

    def _L0_gnn_ref(h, adj, direction, W_forward, W_reverse, attn_forward):
        import jax, jax.numpy as jnp
        import numpy as np
        N_NODES = 12500
        N_EDGES = 200000
        IN_FEATS = 256
        OUT_FEATS = 64
        NUM_HEADS = 4
        N = h.shape[0]
        H = attn_forward.shape[1]
        h_fwd = h @ W_forward.T
        h_rev = h @ W_reverse.T
        src, dst = (adj[0], adj[1])
        messages = h_fwd[src] * direction[:, 0:1] + h_rev[src] * direction[:, 1:2]
        scores = jnp.einsum('ef,hf->eh', messages, attn_forward[0])
        scores = jax.nn.leaky_relu(scores, negative_slope=0.2)
        exp_scores = jnp.exp(scores - scores.max(axis=0, keepdims=True))
        sum_exp = jax.ops.segment_sum(exp_scores, dst, num_segments=N)
        norm = exp_scores / (sum_exp[dst] + 1e-10)
        outs = [jax.ops.segment_sum(messages * norm[:, hd:hd + 1], dst, num_segments=N) for hd in range(H)]
        out = jnp.stack(outs, axis=1)
        return out.reshape(N, -1)

    def _L0_ffn_ref(x, W_gat, att_src, att_dst, b_gat, ln_gamma, ln_beta, W1, b1, W2, b2, edge_index):
        import jax, jax.numpy as jnp
        import numpy as np
        B, N, D = (16, 512, 256)
        NUM_EXPERTS, TOP_K, HEADS = (4, 2, 4)
        N_EDGES = 131072
        LN_EPS = 1e-05

        def _layernorm(x, g, b):
            mu = x.mean(-1, keepdims=True)
            var = ((x - mu) ** 2).mean(-1, keepdims=True)
            return (x - mu) * jax.lax.rsqrt(var + LN_EPS) * g + b

        def _forward(x, edge_index, W_gat, att_src, att_dst, b_gat, ln_gamma, ln_beta, W1, b1, W2, b2):
            Bc, Nc, Dc = x.shape
            M = Bc * Nc
            x_flat = x.reshape(M, Dc)
            h = (x_flat @ W_gat).reshape(M, HEADS, NUM_EXPERTS)
            loops = jnp.arange(M, dtype=edge_index.dtype)
            src = jnp.concatenate([edge_index[0], loops])
            dst = jnp.concatenate([edge_index[1], loops])
            a_src = (h * att_src).sum(-1)
            a_dst = (h * att_dst).sum(-1)
            e = jax.nn.leaky_relu(a_src[src] + a_dst[dst], negative_slope=0.2)
            e_max = jax.ops.segment_max(e, dst, num_segments=M)
            ee = jnp.exp(e - e_max[dst])
            denom = jax.ops.segment_sum(ee, dst, num_segments=M)
            alpha = ee / (denom[dst] + 1e-16)
            msg = h[src] * alpha[:, :, None]
            agg = jax.ops.segment_sum(msg, dst, num_segments=M).reshape(M, HEADS * NUM_EXPERTS) + b_gat
            scores = _layernorm(agg, ln_gamma, ln_beta).reshape(M, HEADS, NUM_EXPERTS).mean(1)
            scores = scores.reshape(Bc, Nc, NUM_EXPERTS)
            topk_s, topk_i = jax.lax.top_k(scores, TOP_K)
            w = jax.nn.softmax(topk_s, axis=-1)
            out = jnp.zeros_like(x)
            for ei in range(NUM_EXPERTS):
                g = jnp.where(topk_i == ei, w, 0.0).sum(-1)
                hh = jax.nn.gelu(x @ W1[ei] + b1[ei], approximate=False)
                out = out + g[..., None] * (hh @ W2[ei] + b2[ei])
            return out
        return _forward(x, edge_index, W_gat, att_src, att_dst, b_gat, ln_gamma, ln_beta, W1, b1, W2, b2)

    def _L1_gnn_ref(x, edge_index, W, b, bn_w, bn_b):
        import jax, jax.numpy as jnp
        import numpy as np
        BN_EPS = 1e-05
        N = x.shape[0]
        src, dst = (edge_index[0], edge_index[1])
        agg = jax.ops.segment_sum(x[src], dst, num_segments=N)
        h = x + agg
        h = jnp.einsum('nf,hf->nh', h, W) + b
        mean = jnp.mean(h, axis=0)
        var = jnp.mean(jnp.square(h - mean), axis=0)
        out = (h - mean) * jax.lax.rsqrt(var + BN_EPS) * bn_w + bn_b
        return out

    def _L1_ffn_ref(features, router_w1, router_b1, router_w2, router_b2, expert_w1, expert_b1, expert_w2, expert_b2, expert_w3, expert_b3):
        import jax, jax.numpy as jnp
        import numpy as np
        E, D, H, TOP_K = (6, 256, 256, 2)
        ROUTER_H = D // 2
        rh = jax.nn.relu(features @ router_w1 + router_b1)
        expert_logits = jax.nn.softmax(rh @ router_w2 + router_b2, axis=-1)
        top_w, top_i = jax.lax.top_k(expert_logits, TOP_K)
        routing_weights = jax.nn.softmax(top_w, axis=-1)
        h1 = jax.nn.relu(jnp.einsum('bsd,edh->bseh', features, expert_w1) + expert_b1)
        h2 = jax.nn.relu(jnp.einsum('bseh,ehf->bsef', h1, expert_w2) + expert_b2)
        expert_out = jnp.einsum('bsef,efo->bseo', h2, expert_w3) + expert_b3
        sel = jnp.take_along_axis(expert_out, top_i[:, :, :, None], axis=2)
        combined = jnp.sum(sel * routing_weights[..., None], axis=2)
        return combined
    edge_index = jnp.stack([src, dst])
    x = x + _L0_gnn_ref(_layernorm(x, axis=-1), edge_index, edge_attr_2, L0_gnn_W_forward, L0_gnn_W_reverse, L0_gnn_attn_forward)
    x = x + _L0_ffn_ref(_layernorm(x, axis=-1)[None], L0_ffn_W_gat, L0_ffn_att_src, L0_ffn_att_dst, L0_ffn_b_gat, L0_ffn_ln_gamma, L0_ffn_ln_beta, L0_ffn_W1, L0_ffn_b1, L0_ffn_W2, L0_ffn_b2, L0_ffn_edge_index)[0]
    x = x + _L1_gnn_ref(_layernorm(x, axis=-1), edge_index, L1_gnn_W, L1_gnn_b, L1_gnn_bn_w, L1_gnn_bn_b)
    x = x + _L1_ffn_ref(_layernorm(x, axis=-1)[None], L1_ffn_router_w1, L1_ffn_router_b1, L1_ffn_router_w2, L1_ffn_router_b2, L1_ffn_expert_w1, L1_ffn_expert_b1, L1_ffn_expert_w2, L1_ffn_expert_b2, L1_ffn_expert_w3, L1_ffn_expert_b3)[0]
    return x

_drawn_inputs = setup_inputs


def setup_inputs(seed=0):
    import zlib

    import numpy as np

    out = dict(_drawn_inputs(seed))
    spreads = {'L0_ffn_b_gat': (0.0, 0.1),
     'L0_ffn_ln_gamma': (1.0, 0.2),
     'L0_ffn_ln_beta': (0.0, 0.1),
     'L0_ffn_b1': (0.0, 0.1),
     'L0_ffn_b2': (0.0, 0.1),
     'L1_gnn_b': (0.0, 0.8),
     'L1_gnn_bn_w': (1.0, 0.2),
     'L1_gnn_bn_b': (0.0, 0.1),
     'L1_ffn_router_b1': (0.0, 0.1),
     'L1_ffn_router_b2': (0.0, 0.303),
     'L1_ffn_expert_b1': (0.0, 0.8),
     'L1_ffn_expert_b2': (0.0, 0.473),
     'L1_ffn_expert_b3': (0.0, 0.1)}
    factors = {}
    for name, (base, spread) in spreads.items():
        noise = np.random.default_rng([zlib.crc32(name.encode()), seed]).standard_normal(out[name].shape)
        drawn = base * np.exp(spread * noise) if base else spread * noise
        out[name] = jnp.asarray(drawn.astype(out[name].dtype))
    for name, factor in factors.items():
        out[name] = (out[name] * factor).astype(out[name].dtype)
    return out
```

```python
import concourse.bass as bass
from concourse import mybir
from contextlib import ExitStack

F32 = mybir.dt.float32
I32 = mybir.dt.int32
ALU = mybir.AluOpType
ACT = mybir.ActivationFunctionType
AX = mybir.AxisListType
RED = bass.bass_isa.ReduceOp

P = 128
N = 6250
D = 256
KD = D // P
NB = 50
VB = N // P
VR = N - VB * P
T = 8
GE = P * T
E1 = 106250
G1 = 104
E2 = 131072 + N
G2 = 136
H = 4
OF = 64
MC = OF + H
AC = H * OF + H
W = 2 * P
EX0 = 4
HB = NB // 2
SC = EX0 * H + H
F0 = 512
M0 = F0 // P
EX1 = 6
LN_EPS = 1e-5
NEG = -3.0e38


class Steps:

    def __init__(self, eng, sem, base=0):
        self.eng, self.sem, self.base, self.n = eng, sem, base, 0

    def __call__(self, ins):
        self.mark(ins)
        self.eng.wait_ge(self.sem, self.base + self.n)

    def mark(self, ins):
        ins.then_inc(self.sem, 1)
        self.n += 1


def at(i, k=1):
    return bass.ds(i * k, k)


class Mem:

    def __init__(self, nc, stack, prefix):
        self.nc, self.stack, self.prefix = nc, stack, prefix

    def sb(self, name, shape, dt=F32):
        return self.stack.enter_context(self.nc.sbuf_tensor(f"{self.prefix}_{name}", shape, dt))

    def ps(self, name, shape):
        return self.stack.enter_context(self.nc.psum_tensor(f"{self.prefix}_{name}", shape, F32))

    def sem(self, name):
        return self.stack.enter_context(self.nc.semaphore(f"{self.prefix}_{name}"))


def layernorm_stats(nc, prefix, X, rstd, nmr):
    with ExitStack() as stack:
        m = Mem(nc, stack, prefix)
        st = m.sb("st", [P, NB, 6])
        t0 = m.sb("t0", [P, NB])
        t1 = m.sb("t1", [P, NB])
        stats_in = m.sem("stats_in")
        step = m.sem("step")
        var_ready = m.sem("var_ready")
        std_ready = m.sem("std_ready")
        block = stack.enter_context(nc.Block())

        @block.vector
        def _(dve):
            with dve.Fori(0, NB) as n:
                nc.vector.bn_stats(st[:, at(n), :], X[:, at(n), :]).then_inc(stats_in, 1)
            dve.wait_ge(stats_in, NB)
            link = Steps(dve, step)
            link(nc.vector.tensor_tensor(t0[:, :], st[:, :, 1], st[:, :, 4], ALU.subtract))
            link(nc.vector.tensor_tensor(t0[:, :], t0[:, :], t0[:, :], ALU.mult))
            link(nc.vector.tensor_tensor(t1[:, :], st[:, :, 2], st[:, :, 5], ALU.add))
            link(nc.vector.scalar_tensor_tensor(t0[:, :], t0[:, :], D / 4.0, t1[:, :], ALU.mult, ALU.add))
            nc.vector.tensor_scalar(t0[:, :], t0[:, :], 1.0 / D, LN_EPS, ALU.mult, ALU.add).then_inc(var_ready, 1)
            dve.wait_ge(std_ready, 1)
            link(nc.vector.reciprocal(rstd[:, :], t1[:, :]))
            link(nc.vector.tensor_tensor(t0[:, :], st[:, :, 1], st[:, :, 4], ALU.add))
            link(nc.vector.scalar_tensor_tensor(nmr[:, :], t0[:, :], -0.5, rstd[:, :], ALU.mult, ALU.mult))

        @block.scalar
        def _(act):
            act.wait_ge(var_ready, 1)
            nc.scalar.activation(t1[:, :], t0[:, :], ACT.Sqrt).then_inc(std_ready, 1)


def normalize_project(nc, prefix, X, rstd, nmr, ident, wproj, ncol, table, tcol, keep, parts, k0,
                      HT):
    with ExitStack() as stack:
        m = Mem(nc, stack, prefix)
        h = [m.sb(f"h{s}", [P, D]) for s in range(2)]
        hT = [m.sb(f"hT{s}", [P, KD, P]) for s in range(2)]
        rows = [m.sb(f"rows{s}", [P, tcol]) for s in range(2)]
        psT = [m.ps(f"psT{s}", [P, KD, P]) for s in range(2)]
        psO = [m.ps(f"psO{s}", [P, ncol]) for s in range(2)]
        h_ready = m.sem("h_ready")
        h_turned = m.sem("h_turned")
        hT_ready = m.sem("hT_ready")
        projected = m.sem("projected")
        kept = m.sem("kept")
        HT_ready = m.sem("HT_ready")
        rows_ready = m.sem("rows_ready")
        stored = [m.sem(f"stored{s}") for s in range(2)]
        block = stack.enter_context(nc.Block())

        @block.scalar
        def _(act):
            act.sem_inc(hT_ready, 2)
            with act.Fori(0, HB) as i:
                for s in range(2):
                    n = i * 2 + s
                    act.wait_ge(h_turned, n + 1)
                    nc.scalar.activation(h[s][:, :], X[:, at(n), :], ACT.Identity, bias=nmr[:, at(n)],
                                         scale=rstd[:, at(n)]).then_inc(h_ready, 1)
                for s in range(2):
                    n = i * 2 + s
                    act.wait_ge(h_turned, n + 3)
                    act.wait_ge(projected, n + 1)
                    if HT is not None:
                        act.wait_ge(HT_ready, n + 1)
                    nc.scalar.activation(hT[s][:, :, :], psT[s][:, :, :], ACT.Copy).then_inc(hT_ready, 1)

        @block.tensor
        def _(pe):
            pe.sem_inc(h_turned, 2)
            pe.sem_inc(projected, 2)
            with pe.Fori(0, HB) as i:
                for s in range(2):
                    n = i * 2 + s
                    pe.wait_ge(h_ready, n + 1)
                    pe.wait_ge(hT_ready, n + 1)
                    for k in range(KD):
                        last = nc.tensor.transpose(psT[s][:, k, :], h[s][:, k * P:(k + 1) * P], ident[:, :])
                    last.then_inc(h_turned, 1)
                for s in range(2):
                    n = i * 2 + s
                    pe.wait_ge(hT_ready, n + 3)
                    pe.wait_ge(rows_ready, n + 1)
                    for k in range(KD):
                        last = nc.tensor.matmul(psO[s][:, :], hT[s][:, k, :], wproj[:, k, :],
                                                start=(k == 0), stop=(k == KD - 1))
                    last.then_inc(projected, 1)

        @block.vector
        def _(dve):
            dve.sem_inc(rows_ready, 2)
            if HT is not None:
                dve.sem_inc(HT_ready, 2)
            with dve.Fori(0, HB) as i:
                for s in range(2):
                    n = i * 2 + s
                    if HT is not None:
                        dve.wait_ge(hT_ready, n + 3)
                        nc.vector.tensor_copy(HT[:, :, at(n, P)], hT[s][:, :, :]).then_inc(HT_ready, 1)
                    dve.wait_ge(projected, n + 3)
                    nc.vector.tensor_copy(
                        keep[:, at(n), :].rearrange("p n (a c) -> p (n a) c", a=parts),
                        psO[s][:, :].rearrange("p (a c) -> p a c", a=parts)[:, :, k0:]).then_inc(kept, 1)
                    dve.wait_ge(stored[s], i * 16 + 16)
                    nc.vector.tensor_copy(rows[s][:, :], psO[s][:, 0:tcol]).then_inc(rows_ready, 1)

        @block.sync
        def _(sp):
            for s in range(2):
                sp.sem_inc(stored[s], 16)
            with sp.Fori(0, HB) as i:
                for s in range(2):
                    n = i * 2 + s
                    sp.wait_ge(rows_ready, n + 3)
                    sp.dma_start(table[at(n, P), :], rows[s][:, :]).then_inc(stored[s], 16)
            for s in range(2):
                sp.wait_ge(stored[s], 16 * (HB + 1))


def gates(nc, prefix, S, GT, ex, tri):
    with ExitStack() as stack:
        m = Mem(nc, stack, prefix)
        cmp = m.sb("cmp", [P, NB, ex, ex])
        eq = m.sb("eq", [P, NB, ex, ex])
        rank = m.sb("rank", [P, NB, ex])
        top = m.sb("top", [P, NB])
        d = m.sb("d", [P, NB, ex])
        step = m.sem("step")
        d_ready = m.sem("d_ready")
        exp_ready = m.sem("exp_ready")
        block = stack.enter_context(nc.Block())
        wide = [P, NB, ex, ex]

        @block.vector
        def _(dve):
            link = Steps(dve, step)
            other = S[:, :, :].unsqueeze(2).to_broadcast(wide)
            own = S[:, :, :].unsqueeze(3).to_broadcast(wide)
            link(nc.vector.tensor_reduce(top[:, :], S[:, :, :], AX.X, ALU.max))
            nc.vector.tensor_tensor(d[:, :, :], S[:, :, :], top[:, :].unsqueeze(2).to_broadcast([P, NB, ex]),
                                    ALU.subtract).then_inc(d_ready, 1)
            link(nc.vector.tensor_tensor(cmp[:, :, :, :], other, own, ALU.is_gt))
            link(nc.vector.tensor_tensor(eq[:, :, :, :], other, own, ALU.is_equal))
            link(nc.vector.tensor_tensor(eq[:, :, :, :], eq[:, :, :, :],
                                         tri[:, 0:ex, 0:ex].unsqueeze(1).to_broadcast(wide), ALU.mult))
            link(nc.vector.tensor_tensor(cmp[:, :, :, :], cmp[:, :, :, :], eq[:, :, :, :], ALU.add))
            link(nc.vector.tensor_reduce(rank[:, :, :], cmp[:, :, :, :], AX.X, ALU.add))
            dve.wait_ge(exp_ready, 1)
            link(nc.vector.scalar_tensor_tensor(GT[:, :, :], rank[:, :, :], 1.5, d[:, :, :], ALU.is_lt, ALU.mult))
            link(nc.vector.tensor_reduce(top[:, :], GT[:, :, :], AX.X, ALU.add))
            link(nc.vector.reciprocal(top[:, :], top[:, :]))
            link(nc.vector.tensor_tensor(GT[:, :, :], GT[:, :, :],
                                         top[:, :].unsqueeze(2).to_broadcast([P, NB, ex]), ALU.mult))

        @block.scalar
        def _(act):
            act.wait_ge(d_ready, 1)
            nc.scalar.activation(d[:, :, :], d[:, :, :], ACT.Exp).then_inc(exp_ready, 1)


def sorted_graph(nc, prefix, table, row, src_in, dst_in, first_in, body_columns, ACC, weigh):
    with ExitStack() as stack:
        m = Mem(nc, stack, prefix)
        C = body_columns
        src = m.sb("src", [P, (G1 + 2) * T], I32)
        dst = m.sb("dst", [P, G1 * T], I32)
        rel = m.sb("rel", [P, G1 * T])
        first = m.sb("first", [P, G1], I32)
        base = m.sb("base", [P, G1], I32)
        basef = m.sb("basef", [P, G1])
        iota = m.sb("iota", [P, W])
        iotai = m.sb("iotai", [P, W], I32)
        stage = [m.sb(f"stage{s}", [P, T], I32) for s in range(2)]
        rows = [m.sb(f"rows{s}", [P, T, row]) for s in range(2)]
        hot = [m.sb(f"hot{s}", [P, T, W]) for s in range(2)]
        sums = [m.ps(f"sums{s}", [P, 2, 512]) for s in range(2)]
        if weigh:
            attr_in, shift, smax = weigh
            attr = m.sb("attr", [P, G1 * T, 2])
            val = [m.sb(f"val{s}", [P, T, C]) for s in range(2)]
            prod = m.sb("prod", [P, T, 2, MC])
            msg = m.sb("msg", [P, T, MC])
            sco = m.sb("sco", [P, T, H])
        else:
            val = rows
        loaded = m.sem("loaded")
        iota_done = m.sem("iota_done")
        step = m.sem("step")
        src_staged = m.sem("src_staged")
        landed = [m.sem(f"landed{s}") for s in range(2)]
        rows_used = m.sem("rows_used")
        gathering = m.sem("gathering")
        hot_ready = m.sem("hot_ready")
        scores_ready = m.sem("scores_ready")
        weights_ready = m.sem("weights_ready")
        val_ready = m.sem("val_ready")
        summed = m.sem("summed")
        added = m.sem("added")
        block = stack.enter_context(nc.Block())

        @block.sync
        def _(sp):
            sp.dma_start(src[:, :], src_in).then_inc(loaded, 16)
            sp.dma_start(dst[:, :], dst_in).then_inc(loaded, 16)
            sp.dma_start(first[:, :], first_in.partition_broadcast(P)).then_inc(loaded, 16)
            if weigh:
                sp.dma_start(attr[:, :, :], attr_in.rearrange("p (e c) -> p e c", c=2)).then_inc(loaded, 16)

        @block.gpsimd
        def _(pool):
            nc.gpsimd.iota(iotai[:, :], pattern=[[1, W]], base=0, channel_multiplier=0).then_inc(iota_done, 1)

            def gather(i, s, peeled):
                n = i * 2 + s
                pool.wait_ge(src_staged, n + 1)
                if not peeled:
                    pool.wait_ge(rows_used if weigh else summed, n - 1)
                pool.sem_inc(gathering, 1)
                for t in range(T):
                    pool.indirect_dma_start(
                        out=rows[s][:, t, :], out_offset=None, in_=table,
                        in_offset=bass.IndirectOffsetOnAxis(ap=stage[s][:, t:t + 1], axis=0),
                    ).then_inc(landed[s], 16)

            for s in range(2):
                gather(0, s, True)
            with pool.Fori(1, G1 // 2) as i:
                for s in range(2):
                    gather(i, s, False)

        @block.vector
        def _(dve):
            dve.wait_ge(loaded, 64 if weigh else 48)
            dve.wait_ge(iota_done, 1)
            link = Steps(dve, step)
            link(nc.vector.tensor_single_scalar(base[:, :], first[:, :], 7, ALU.arith_shift_right))
            link(nc.vector.tensor_scalar(base[:, :], base[:, :], VB, 0, ALU.min, ALU.max))
            link(nc.vector.tensor_scalar(basef[:, :], base[:, :], float(P), None, ALU.mult))
            link(nc.vector.tensor_tensor(rel[:, :].rearrange("p (g t) -> p g t", t=T),
                                         dst[:, :].rearrange("p (g t) -> p g t", t=T),
                                         basef[:, :].unsqueeze(2).to_broadcast([P, G1, T]), ALU.subtract))
            link(nc.vector.tensor_copy(iota[:, :], iotai[:, :]))
            if weigh:
                link(nc.vector.memset(smax[:, :, :], NEG))
            setup = link.n
            for s in range(2):
                nc.vector.tensor_scalar(stage[s][:, :], src[:, s * T:(s + 1) * T], N - 1, 0,
                                        ALU.min, ALU.max).then_inc(src_staged, 1)
            LINKS = 3 if weigh else 0

            def add_sums(n, s):
                b = dve.value_load(base[0:1, at(n)], min_val=0, max_val=VB)
                dve.wait_ge(summed, n + 1)
                if not (isinstance(n, int) and n == 0):
                    dve.wait_ge(added, n)
                nc.vector.tensor_tensor(ACC[:, bass.ds(b, 2), :], ACC[:, bass.ds(b, 2), :],
                                        sums[s][:, :, 0:C], ALU.add).then_inc(added, 1)

            def group(i, s, peeled):
                n = i * 2 + s
                link = Steps(dve, step, setup + n * LINKS)
                if not peeled:
                    dve.wait_ge(summed, n - 1)
                nc.vector.tensor_tensor(hot[s][:, :, :], iota[:, :].unsqueeze(1).to_broadcast([P, T, W]),
                                        rel[:, at(n, T)].unsqueeze(2).to_broadcast([P, T, W]),
                                        ALU.is_equal).then_inc(hot_ready, 1)
                dve.wait_ge(landed[s], i * 16 * T + 16 * T)
                nc.vector.tensor_scalar(stage[s][:, :], src[:, at(n + 2, T)], N - 1, 0,
                                        ALU.min, ALU.max).then_inc(src_staged, 1)
                if weigh:
                    nc.vector.tensor_tensor(prod[:, :, :, :],
                                            rows[s][:, :, :].rearrange("p t (a c) -> p t a c", a=2),
                                            attr[:, at(n, T), :].unsqueeze(3).to_broadcast([P, T, 2, MC]),
                                            ALU.mult).then_inc(rows_used, 1)
                    dve.wait_ge(rows_used, n + 1)
                    link(nc.vector.tensor_tensor(msg[:, :, :], prod[:, :, 0, :], prod[:, :, 1, :], ALU.add))
                    nsc = msg[:, :, OF:MC]
                    link.mark(nc.vector.tensor_tensor(smax[:, :, :], smax[:, :, :], nsc, ALU.max))
                    link(nc.vector.scalar_tensor_tensor(sco[:, :, :], nsc, 0.2, nsc, ALU.mult, ALU.max))
                    assert link.n == LINKS
                    nc.vector.tensor_tensor(sco[:, :, :], sco[:, :, :],
                                            shift[:, :].unsqueeze(1).to_broadcast([P, T, H]),
                                            ALU.subtract).then_inc(scores_ready, 1)
                if not (peeled and s == 0):
                    add_sums(n - 1, 1 - s)
                if weigh:
                    dve.wait_ge(weights_ready, n + 1)
                    for hd in range(H):
                        last = nc.vector.tensor_tensor(
                            val[s][:, :, hd * OF:(hd + 1) * OF], msg[:, :, 0:OF],
                            val[s][:, :, H * OF + hd:H * OF + hd + 1].to_broadcast([P, T, OF]), ALU.mult)
                    last.then_inc(val_ready, 1)

            for s in range(2):
                group(0, s, True)
            with dve.Fori(1, G1 // 2) as i:
                for s in range(2):
                    group(i, s, False)
            add_sums(G1 - 1, 1)

        if weigh:
            @block.scalar
            def _(act):
                def group(i, s, peeled):
                    n = i * 2 + s
                    act.wait_ge(scores_ready, n + 1)
                    if not peeled:
                        act.wait_ge(summed, n - 1)
                    nc.scalar.activation(val[s][:, :, H * OF:C], sco[:, :, :], ACT.Exp).then_inc(weights_ready, 1)

                for s in range(2):
                    group(0, s, True)
                with act.Fori(1, G1 // 2) as i:
                    for s in range(2):
                        group(i, s, False)

        @block.tensor
        def _(pe):
            def group(i, s, peeled):
                n = i * 2 + s
                pe.wait_ge(hot_ready, n + 1)
                if weigh:
                    pe.wait_ge(val_ready, n + 1)
                else:
                    pe.wait_ge(landed[s], i * 16 * T + 16 * T)
                if not peeled:
                    pe.wait_ge(added, n - 1)
                for half in range(2):
                    for t in range(T):
                        last = nc.tensor.matmul(sums[s][:, half, 0:C], hot[s][:, t, half * P:(half + 1) * P],
                                                val[s][:, t, :], start=(t == 0), stop=(t == T - 1))
                last.then_inc(summed, 1)

            for s in range(2):
                group(0, s, True)
            with pe.Fori(1, G1 // 2) as i:
                for s in range(2):
                    group(i, s, False)


def attention_bound(nc, prefix, keep, attr_in, shift):
    with ExitStack() as stack:
        m = Mem(nc, stack, prefix)
        attr = m.sb("attr", [P, G1 * T, 2])
        big = m.sb("big", [P, 2 * H + 2])
        all_big = m.sb("all_big", [P, 2 * H + 2])
        t0 = m.sb("t0", [P, 2, H])
        loaded = m.sem("loaded")
        step = m.sem("step")
        big_ready = m.sem("big_ready")
        all_ready = m.sem("all_ready")
        block = stack.enter_context(nc.Block())

        @block.sync
        def _(sp):
            sp.dma_start(attr[:, :, :], attr_in.rearrange("p (e c) -> p e c", c=2)).then_inc(loaded, 16)

        @block.vector
        def _(dve):
            link = Steps(dve, step)
            nc.vector.tensor_reduce(big[:, 0:2 * H], keep[:, :, :].rearrange("p n c -> p c n"), AX.X, ALU.max,
                                    apply_absolute_value=True).then_inc(big_ready, 1)
            dve.wait_ge(loaded, 16)
            nc.vector.tensor_reduce(big[:, 2 * H:], attr[:, :, :].rearrange("p e c -> p c e"), AX.X, ALU.max,
                                    apply_absolute_value=True).then_inc(big_ready, 1)
            dve.wait_ge(all_ready, 1)
            link(nc.vector.tensor_tensor(t0[:, :, :], all_big[:, 0:2 * H].rearrange("p (a h) -> p a h", a=2),
                                         all_big[:, 2 * H:].unsqueeze(2).to_broadcast([P, 2, H]), ALU.mult))
            link(nc.vector.tensor_tensor(shift[:, :], t0[:, 0, :], t0[:, 1, :], ALU.add))

        @block.gpsimd
        def _(pool):
            pool.wait_ge(big_ready, 2)
            nc.gpsimd.partition_all_reduce(all_big[:, :], big[:, :], P, RED.max).then_inc(all_ready, 1)


def attention_finish(nc, prefix, X, ACC, shift, smax):
    with ExitStack() as stack:
        m = Mem(nc, stack, prefix)
        top = m.sb("top", [P, H])
        all_top = m.sb("all_top", [P, H])
        eps = m.sb("eps", [P, H])
        rec = m.sb("rec", [P, NB, H])
        step = m.sem("step")
        top_ready = m.sem("top_ready")
        all_ready = m.sem("all_ready")
        gap_ready = m.sem("gap_ready")
        eps_ready = m.sem("eps_ready")
        block = stack.enter_context(nc.Block())

        @block.vector
        def _(dve):
            link = Steps(dve, step)
            nc.vector.tensor_reduce(top[:, :], smax[:, :, :].rearrange("p t h -> p h t"), AX.X,
                                    ALU.max).then_inc(top_ready, 1)
            dve.wait_ge(all_ready, 1)
            link(nc.vector.scalar_tensor_tensor(eps[:, :], all_top[:, :], 0.2, all_top[:, :], ALU.mult, ALU.max))
            nc.vector.tensor_tensor(eps[:, :], eps[:, :], shift[:, :], ALU.subtract).then_inc(gap_ready, 1)
            dve.wait_ge(eps_ready, 1)
            link(nc.vector.tensor_scalar(eps[:, :], eps[:, :], 1e-10, 1e-37, ALU.mult, ALU.max))
            link(nc.vector.tensor_tensor(rec[:, :, :], ACC[:, :, H * OF:AC],
                                         eps[:, :].unsqueeze(1).to_broadcast([P, NB, H]), ALU.add))
            link(nc.vector.reciprocal(rec[:, :, :], rec[:, :, :]))
            for hd in range(H):
                link.mark(nc.vector.tensor_tensor(ACC[:, :, hd * OF:(hd + 1) * OF], ACC[:, :, hd * OF:(hd + 1) * OF],
                                                  rec[:, :, hd:hd + 1].to_broadcast([P, NB, OF]), ALU.mult))
            dve.wait_ge(step, link.n)
            link(nc.vector.tensor_tensor(X[:, :, :], X[:, :, :], ACC[:, :, 0:D], ALU.add))

        @block.gpsimd
        def _(pool):
            pool.wait_ge(top_ready, 1)
            nc.gpsimd.partition_all_reduce(all_top[:, :], top[:, :], P, RED.max).then_inc(all_ready, 1)

        @block.scalar
        def _(act):
            act.wait_ge(gap_ready, 1)
            nc.scalar.activation(eps[:, :], eps[:, :], ACT.Exp).then_inc(eps_ready, 1)


def routing_tables(nc, prefix, keep, table_dst):
    with ExitStack() as stack:
        m = Mem(nc, stack, prefix)
        top = m.sb("top", [P, H])
        all_top = m.sb("all_top", [P, H])
        t0 = m.sb("t0", [P, NB, H])
        rows = m.sb("rows", [P, NB, 2 * H])
        step = m.sem("step")
        top_ready = m.sem("top_ready")
        all_ready = m.sem("all_ready")
        rows_ready = m.sem("rows_ready")
        stored = m.sem("stored")
        block = stack.enter_context(nc.Block())

        @block.vector
        def _(dve):
            link = Steps(dve, step)
            nc.vector.tensor_reduce(top[:, :], keep[:, :, 0:H].rearrange("p n c -> p c n"), AX.X,
                                    ALU.max).then_inc(top_ready, 1)
            dve.wait_ge(all_ready, 1)
            link(nc.vector.tensor_tensor(t0[:, :, :], keep[:, :, H:2 * H],
                                         all_top[:, :].unsqueeze(1).to_broadcast([P, NB, H]), ALU.add))
            nc.vector.tensor_copy(rows[:, :, 0:H], keep[:, :, H:2 * H]).then_inc(rows_ready, 1)
            nc.vector.scalar_tensor_tensor(rows[:, :, H:], t0[:, :, :], 0.2, t0[:, :, :], ALU.mult,
                                           ALU.max).then_inc(rows_ready, 1)

        @block.gpsimd
        def _(pool):
            pool.wait_ge(top_ready, 1)
            nc.gpsimd.partition_all_reduce(all_top[:, :], top[:, :], P, RED.max).then_inc(all_ready, 1)

        @block.sync
        def _(sp):
            sp.wait_ge(rows_ready, 2)
            sp.dma_start(table_dst.rearrange("(n p) c -> p n c", p=P), rows[:, :, :]).then_inc(stored, 16)
            sp.wait_ge(stored, 16)


def routing_graph(nc, prefix, table_src, table_dst, src_in, dst_in, AGG):
    with ExitStack() as stack:
        m = Mem(nc, stack, prefix)
        V = EX0 * H
        src = m.sb("src", [P, (G2 + 2) * T], I32)
        dst = m.sb("dst", [P, (G2 + 2) * T], I32)
        parti = m.sb("parti", [P, G2 * T], I32)
        lo = m.sb("lo", [P, G2 * T])
        hi = m.sb("hi", [P, G2 * T])
        iotai = m.sb("iotai", [P, W], I32)
        iota = m.sb("iota", [P, W])
        stage = [[m.sb(f"stage{s}{e}", [P, T], I32) for e in range(2)] for s in range(2)]
        rows = [m.sb(f"rows{s}", [P, T, V + H]) for s in range(2)]
        rowd = [m.sb(f"rowd{s}", [P, T, 2 * H]) for s in range(2)]
        hot = [m.sb(f"hot{s}", [P, T, W]) for s in range(2)]
        hoth = m.sb("hoth", [P, T, HB])
        sco = m.sb("sco", [P, T, H])
        sc2 = m.sb("sc2", [P, T, H])
        val = m.sb("val", [P, T, SC])
        wide = [m.sb(f"wide{s}", [P, T, HB, SC]) for s in range(2)]
        zero = m.sb("zero", [P, HB * SC])
        sums = m.ps("sums", [P, 2, 512])
        loaded = m.sem("loaded")
        iota_done = m.sem("iota_done")
        step = m.sem("step")
        staged = m.sem("staged")
        landed = [m.sem(f"landed{s}") for s in range(2)]
        rows_used = m.sem("rows_used")
        gathering = m.sem("gathering")
        scores_ready = m.sem("scores_ready")
        weights_ready = m.sem("weights_ready")
        zero_ready = m.sem("zero_ready")
        wide_ready = m.sem("wide_ready")
        summed = m.sem("summed")
        copied = m.sem("copied")
        block = stack.enter_context(nc.Block())

        @block.sync
        def _(sp):
            sp.dma_start(src[:, :], src_in).then_inc(loaded, 16)
            sp.dma_start(dst[:, :], dst_in).then_inc(loaded, 16)

        @block.gpsimd
        def _(pool):
            nc.gpsimd.iota(iotai[:, :], pattern=[[1, W]], base=0, channel_multiplier=0).then_inc(iota_done, 1)

            def gather(i, s, peeled):
                n = i * 2 + s
                pool.wait_ge(staged, n * 2 + 2)
                if not peeled:
                    pool.wait_ge(rows_used, n - 1)
                pool.sem_inc(gathering, 1)
                for t in range(T):
                    for k, (to, table) in enumerate(((rows, table_src), (rowd, table_dst))):
                        pool.indirect_dma_start(
                            out=to[s][:, t, :], out_offset=None, in_=table,
                            in_offset=bass.IndirectOffsetOnAxis(ap=stage[s][k][:, t:t + 1], axis=0),
                        ).then_inc(landed[s], 16)

            for s in range(2):
                gather(0, s, True)
            with pool.Fori(1, G2 // 2) as i:
                for s in range(2):
                    gather(i, s, False)

        @block.vector
        def _(dve):
            nc.vector.memset(zero[:, :], 0.0).then_inc(zero_ready, 1)
            dve.wait_ge(loaded, 32)
            dve.wait_ge(iota_done, 1)
            link = Steps(dve, step)
            link(nc.vector.tensor_copy(iota[:, :], iotai[:, :]))
            link(nc.vector.tensor_single_scalar(parti[:, :], dst[:, 0:G2 * T], W - 1, ALU.bitwise_and))
            link(nc.vector.tensor_copy(lo[:, :], parti[:, :]))
            link(nc.vector.tensor_single_scalar(parti[:, :], dst[:, 0:G2 * T], 8, ALU.arith_shift_right))
            link(nc.vector.tensor_copy(hi[:, :], parti[:, :]))
            setup = link.n

            def put(s, at_columns):
                for k, of in enumerate((src, dst)):
                    nc.vector.tensor_scalar(stage[s][k][:, :], of[:, at_columns], N - 1, 0,
                                            ALU.min, ALU.max).then_inc(staged, 1)

            for s in range(2):
                put(s, slice(s * T, (s + 1) * T))
            LINKS = 3

            def group(i, s, peeled):
                n = i * 2 + s
                link = Steps(dve, step, setup + n * LINKS)
                if not peeled:
                    dve.wait_ge(summed, n)
                nc.vector.tensor_tensor(hot[s][:, :, :], iota[:, :].unsqueeze(1).to_broadcast([P, T, W]),
                                        lo[:, at(n, T)].unsqueeze(2).to_broadcast([P, T, W]), ALU.is_equal)
                if not (peeled and s == 0):
                    dve.wait_ge(wide_ready, n)
                link.mark(nc.vector.tensor_tensor(hoth[:, :, :], iota[:, 0:HB].unsqueeze(1).to_broadcast([P, T, HB]),
                                                  hi[:, at(n, T)].unsqueeze(2).to_broadcast([P, T, HB]),
                                                  ALU.is_equal))
                dve.wait_ge(landed[s], i * 32 * T + 32 * T)
                put(s, at(n + 2, T))
                link(nc.vector.tensor_tensor(sco[:, :, :], rows[s][:, :, V:], rowd[s][:, :, 0:H], ALU.add))
                link(nc.vector.scalar_tensor_tensor(sc2[:, :, :], sco[:, :, :], 0.2, sco[:, :, :],
                                                    ALU.mult, ALU.max))
                assert link.n == LINKS
                nc.vector.tensor_tensor(sc2[:, :, :], sc2[:, :, :], rowd[s][:, :, H:],
                                        ALU.subtract).then_inc(scores_ready, 1)
                dve.wait_ge(weights_ready, n + 1)
                nc.vector.tensor_tensor(val[:, :, 0:V].rearrange("p t (h e) -> p t h e", e=EX0),
                                        rows[s][:, :, 0:V].rearrange("p t (h e) -> p t h e", e=EX0),
                                        val[:, :, V:].unsqueeze(3).to_broadcast([P, T, H, EX0]),
                                        ALU.mult).then_inc(rows_used, 1)
                dve.wait_ge(rows_used, n + 1)
                nc.vector.tensor_tensor(wide[s][:, :, :, :],
                                        hoth[:, :, :].unsqueeze(3).to_broadcast([P, T, HB, SC]),
                                        val[:, :, :].unsqueeze(2).to_broadcast([P, T, HB, SC]),
                                        ALU.mult).then_inc(wide_ready, 1)

            for s in range(2):
                group(0, s, True)
            with dve.Fori(1, G2 // 2) as i:
                for s in range(2):
                    group(i, s, False)
            dve.wait_ge(summed, G2 + 2)
            for half in range(2):
                nc.vector.tensor_copy(AGG[:, :, half, :],
                                      sums[:, half, 0:HB * SC].rearrange("p (n c) -> p n c", c=SC)).then_inc(copied, 1)
            dve.wait_ge(copied, 2)

        @block.scalar
        def _(act):
            def group(n, peeled):
                act.wait_ge(scores_ready, n + 1)
                if not peeled:
                    act.wait_ge(wide_ready, n)
                nc.scalar.activation(val[:, :, V:], sc2[:, :, :], ACT.Exp).then_inc(weights_ready, 1)

            group(0, True)
            with act.Fori(1, G2) as n:
                group(n, False)

        @block.tensor
        def _(pe):
            pe.wait_ge(zero_ready, 1)
            for half in range(2):
                last = nc.tensor.matmul(sums[:, half, 0:HB * SC], zero[:, 0:P], zero[:, :], start=True, stop=False)
            last.then_inc(summed, 1)
            with pe.Fori(0, G2 // 2) as i:
                for s in range(2):
                    n = i * 2 + s
                    pe.wait_ge(wide_ready, n + 1)
                    for t in range(T):
                        for half in range(2):
                            last = nc.tensor.matmul(sums[:, half, 0:HB * SC], hot[s][:, t, half * P:(half + 1) * P],
                                                    wide[s][:, t, :, :].rearrange("p n c -> p (n c)"),
                                                    start=False, stop=False)
                    last.then_inc(summed, 1)
            for half in range(2):
                last = nc.tensor.matmul(sums[:, half, 0:HB * SC], zero[:, 0:P], zero[:, :], start=False, stop=True)
            last.then_inc(summed, 1)


def routing_scores(nc, prefix, AGG, b_gat, gamma, beta, S):
    with ExitStack() as stack:
        m = Mem(nc, stack, prefix)
        V = EX0 * H
        A = AGG[:, :, :, :].rearrange("p n a c -> p (n a) c")
        y = m.sb("y", [P, NB, V])
        sq = m.sb("sq", [P, NB, V])
        rec = m.sb("rec", [P, NB, H])
        t0 = m.sb("t0", [P, NB])
        t1 = m.sb("t1", [P, NB])
        step = m.sem("step")
        var_ready = m.sem("var_ready")
        std_ready = m.sem("std_ready")
        block = stack.enter_context(nc.Block())
        full = [P, NB, V]

        @block.vector
        def _(dve):
            link = Steps(dve, step)
            link(nc.vector.tensor_scalar(rec[:, :, :], A[:, :, V:], 1e-16, None, ALU.add))
            link(nc.vector.reciprocal(rec[:, :, :], rec[:, :, :]))
            link(nc.vector.tensor_tensor(y[:, :, :].rearrange("p n (h e) -> p n h e", e=EX0),
                                         A[:, :, 0:V].rearrange("p n (h e) -> p n h e", e=EX0),
                                         rec[:, :, :].unsqueeze(3).to_broadcast([P, NB, H, EX0]), ALU.mult))
            link(nc.vector.tensor_tensor(y[:, :, :], y[:, :, :], b_gat[:, :].unsqueeze(1).to_broadcast(full), ALU.add))
            link(nc.vector.tensor_reduce(t0[:, :], y[:, :, :], AX.X, ALU.add))
            link(nc.vector.tensor_scalar(t0[:, :], t0[:, :], 1.0 / V, None, ALU.mult))
            link(nc.vector.tensor_tensor(y[:, :, :], y[:, :, :], t0[:, :].unsqueeze(2).to_broadcast(full), ALU.subtract))
            link(nc.vector.tensor_tensor(sq[:, :, :], y[:, :, :], y[:, :, :], ALU.mult))
            link(nc.vector.tensor_reduce(t0[:, :], sq[:, :, :], AX.X, ALU.add))
            nc.vector.tensor_scalar(t0[:, :], t0[:, :], 1.0 / V, LN_EPS, ALU.mult, ALU.add).then_inc(var_ready, 1)
            dve.wait_ge(std_ready, 1)
            link(nc.vector.reciprocal(t1[:, :], t1[:, :]))
            link(nc.vector.tensor_tensor(y[:, :, :], y[:, :, :], t1[:, :].unsqueeze(2).to_broadcast(full), ALU.mult))
            link(nc.vector.tensor_tensor(y[:, :, :], y[:, :, :], gamma[:, :].unsqueeze(1).to_broadcast(full), ALU.mult))
            link(nc.vector.tensor_tensor(y[:, :, :], y[:, :, :], beta[:, :].unsqueeze(1).to_broadcast(full), ALU.add))
            link(nc.vector.tensor_reduce(S[:, :, :], y[:, :, :].rearrange("p n (h e) -> p n e h", e=EX0), AX.X, ALU.add))
            link(nc.vector.tensor_scalar(S[:, :, :], S[:, :, :], 1.0 / H, None, ALU.mult))

        @block.scalar
        def _(act):
            act.wait_ge(var_ready, 1)
            nc.scalar.activation(t1[:, :], t0[:, :], ACT.Sqrt).then_inc(std_ready, 1)


def experts(nc, prefix, X, HT, GT, ex, sizes, weights, biases, out_bias, funcs, out_dram):
    with ExitStack() as stack:
        m = Mem(nc, stack, prefix)
        L = len(sizes)
        hid = [[m.sb(f"hid{l}{s}", [P, sizes[l], W]) for s in range(2)] for l in range(L)]
        psH = [m.ps(f"psH{s}", [P, W]) for s in range(4)]
        psY = [m.ps(f"psY{s}", [P, D]) for s in range(4)]
        PER = ex * sum(sizes)
        assert PER % 4 == 0 and (ex * 2) % 4 == 0
        order = [(l, e - l) for e in range(ex + L) for l in reversed(range(L + 1)) if 0 <= e - l < ex]
        pos, c = {}, 0
        for l, e in order:
            if l < L:
                pos[l, e] = c
                c += sizes[l]
        made = m.sem("made")
        hid_ready = m.sem("hid_ready")
        y_ready = m.sem("y_ready")
        y_added = m.sem("y_added")
        bias_added = m.sem("bias_added")
        stored = m.sem("stored")
        block = stack.enter_context(nc.Block())

        @block.tensor
        def _(pe):
            pe.sem_inc(y_ready, 4)
            with pe.Fori(0, HB) as i:
                for l, e in order:
                    if l > 0:
                        pe.wait_ge(hid_ready, i * PER + (pos[l - 1, e] + sizes[l - 1] + 4))
                    if l < L:
                        for j in range(sizes[l]):
                            c = pos[l, e] + j
                            pe.wait_ge(hid_ready, i * PER + (c + 1))
                            K = KD if l == 0 else sizes[l - 1]
                            for k in range(K):
                                x = HT[:, k, at(i, W)] if l == 0 else hid[l - 1][e % 2][:, k, :]
                                last = nc.tensor.matmul(psH[c % 4][:, :], weights[l][:, e, k, j * P:(j + 1) * P],
                                                        x, start=(k == 0), stop=(k == K - 1))
                            last.then_inc(made, 1)
                    else:
                        for q in range(2):
                            c = 2 * e + q
                            pe.wait_ge(y_added, i * (2 * ex) + (c + 1))
                            for k in range(sizes[-1]):
                                last = nc.tensor.matmul(psY[c % 4][:, :], hid[-1][e % 2][:, k, q * P:(q + 1) * P],
                                                        weights[L][:, e, k, :], start=(k == 0),
                                                        stop=(k == sizes[-1] - 1))
                            last.then_inc(y_ready, 1)

        @block.scalar
        def _(act):
            act.sem_inc(hid_ready, 4)
            with act.Fori(0, HB) as i:
                for l, e in order:
                    if l == L:
                        continue
                    act.wait_ge(y_ready, i * (2 * ex) + (2 * e + 2))
                    for j in range(sizes[l]):
                        c = pos[l, e] + j
                        act.wait_ge(made, i * PER + (c + 1))
                        nc.scalar.activation(hid[l][e % 2][:, j, :], psH[c % 4][:, :], funcs[l],
                                             bias=biases[l][:, e, j:j + 1]).then_inc(hid_ready, 1)

        @block.vector
        def _(dve):
            dve.sem_inc(y_added, 4)
            with dve.Fori(0, HB) as i:
                for e in range(ex):
                    for q in range(2):
                        b = i * 2 + q
                        if e > 0:
                            dve.wait_ge(bias_added, i * (2 * ex) + 2 * (e - 1) + q + 1)
                        nc.vector.scalar_tensor_tensor(X[:, at(b), :], out_bias[:, e:e + 1, :], GT[:, at(b), e],
                                                       X[:, at(b), :], ALU.mult, ALU.add).then_inc(bias_added, 1)
                dve.wait_ge(bias_added, i * (2 * ex) + 2 * ex)
                for e in range(ex):
                    for q in range(2):
                        b = i * 2 + q
                        c = 2 * e + q
                        dve.wait_ge(y_ready, i * (2 * ex) + (c + 5))
                        if e > 0:
                            dve.wait_ge(y_added, i * (2 * ex) + (c + 3))
                        nc.vector.scalar_tensor_tensor(X[:, at(b), :],
                                                       psY[c % 4][:, :].rearrange("p (a d) -> p a d", a=1),
                                                       GT[:, at(b), e], X[:, at(b), :],
                                                       ALU.mult, ALU.add).then_inc(y_added, 1)

        if out_dram is not None:
            @block.sync
            def _(sp):
                with sp.Fori(0, VB // 2) as i:
                    sp.wait_ge(y_added, i * (2 * ex) + (2 * ex + 4))
                    sp.dma_start(out_dram[at(i, W), :].rearrange("(b p) d -> p b d", p=P),
                                 X[:, at(i, 2), :]).then_inc(stored, 16)
                sp.wait_ge(y_added, (VB // 2 + 1) * (2 * ex) + 4)
                sp.dma_start(out_dram[VB * P:N, :], X[0:VR, VB, :]).then_inc(stored, 16)
                sp.wait_ge(stored, 16 * (VB // 2 + 1))


def router(nc, prefix, HT, w1, b1, w2, b2, LG):
    with ExitStack() as stack:
        m = Mem(nc, stack, prefix)
        hid = [m.sb(f"hid{s}", [P, W]) for s in range(2)]
        top = m.sb("top", [P, NB])
        psH = [m.ps(f"psH{s}", [P, W]) for s in range(2)]
        psL = [m.ps(f"psL{s}", [P, 2, EX1]) for s in range(2)]
        made = m.sem("made")
        hid_ready = m.sem("hid_ready")
        logits_ready = m.sem("logits_ready")
        logits_taken = m.sem("logits_taken")
        step = m.sem("step")
        d_ready = m.sem("d_ready")
        exp_ready = m.sem("exp_ready")
        block = stack.enter_context(nc.Block())
        full = [P, NB, EX1]

        def groups(eng, body):
            with eng.Fori(0, HB // 2) as i:
                for s in range(2):
                    body(i * 2 + s, s)
            body(HB - 1, 0)

        @block.tensor
        def _(pe):
            pe.sem_inc(logits_ready, 2)

            def pair(n, s):
                pe.wait_ge(hid_ready, n + 1)
                for k in range(KD):
                    last = nc.tensor.matmul(psH[s][:, :], w1[:, k, :], HT[:, k, at(n, W)],
                                            start=(k == 0), stop=(k == KD - 1))
                last.then_inc(made, 1)
                pe.wait_ge(hid_ready, n + 3)
                pe.wait_ge(logits_taken, n + 1)
                for q in range(2):
                    last = nc.tensor.matmul(psL[s][:, q, :], hid[s][:, q * P:(q + 1) * P], w2[:, :],
                                            start=True, stop=True)
                last.then_inc(logits_ready, 1)

            groups(pe, pair)

        @block.scalar
        def _(act):
            act.sem_inc(hid_ready, 2)

            def pair(n, s):
                act.wait_ge(made, n + 1)
                act.wait_ge(logits_ready, n + 1)
                nc.scalar.activation(hid[s][:, :], psH[s][:, :], ACT.Relu, bias=b1[:, 0:1]).then_inc(hid_ready, 1)

            groups(act, pair)
            act.wait_ge(d_ready, 1)
            nc.scalar.activation(LG[:, :, :], LG[:, :, :], ACT.Exp).then_inc(exp_ready, 1)

        @block.vector
        def _(dve):
            dve.sem_inc(logits_taken, 2)

            def pair(n, s):
                dve.wait_ge(logits_ready, n + 3)
                nc.vector.tensor_tensor(LG[:, at(n, 2), :], psL[s][:, :, :],
                                        b2[:, :].unsqueeze(1).to_broadcast([P, 2, EX1]),
                                        ALU.add).then_inc(logits_taken, 1)

            groups(dve, pair)
            dve.wait_ge(logits_taken, HB + 2)
            link = Steps(dve, step)
            link(nc.vector.tensor_reduce(top[:, :], LG[:, :, :], AX.X, ALU.max))
            nc.vector.tensor_tensor(LG[:, :, :], LG[:, :, :], top[:, :].unsqueeze(2).to_broadcast(full),
                                    ALU.subtract).then_inc(d_ready, 1)
            dve.wait_ge(exp_ready, 1)
            link(nc.vector.tensor_reduce(top[:, :], LG[:, :, :], AX.X, ALU.add))
            link(nc.vector.reciprocal(top[:, :], top[:, :]))
            link(nc.vector.tensor_tensor(LG[:, :, :], LG[:, :, :], top[:, :].unsqueeze(2).to_broadcast(full),
                                         ALU.mult))


def normalize(nc, prefix, X, rstd, nmr, ACC, table):
    with ExitStack() as stack:
        m = Mem(nc, stack, prefix)
        ready = m.sem("ready")
        stored = m.sem("stored")
        block = stack.enter_context(nc.Block())

        @block.scalar
        def _(act):
            with act.Fori(0, NB) as n:
                nc.scalar.activation(ACC[:, at(n), :], X[:, at(n), :], ACT.Identity, bias=nmr[:, at(n)],
                                     scale=rstd[:, at(n)]).then_inc(ready, 1)

        @block.sync
        def _(sp):
            with sp.Fori(0, HB) as i:
                sp.wait_ge(ready, i * 2 + 2)
                sp.dma_start(table[at(i, W), :].rearrange("(b p) d -> p b d", p=P),
                             ACC[:, at(i, 2), :]).then_inc(stored, 16)
            sp.wait_ge(stored, 16 * HB)


def batch_normalized(nc, prefix, X, ACC, HT, ident, w, b, bn_w, bn_b):
    with ExitStack() as stack:
        m = Mem(nc, stack, prefix)
        rows = [m.sb(f"rows{s}", [P, D]) for s in range(2)]
        rT = [m.sb(f"rT{s}", [P, KD, P]) for s in range(2)]
        FS = 512
        NF = -(-N // FS)
        st = m.sb("st", [P, KD, NF, 6])
        mv = m.sb("mv", [P, KD, 2])
        sc = m.sb("sc", [P, KD])
        sh = m.sb("sh", [P, KD])
        psT = [m.ps(f"psT{s}", [P, KD, P]) for s in range(2)]
        psH = [m.ps(f"psH{s}", [P, KD, P]) for s in range(2)]
        rows_ready = m.sem("rows_ready")
        turned = m.sem("turned")
        rT_ready = m.sem("rT_ready")
        made = m.sem("made")
        h_ready = m.sem("h_ready")
        step = m.sem("step")
        var_ready = m.sem("var_ready")
        std_ready = m.sem("std_ready")
        scale_ready = m.sem("scale_ready")
        out_rows = m.sem("out_rows")
        out_turned = m.sem("out_turned")
        added = m.sem("added")
        block = stack.enter_context(nc.Block())

        @block.scalar
        def _(act):
            act.sem_inc(h_ready, 2)
            with act.Fori(0, HB) as i:
                for s in range(2):
                    n = i * 2 + s
                    act.wait_ge(turned, n + 1)
                    nc.scalar.activation(rows[s][:, :].rearrange("p (a d) -> p a d", a=1), ACC[:, at(n), :],
                                         ACT.Copy).then_inc(rows_ready, 1)
                for s in range(2):
                    n = i * 2 + s
                    act.wait_ge(made, n + 3)
                    for j in range(KD):
                        last = nc.scalar.activation(HT[:, j, at(n, P)], psH[s][:, j, :], ACT.Identity,
                                                    bias=b[:, j:j + 1])
                    last.then_inc(h_ready, 1)
            act.wait_ge(var_ready, 1)
            nc.scalar.activation(sc[:, :], sc[:, :], ACT.Sqrt).then_inc(std_ready, 1)
            act.wait_ge(scale_ready, 1)
            with act.Fori(0, HB) as i:
                for s in range(2):
                    n = i * 2 + s
                    act.wait_ge(out_turned, n + 1)
                    for j in range(KD):
                        last = nc.scalar.activation(rT[s][:, j, :], HT[:, j, at(n, P)], ACT.Identity,
                                                    bias=sh[:, j:j + 1], scale=sc[:, j:j + 1])
                    last.then_inc(out_rows, 1)

        @block.tensor
        def _(pe):
            pe.sem_inc(turned, 2)
            pe.sem_inc(made, 2)
            with pe.Fori(0, HB) as i:
                for s in range(2):
                    n = i * 2 + s
                    pe.wait_ge(rows_ready, n + 1)
                    pe.wait_ge(rT_ready, n + 1)
                    for k in range(KD):
                        last = nc.tensor.transpose(psT[s][:, k, :], rows[s][:, k * P:(k + 1) * P], ident[:, :])
                    last.then_inc(turned, 1)
                for s in range(2):
                    n = i * 2 + s
                    pe.wait_ge(rT_ready, n + 3)
                    pe.wait_ge(h_ready, n + 1)
                    for j in range(KD):
                        for k in range(KD):
                            last = nc.tensor.matmul(psH[s][:, j, :], w[:, k, j * P:(j + 1) * P], rT[s][:, k, :],
                                                    start=(k == 0), stop=(k == KD - 1))
                    last.then_inc(made, 1)
            pe.wait_ge(made, NB + 2)
            pe.sem_inc(out_turned, 2)
            with pe.Fori(0, HB) as i:
                for s in range(2):
                    n = i * 2 + s
                    pe.wait_ge(out_rows, n + 1)
                    pe.wait_ge(added, n + 1)
                    for j in range(KD):
                        last = nc.tensor.transpose(psT[s][:, j, :], rT[s][:, j, :], ident[:, :])
                    last.then_inc(out_turned, 1)

        @block.vector
        def _(dve):
            dve.sem_inc(rT_ready, 2)
            with dve.Fori(0, HB) as i:
                for s in range(2):
                    n = i * 2 + s
                    dve.wait_ge(turned, n + 3)
                    dve.wait_ge(made, n + 1)
                    nc.vector.tensor_copy(rT[s][:, :, :], psT[s][:, :, :]).then_inc(rT_ready, 1)
            dve.wait_ge(h_ready, NB + 2)
            link = Steps(dve, step)
            for j in range(KD):
                for f in range(NF):
                    link.mark(nc.vector.bn_stats(st[:, j, f, :], HT[:, j, f * FS:min(N, (f + 1) * FS)]))
            dve.wait_ge(step, link.n)
            for j in range(KD):
                link(nc.vector.bn_aggr(mv[:, j, :], st[:, j, :, :].rearrange("p f c -> p (f c)")))
            nc.vector.tensor_scalar(sc[:, :], mv[:, :, 1], LN_EPS, None, ALU.add).then_inc(var_ready, 1)
            dve.wait_ge(std_ready, 1)
            link(nc.vector.reciprocal(sc[:, :], sc[:, :]))
            link(nc.vector.tensor_tensor(sc[:, :], sc[:, :], bn_w[:, :], ALU.mult))
            link(nc.vector.tensor_tensor(sh[:, :], mv[:, :, 0], sc[:, :], ALU.mult))
            nc.vector.tensor_tensor(sh[:, :], bn_b[:, :], sh[:, :], ALU.subtract).then_inc(scale_ready, 1)
            dve.sem_inc(added, 2)
            with dve.Fori(0, HB) as i:
                for s in range(2):
                    n = i * 2 + s
                    dve.wait_ge(out_turned, n + 3)
                    nc.vector.tensor_tensor(X[:, at(n), :], X[:, at(n), :],
                                            psT[s][:, :, :].rearrange("p k c -> p (k c)").unsqueeze(1),
                                            ALU.add).then_inc(added, 1)


def load(nc, prefix, pairs):
    with ExitStack() as stack:
        m = Mem(nc, stack, prefix)
        loaded = m.sem("loaded")
        block = stack.enter_context(nc.Block())

        @block.sync
        def _(sp):
            for to, of in pairs:
                sp.dma_start(to, of).then_inc(loaded, 16)
            sp.wait_ge(loaded, 16 * len(pairs))


def constants(nc, prefix, ident, ACC, tri, ex):
    with ExitStack() as stack:
        m = Mem(nc, stack, prefix)
        zeroed = m.sem("zeroed")
        ident_done = m.sem("ident_done")
        tri_zeroed = m.sem("tri_zeroed")
        block = stack.enter_context(nc.Block())

        @block.gpsimd
        def _(pool):
            nc.gpsimd.memset(ident[:, :], 0.0).then_inc(zeroed, 1)
            pool.wait_ge(zeroed, 1)
            nc.gpsimd.affine_select(out=ident[:, :], in_=ident[:, :], compare_op=ALU.not_equal, fill=1.0,
                                    base=0, pattern=[[-1, P]], channel_multiplier=1).then_inc(ident_done, 1)

        @block.vector
        def _(dve):
            nc.vector.memset(ACC[:, :, :], 0.0)
            nc.vector.memset(tri[:, :, :], 0.0).then_inc(tri_zeroed, 1)
            dve.wait_ge(tri_zeroed, 1)
            for i in range(1, ex):
                nc.vector.memset(tri[:, i, 0:i], 1.0)


def score_columns(nc, prefix, wf, attn, wproj, wgat, att, wg):
    with ExitStack() as stack:
        m = Mem(nc, stack, prefix)
        V = EX0 * H
        prod = m.sb("prod", [P, KD, 2, V])
        psA = m.ps("psA", [P, 2, KD, H])
        made = m.sem("made")
        step = m.sem("step")
        block = stack.enter_context(nc.Block())

        @block.tensor
        def _(pe):
            for a in range(2):
                for k in range(KD):
                    last = nc.tensor.matmul(psA[:, a, k, :], wf[:, a, k * P:(k + 1) * P], attn[:, :],
                                            start=True, stop=True)
            last.then_inc(made, 1)

        @block.vector
        def _(dve):
            link = Steps(dve, step)
            for a in range(2):
                link.mark(nc.vector.tensor_tensor(prod[:, :, a, :], wgat[:, :, :],
                                                  att[:, a, :].unsqueeze(1).to_broadcast([P, KD, V]), ALU.mult))
            dve.wait_ge(step, 2)
            nc.vector.tensor_copy(wg[:, :, 0:V], wgat[:, :, :])
            for k in range(KD):
                nc.vector.tensor_reduce(wg[:, k, V:].rearrange("p (a h) -> p a h", a=2),
                                        prod[:, k, :, :].rearrange("p a (h e) -> p a h e", e=EX0), AX.X, ALU.add)
            dve.wait_ge(made, 1)
            for a in range(2):
                nc.vector.tensor_copy(wproj[:, :, a * MC + OF:(a + 1) * MC], psA[:, a, :, :])


def gnn_ffn(nc, x_in, src1, dst1, first1, attr, w_msg, w_rows, attn_t, w_gat, att, b_gat, gamma, beta,
            e0_w1, e0_b1, e0_w2, e0_b2, src2, dst2, w_gin, b_gin, bn_w, bn_b, r_w1, r_b1, r_w2, r_b2,
            e1_w1, e1_b1, e1_w2, e1_b2, e1_w3, e1_b3, out):
    V = EX0 * H
    t_msg = nc.dram_tensor("t_msg", [NB * P, 2 * MC], F32).ap()
    t_src = nc.dram_tensor("t_src", [NB * P, V + H], F32).ap()
    t_dst = nc.dram_tensor("t_dst", [NB * P, 2 * H], F32).ap()
    t_row = nc.dram_tensor("t_row", [NB * P, D], F32).ap()
    with ExitStack() as whole:
        g = Mem(nc, whole, "all")
        X = g.sb("X", [P, NB, D])
        rstd = g.sb("rstd", [P, NB])
        nmr = g.sb("nmr", [P, NB])
        ident = g.sb("ident", [P, P])
        tri = g.sb("tri", [P, EX1, EX1])
        wg = g.sb("wg", [P, KD, V + 2 * H])

        with ExitStack() as layer:
            a = Mem(nc, layer, "l0g")
            ACC = a.sb("ACC", [P, NB, AC])
            wproj = a.sb("wproj", [P, KD, 2 * MC])
            keep = a.sb("keep", [P, NB, 2 * H])
            shift = a.sb("shift", [P, H])
            smax = a.sb("smax", [P, T, H])
            with ExitStack() as first:
                f = Mem(nc, first, "prep")
                wf = f.sb("wf", [OF, 2, D])
                attn = f.sb("attn", [OF, H])
                wgat = f.sb("wgat", [P, KD, V])
                att_b = f.sb("att", [P, 2, V])
                constants(nc, "const", ident, ACC, tri, EX1)
                load(nc, "load0", [
                    (X[:, :, :], x_in), (wproj[:, :, :], w_msg), (wf[:, :, :], w_rows), (attn[:, :], attn_t),
                    (wgat[:, :, :], w_gat), (att_b[:, :, :], att.partition_broadcast(P)),
                ])
                score_columns(nc, "scols", wf, attn, wproj, wgat, att_b, wg)
            layernorm_stats(nc, "ln0", X, rstd, nmr)
            normalize_project(nc, "proj0", X, rstd, nmr, ident, wproj, 2 * MC, t_msg, 2 * MC, keep, 2, OF, None)
            attention_bound(nc, "bound", keep, attr, shift)
            sorted_graph(nc, "att", t_msg, 2 * MC, src1, dst1, first1, AC, ACC, (attr, shift, smax))
            attention_finish(nc, "attfin", X, ACC, shift, smax)

        with ExitStack() as layer:
            a = Mem(nc, layer, "l0f")
            HT = a.sb("HT", [P, KD, NB * P])
            S = a.sb("S", [P, NB, EX0])
            GT = a.sb("GT", [P, NB, EX0])
            layernorm_stats(nc, "ln1", X, rstd, nmr)
            with ExitStack() as part:
                q = Mem(nc, part, "rout")
                keep = q.sb("keep", [P, NB, 2 * H])
                AGG = q.sb("AGG", [P, HB, 2, SC])
                small = [q.sb(f"small{k}", [P, V]) for k in range(3)]
                load(nc, "load1", [(small[k][:, :], v.partition_broadcast(P))
                                   for k, v in enumerate((b_gat, gamma, beta))])
                normalize_project(nc, "proj1", X, rstd, nmr, ident, wg, V + 2 * H, t_src, V + H, keep, 1, V, HT)
                routing_tables(nc, "rtab", keep, t_dst)
                routing_graph(nc, "rgraph", t_src, t_dst, src2, dst2, AGG)
                routing_scores(nc, "rscore", AGG, *small, S)
                gates(nc, "gate0", S, GT, EX0, tri)
            w1 = a.sb("w1", [P, EX0, KD, F0])
            w2 = a.sb("w2", [P, EX0, M0, D])
            b1 = a.sb("b1", [P, EX0, M0])
            b2 = a.sb("b2", [P, EX0, D])
            load(nc, "load2", [(w1[:, :, :, :], e0_w1), (w2[:, :, :, :], e0_w2), (b1[:, :, :], e0_b1),
                               (b2[:, :, :], e0_b2.partition_broadcast(P))])
            experts(nc, "ex0", X, HT, GT, EX0, [M0], [w1, w2], [b1], b2, [ACT.Gelu], None)

        with ExitStack() as layer:
            a = Mem(nc, layer, "l1g")
            ACC = a.sb("ACC", [P, NB, D])
            layernorm_stats(nc, "ln2", X, rstd, nmr)
            normalize(nc, "norm", X, rstd, nmr, ACC, t_row)
            sorted_graph(nc, "gin", t_row, D, src1, dst1, first1, D, ACC, None)
            HT = a.sb("HT", [P, KD, NB * P])
            wgin = a.sb("w", [P, KD, D])
            vec = [a.sb(f"vec{k}", [P, KD]) for k in range(3)]
            load(nc, "load3", [(wgin[:, :, :], w_gin)] + [
                (vec[k][:, :], v) for k, v in enumerate((b_gin, bn_w, bn_b))])
            batch_normalized(nc, "bn", X, ACC, HT, ident, wgin, *vec)

        with ExitStack() as layer:
            a = Mem(nc, layer, "l1f")
            HT = a.sb("HT", [P, KD, NB * P])
            GT = a.sb("GT", [P, NB, EX1])
            S = a.sb("S", [P, NB, EX1])
            layernorm_stats(nc, "ln3", X, rstd, nmr)
            transpose_normalized(nc, "turn", X, rstd, nmr, ident, HT)
            rw1 = a.sb("rw1", [P, KD, P])
            rb1 = a.sb("rb1", [P, 1])
            rw2 = a.sb("rw2", [P, EX1])
            rb2 = a.sb("rb2", [P, EX1])
            w1 = a.sb("w1", [P, EX1, KD, D])
            w2 = a.sb("w2", [P, EX1, KD, D])
            w3 = a.sb("w3", [P, EX1, KD, D])
            b1 = a.sb("b1", [P, EX1, KD])
            b2 = a.sb("b2", [P, EX1, KD])
            b3 = a.sb("b3", [P, EX1, D])
            load(nc, "load4", [
                (rw1[:, :, :], r_w1), (rb1[:, :], r_b1), (rw2[:, :], r_w2), (rb2[:, :], r_b2.partition_broadcast(P)),
                (w1[:, :, :, :], e1_w1), (w2[:, :, :, :], e1_w2), (w3[:, :, :, :], e1_w3),
                (b1[:, :, :], e1_b1), (b2[:, :, :], e1_b2), (b3[:, :, :], e1_b3.partition_broadcast(P))])
            router(nc, "router", HT, rw1, rb1, rw2, rb2, S)
            gates(nc, "gate1", S, GT, EX1, tri)
            experts(nc, "ex1", X, HT, GT, EX1, [KD, KD], [w1, w2, w3], [b1, b2], b3, [ACT.Relu] * 2, out)


def transpose_normalized(nc, prefix, X, rstd, nmr, ident, HT):
    with ExitStack() as stack:
        m = Mem(nc, stack, prefix)
        h = [m.sb(f"h{s}", [P, D]) for s in range(2)]
        psT = [m.ps(f"psT{s}", [P, KD, P]) for s in range(2)]
        h_ready = m.sem("h_ready")
        h_turned = m.sem("h_turned")
        HT_ready = m.sem("HT_ready")
        block = stack.enter_context(nc.Block())

        @block.scalar
        def _(act):
            with act.Fori(0, HB) as i:
                for s in range(2):
                    n = i * 2 + s
                    act.wait_ge(h_turned, n + 1)
                    nc.scalar.activation(h[s][:, :], X[:, at(n), :], ACT.Identity, bias=nmr[:, at(n)],
                                         scale=rstd[:, at(n)]).then_inc(h_ready, 1)

        @block.tensor
        def _(pe):
            pe.sem_inc(h_turned, 2)
            with pe.Fori(0, HB) as i:
                for s in range(2):
                    n = i * 2 + s
                    pe.wait_ge(h_ready, n + 1)
                    pe.wait_ge(HT_ready, n + 1)
                    for k in range(KD):
                        last = nc.tensor.transpose(psT[s][:, k, :], h[s][:, k * P:(k + 1) * P], ident[:, :])
                    last.then_inc(h_turned, 1)

        @block.vector
        def _(dve):
            dve.sem_inc(HT_ready, 2)
            with dve.Fori(0, HB) as i:
                for s in range(2):
                    n = i * 2 + s
                    dve.wait_ge(h_turned, n + 3)
                    nc.vector.tensor_copy(HT[:, :, at(n, P)], psT[s][:, :, :]).then_inc(HT_ready, 1)


def layouts(i, np):
    def blocks(a):
        a = np.concatenate([a, np.zeros((NB * P - N, a.shape[1]), a.dtype)])
        return a.reshape(NB, P, -1).transpose(1, 0, 2)

    def edges(a, groups, pad, extra=0):
        tail = np.repeat(a[-1:] if pad is None else np.full_like(a[-1:], pad), groups * GE - len(a), axis=0)
        a = np.concatenate([a, tail]).reshape((groups, P, T) + a.shape[1:])
        a = np.moveaxis(a, 0, 1).reshape((P, -1))
        return np.concatenate([a, np.zeros((P, extra * T), a.dtype)], axis=1)

    def slices(a):
        a = a.reshape(a.shape[:-2] + (-1, P, a.shape[-1]))
        return np.moveaxis(a, -2, 0)

    def cols(a):
        return np.moveaxis(a.reshape(a.shape[:-1] + (-1, P)), -1, 0)

    src, dst = i["src"], i["dst"]
    wf, wr = i["L0_gnn_W_forward"], i["L0_gnn_W_reverse"]
    gap = np.zeros((D, H), wf.dtype)
    loops = np.arange(N, dtype=src.dtype)
    ei = i["L0_ffn_edge_index"]
    firsts = np.concatenate([dst, dst[-1:].repeat(G1 * GE - E1)])[::GE]
    return {
        "x_in": blocks(i["x"]), "src1": edges(src, G1, None, 2), "dst1": edges(dst, G1, -1),
        "first1": firsts, "attr": edges(i["edge_attr_2"], G1, None),
        "w_msg": slices(np.concatenate([wf.T, gap, wr.T, gap], axis=1)),
        "w_rows": np.stack([wf, wr]).transpose(1, 0, 2), "attn_t": i["L0_gnn_attn_forward"][0].T,
        "w_gat": slices(i["L0_ffn_W_gat"]),
        "att": np.stack([i["L0_ffn_att_src"].reshape(-1), i["L0_ffn_att_dst"].reshape(-1)]),
        "b_gat": i["L0_ffn_b_gat"], "gamma": i["L0_ffn_ln_gamma"], "beta": i["L0_ffn_ln_beta"],
        "e0_w1": slices(i["L0_ffn_W1"]), "e0_b1": cols(i["L0_ffn_b1"]),
        "e0_w2": slices(i["L0_ffn_W2"]), "e0_b2": i["L0_ffn_b2"],
        "src2": edges(np.concatenate([ei[0], loops]), G2, None, 2),
        "dst2": edges(np.concatenate([ei[1], loops]), G2, -1, 2),
        "w_gin": slices(i["L1_gnn_W"].T), "b_gin": cols(i["L1_gnn_b"]),
        "bn_w": cols(i["L1_gnn_bn_w"]), "bn_b": cols(i["L1_gnn_bn_b"]),
        "r_w1": slices(i["L1_ffn_router_w1"]), "r_b1": cols(i["L1_ffn_router_b1"]),
        "r_w2": i["L1_ffn_router_w2"], "r_b2": i["L1_ffn_router_b2"],
        "e1_w1": slices(i["L1_ffn_expert_w1"]), "e1_b1": cols(i["L1_ffn_expert_b1"]),
        "e1_w2": slices(i["L1_ffn_expert_w2"]), "e1_b2": cols(i["L1_ffn_expert_b2"]),
        "e1_w3": slices(i["L1_ffn_expert_w3"]), "e1_b3": i["L1_ffn_expert_b3"],
    }


def kernel(**inputs):
    import numpy as np
    import concourse.bacc as bacc
    from concourse.bass_utils import run_bass_kernel_spmd

    nc = bacc.Bacc("TRN2", target_bir_lowering=False, num_devices=1)
    arrays = {k: np.ascontiguousarray(v) for k, v in
              layouts({k: np.asarray(v) for k, v in inputs.items()}, np).items()}
    args = {k: nc.dram_tensor(k, v.shape, mybir.dt.from_np(v.dtype), kind="ExternalInput").ap()
            for k, v in arrays.items()}
    out = nc.dram_tensor("out", (N, D), F32, kind="ExternalOutput").ap()
    gnn_ffn(nc, out=out, **args)
    return run_bass_kernel_spmd(nc, [arrays], core_ids=[0]).results[0]["out"]
```

```python
import collections

import concourse.bass as bass
from concourse import mybir
from contextlib import ExitStack

F32 = mybir.dt.float32
I32 = mybir.dt.int32
F32R = mybir.dt.float32r
ALU = mybir.AluOpType
ACT = mybir.ActivationFunctionType
AX = mybir.AxisListType
RED = bass.bass_isa.ReduceOp

P = 128
N = 6250
D = 256
KD = D // P
NB = 50
VB = N // P
VR = N - VB * P
T = 8
GE = P * T
E1 = 106250
G1 = 104
E2 = 131072
G2 = E2 // GE
H = 4
OF = 64
MC = OF + H
AC = H * OF + H
W = 2 * P
EX0 = 4
HB = NB // 2
SC = EX0 * H + H
F0 = 512
M0 = F0 // P
EX1 = 6
LN_EPS = 1e-5
NEG = -3.0e38
FAR = 40.0


class Steps:

    def __init__(self, eng, sem, base=0):
        self.eng, self.sem, self.base, self.n = eng, sem, base, 0

    def __call__(self, ins):
        self.mark(ins)
        self.eng.wait_ge(self.sem, self.base + self.n)

    def mark(self, ins):
        ins.then_inc(self.sem, 1)
        self.n += 1


def at(i, k=1):
    return bass.ds(i * k, k)


class Mem:

    order = {}

    def __init__(self, nc, stack, prefix):
        self.nc, self.stack, self.prefix = nc, stack, prefix
        self.sems, self.nums = [], []
        self.waiting = Mem.order.setdefault(id(nc), collections.deque(nc.free_semaphores))
        stack.callback(self.free_sems)

    def free_sems(self):
        if self.sems:
            self.nc.clear_and_free_semaphores(self.sems)
            self.waiting.extend(self.nums)

    def sb(self, name, shape, dt=F32):
        return self.stack.enter_context(self.nc.sbuf_tensor(f"{self.prefix}_{name}", shape, dt))

    def ps(self, name, shape):
        return self.stack.enter_context(self.nc.psum_tensor(f"{self.prefix}_{name}", shape, F32))

    def sem(self, name):
        self.nums.append(self.waiting.popleft())
        self.sems.append(self.nc.alloc_semaphore(f"{self.prefix}_{name}", self.nums[-1]))
        return self.sems[-1]


def layernorm_stats(nc, prefix, X, rstd, nmr):
    with ExitStack() as stack:
        m = Mem(nc, stack, prefix)
        st = m.sb("st", [P, NB, 6])
        t0 = m.sb("t0", [P, NB])
        t1 = m.sb("t1", [P, NB])
        stats_in = m.sem("stats_in")
        step = m.sem("step")
        var_ready = m.sem("var_ready")
        std_ready = m.sem("std_ready")
        block = stack.enter_context(nc.Block())

        @block.vector
        def _(dve):
            with dve.Fori(0, NB) as n:
                nc.vector.bn_stats(st[:, at(n), :], X[:, at(n), :]).then_inc(stats_in, 1)
            dve.wait_ge(stats_in, NB)
            link = Steps(dve, step)
            link(nc.vector.tensor_tensor(t0[:, :], st[:, :, 1], st[:, :, 4], ALU.subtract))
            link(nc.vector.tensor_tensor(t0[:, :], t0[:, :], t0[:, :], ALU.mult))
            link(nc.vector.tensor_tensor(t1[:, :], st[:, :, 2], st[:, :, 5], ALU.add))
            link(nc.vector.scalar_tensor_tensor(t0[:, :], t0[:, :], D / 4.0, t1[:, :], ALU.mult, ALU.add))
            nc.vector.tensor_scalar(t0[:, :], t0[:, :], 1.0 / D, LN_EPS, ALU.mult, ALU.add).then_inc(var_ready, 1)
            dve.wait_ge(std_ready, 1)
            link(nc.vector.reciprocal(rstd[:, :], t1[:, :]))
            link(nc.vector.tensor_tensor(t0[:, :], st[:, :, 1], st[:, :, 4], ALU.add))
            link(nc.vector.scalar_tensor_tensor(nmr[:, :], t0[:, :], -0.5, rstd[:, :], ALU.mult, ALU.mult))

        @block.scalar
        def _(act):
            act.wait_ge(var_ready, 1)
            nc.scalar.activation(t1[:, :], t0[:, :], ACT.Sqrt).then_inc(std_ready, 1)


def normalize_project(nc, prefix, X, rstd, nmr, ident, wproj, ncol, table, tcol, keep, parts, k0,
                      t_hT):
    with ExitStack() as stack:
        m = Mem(nc, stack, prefix)
        h = [m.sb(f"h{s}", [P, D]) for s in range(2)]
        hT = [m.sb(f"hT{s}", [P, KD, P]) for s in range(2)]
        rows = [m.sb(f"rows{s}", [P, tcol]) for s in range(2)]
        psT = [m.ps(f"psT{s}", [P, KD, P]) for s in range(2)]
        psO = [m.ps(f"psO{s}", [P, ncol]) for s in range(2)]
        h_ready = m.sem("h_ready")
        h_turned = m.sem("h_turned")
        hT_ready = m.sem("hT_ready")
        projected = m.sem("projected")
        kept = m.sem("kept")
        hT_stored = [m.sem(f"hT_stored{s}") for s in range(2)]
        rows_ready = m.sem("rows_ready")
        stored = [m.sem(f"stored{s}") for s in range(2)]
        block = stack.enter_context(nc.Block())

        @block.scalar
        def _(act):
            act.sem_inc(hT_ready, 2)
            with act.Fori(0, HB) as i:
                for s in range(2):
                    n = i * 2 + s
                    act.wait_ge(h_turned, n + 1)
                    nc.scalar.activation(h[s][:, :], X[:, at(n), :], ACT.Identity, bias=nmr[:, at(n)],
                                         scale=rstd[:, at(n)]).then_inc(h_ready, 1)
                for s in range(2):
                    n = i * 2 + s
                    act.wait_ge(h_turned, n + 3)
                    act.wait_ge(projected, n + 1)
                    if t_hT is not None:
                        act.wait_ge(hT_stored[s], i * 16 + 16)
                    nc.scalar.activation(hT[s][:, :, :], psT[s][:, :, :], ACT.Copy).then_inc(hT_ready, 1)

        @block.tensor
        def _(pe):
            pe.sem_inc(h_turned, 2)
            pe.sem_inc(projected, 2)
            with pe.Fori(0, HB) as i:
                for s in range(2):
                    n = i * 2 + s
                    pe.wait_ge(h_ready, n + 1)
                    pe.wait_ge(hT_ready, n + 1)
                    for k in range(KD):
                        last = nc.tensor.transpose(psT[s][:, k, :], h[s][:, k * P:(k + 1) * P], ident[:, :])
                    last.then_inc(h_turned, 1)
                for s in range(2):
                    n = i * 2 + s
                    pe.wait_ge(hT_ready, n + 3)
                    pe.wait_ge(rows_ready, n + 1)
                    for k in range(KD):
                        last = nc.tensor.matmul(psO[s][:, :], hT[s][:, k, :], wproj[:, k, :],
                                                start=(k == 0), stop=(k == KD - 1))
                    last.then_inc(projected, 1)

        @block.vector
        def _(dve):
            dve.sem_inc(rows_ready, 2)
            with dve.Fori(0, HB) as i:
                for s in range(2):
                    n = i * 2 + s
                    dve.wait_ge(projected, n + 3)
                    nc.vector.tensor_copy(
                        keep[:, at(n), :].rearrange("p n (a c) -> p (n a) c", a=parts),
                        psO[s][:, :].rearrange("p (a c) -> p a c", a=parts)[:, :, k0:]).then_inc(kept, 1)
                    dve.wait_ge(stored[s], i * 16 + 16)
                    nc.vector.tensor_copy(rows[s][:, :], psO[s][:, 0:tcol]).then_inc(rows_ready, 1)

        @block.sync
        def _(sp):
            for s in range(2):
                sp.sem_inc(stored[s], 16)
                sp.sem_inc(hT_stored[s], 16)
            with sp.Fori(0, HB) as i:
                for s in range(2):
                    n = i * 2 + s
                    if t_hT is not None:
                        sp.wait_ge(hT_ready, n + 3)
                        sp.dma_start(t_hT[at(i), :, :].rearrange("a p (k c) -> (a p) k c", k=KD)[:, :, s * P:(s + 1) * P],
                                     hT[s][:, :, :]).then_inc(hT_stored[s], 16)
                    sp.wait_ge(rows_ready, n + 3)
                    sp.dma_start(table[at(n, P), :], rows[s][:, :]).then_inc(stored[s], 16)
            for s in range(2):
                sp.wait_ge(stored[s], 16 * (HB + 1))
                if t_hT is not None:
                    sp.wait_ge(hT_stored[s], 16 * (HB + 1))


def gates(nc, prefix, S, GT, ex, tri):
    with ExitStack() as stack:
        m = Mem(nc, stack, prefix)
        cmp = m.sb("cmp", [P, NB, ex, ex])
        eq = m.sb("eq", [P, NB, ex, ex])
        rank = m.sb("rank", [P, NB, ex])
        top = m.sb("top", [P, NB])
        d = m.sb("d", [P, NB, ex])
        step = m.sem("step")
        d_ready = m.sem("d_ready")
        exp_ready = m.sem("exp_ready")
        block = stack.enter_context(nc.Block())
        wide = [P, NB, ex, ex]

        @block.vector
        def _(dve):
            link = Steps(dve, step)
            other = S[:, :, :].unsqueeze(2).to_broadcast(wide)
            own = S[:, :, :].unsqueeze(3).to_broadcast(wide)
            link(nc.vector.tensor_reduce(top[:, :], S[:, :, :], AX.X, ALU.max))
            nc.vector.tensor_tensor(d[:, :, :], S[:, :, :], top[:, :].unsqueeze(2).to_broadcast([P, NB, ex]),
                                    ALU.subtract).then_inc(d_ready, 1)
            link(nc.vector.tensor_tensor(cmp[:, :, :, :], other, own, ALU.is_gt))
            link(nc.vector.tensor_tensor(eq[:, :, :, :], other, own, ALU.is_equal))
            link(nc.vector.tensor_tensor(eq[:, :, :, :], eq[:, :, :, :],
                                         tri[:, 0:ex, 0:ex].unsqueeze(1).to_broadcast(wide), ALU.mult))
            link(nc.vector.tensor_tensor(cmp[:, :, :, :], cmp[:, :, :, :], eq[:, :, :, :], ALU.add))
            link(nc.vector.tensor_reduce(rank[:, :, :], cmp[:, :, :, :], AX.X, ALU.add))
            dve.wait_ge(exp_ready, 1)
            link(nc.vector.scalar_tensor_tensor(GT[:, :, :], rank[:, :, :], 1.5, d[:, :, :], ALU.is_lt, ALU.mult))
            link(nc.vector.tensor_reduce(top[:, :], GT[:, :, :], AX.X, ALU.add))
            link(nc.vector.reciprocal(top[:, :], top[:, :]))
            link(nc.vector.tensor_tensor(GT[:, :, :], GT[:, :, :],
                                         top[:, :].unsqueeze(2).to_broadcast([P, NB, ex]), ALU.mult))

        @block.scalar
        def _(act):
            act.wait_ge(d_ready, 1)
            nc.scalar.activation(d[:, :, :], d[:, :, :], ACT.Exp).then_inc(exp_ready, 1)


def wait(eng, sem, n):
    if not (isinstance(n, int) and n <= 0):
        eng.wait_ge(sem, n)


def when(eng, flag, body):
    if flag is None:
        body()
    else:
        set_ = eng.value_load(flag[0:1, 0:1], min_val=0, max_val=1)
        with eng.If(set_ > 0):
            body()


def pairs(eng, count, body):
    for s in range(2):
        body(s, s)
    with eng.Fori(1, count // 2) as i:
        for s in range(2):
            body(i * 2 + s, s)


class Graph:

    def __init__(self, m):
        self.src = m.sb("src", [P, (G1 + 2) * T], I32)
        self.rel = m.sb("rel", [P, G1 * T])
        self.first = m.sb("first", [P, G1])
        self.base = m.sb("base", [P, G1], I32)
        self.off = m.sb("off", [P, G1])
        self.stray = m.sb("stray", [P, 1], I32)
        self.iota = m.sb("iota", [P, W])
        self.diff = m.sb("diff", [P, W])


def read_graph(nc, prefix, gr, src_in, dst_in, first_in):
    with ExitStack() as stack:
        m = Mem(nc, stack, prefix)
        dst = m.sb("dst", [P, G1 * T], I32)
        first = m.sb("first", [P, G1], I32)
        basef = m.sb("basef", [P, G1])
        iotai = m.sb("iotai", [P, W], I32)
        diffi = m.sb("diffi", [P, W], I32)
        out0 = m.sb("out0", [P, G1 * T])
        out1 = m.sb("out1", [P, G1 * T])
        some = m.sb("some", [P, 1])
        any_ = m.sb("any", [P, 1])
        loaded = m.sem("loaded")
        iota_done = m.sem("iota_done")
        step = m.sem("step")
        some_ready = m.sem("some_ready")
        any_ready = m.sem("any_ready")
        block = stack.enter_context(nc.Block())

        @block.sync
        def _(sp):
            sp.dma_start(dst[:, :], dst_in).then_inc(loaded, 16)
            sp.dma_start(first[:, :], first_in.partition_broadcast(P)).then_inc(loaded, 16)
            sp.dma_start(gr.src[:, :], src_in).then_inc(loaded, 16)

        @block.gpsimd
        def _(pool):
            nc.gpsimd.iota(iotai[:, :], pattern=[[1, W]], base=0, channel_multiplier=0).then_inc(iota_done, 1)
            nc.gpsimd.iota(diffi[:, :], pattern=[[1, W]], base=0, channel_multiplier=-1).then_inc(iota_done, 1)
            pool.wait_ge(some_ready, 1)
            nc.gpsimd.partition_all_reduce(any_[:, :], some[:, :], P, RED.max).then_inc(any_ready, 1)

        @block.vector
        def _(dve):
            dve.wait_ge(loaded, 48)
            dve.wait_ge(iota_done, 2)
            link = Steps(dve, step)
            link.mark(nc.vector.tensor_copy(gr.iota[:, :], iotai[:, :]))
            link.mark(nc.vector.tensor_copy(gr.diff[:, :], diffi[:, :]))
            link.mark(nc.vector.tensor_copy(gr.first[:, :], first[:, :]))
            link(nc.vector.tensor_single_scalar(gr.base[:, :], first[:, :], 7, ALU.arith_shift_right))
            link(nc.vector.tensor_scalar(gr.base[:, :], gr.base[:, :], VB, 0, ALU.min, ALU.max))
            link(nc.vector.tensor_scalar(basef[:, :], gr.base[:, :], float(P), None, ALU.mult))
            link(nc.vector.tensor_tensor(gr.off[:, :], gr.first[:, :], basef[:, :], ALU.subtract))
            link(nc.vector.tensor_tensor(gr.rel[:, :].rearrange("p (g t) -> p g t", t=T),
                                         dst[:, :].rearrange("p (g t) -> p g t", t=T),
                                         gr.first[:, :].unsqueeze(2).to_broadcast([P, G1, T]), ALU.subtract))
            link(nc.vector.tensor_scalar(out0[:, :], gr.rel[:, :], 0.0, None, ALU.is_lt))
            link(nc.vector.scalar_tensor_tensor(out1[:, :], gr.rel[:, :], float(P), out0[:, :], ALU.is_ge, ALU.add))
            link(nc.vector.scalar_tensor_tensor(out0[:, :], dst[:, :], 0.0, out1[:, :], ALU.is_ge, ALU.mult))
            nc.vector.tensor_reduce(some[:, :], out0[:, :], AX.X, ALU.max).then_inc(some_ready, 1)
            dve.wait_ge(any_ready, 1)
            link(nc.vector.tensor_copy(gr.stray[:, :], any_[:, :]))


class Weigh:

    def __init__(self, attr, shift, smax):
        self.attr, self.shift, self.smax = attr, shift, smax


def sorted_graph(nc, prefix, table, row, gr, C, ACC, weigh, flag=None):
    with ExitStack() as stack:
        m = Mem(nc, stack, prefix)
        stage = [m.sb(f"stage{s}", [P, T], I32) for s in range(2)]
        rows = [m.sb(f"rows{s}", [P, T, row]) for s in range(2)]
        hot = [m.sb(f"hot{s}", [P, T, P]) for s in range(2)]
        move = [m.sb(f"move{s}", [P, W]) for s in range(2)]
        wsum = [m.sb(f"wsum{s}", [P, C]) for s in range(2)]
        psW = [m.ps(f"psW{s}", [P, 512]) for s in range(2)]
        psB = [m.ps(f"psB{s}", [P, 2, 512]) for s in range(2)]
        if weigh:
            val = [m.sb(f"val{s}", [P, T, C]) for s in range(2)]
            prod = m.sb("prod", [P, T, 2, MC])
            msg = m.sb("msg", [P, T, MC])
            sco = m.sb("sco", [P, T, H])
        else:
            val = rows
        step = m.sem("step")
        src_staged = m.sem("src_staged")
        gathering = m.sem("gathering")
        landed = [m.sem(f"landed{s}") for s in range(2)]
        rows_used = m.sem("rows_used")
        hot_ready = m.sem("hot_ready")
        move_ready = m.sem("move_ready")
        scores_ready = m.sem("scores_ready")
        weights_ready = m.sem("weights_ready")
        val_ready = m.sem("val_ready")
        summed = m.sem("summed")
        wsum_ready = m.sem("wsum_ready")
        moved = m.sem("moved")
        added = m.sem("added")
        block = stack.enter_context(nc.Block())

        @block.gpsimd
        def _(pool):
            def gather(n, s):
                pool.wait_ge(src_staged, n + 1)
                wait(pool, rows_used if weigh else summed, n - 1)
                pool.sem_inc(gathering, 1)
                for t in range(T):
                    pool.indirect_dma_start(
                        out=rows[s][:, t, :], out_offset=None, in_=table,
                        in_offset=bass.IndirectOffsetOnAxis(ap=stage[s][:, t:t + 1], axis=0),
                    ).then_inc(landed[s], 16)

            when(pool, flag, lambda: pairs(pool, G1, gather))

        @block.vector
        def _(dve):
            def put(n, s):
                nc.vector.tensor_scalar(stage[s][:, :], gr.src[:, at(n, T)], N - 1, 0,
                                        ALU.min, ALU.max).then_inc(src_staged, 1)

            def add_sums(n, s):
                b = dve.value_load(gr.base[0:1, at(n)], min_val=0, max_val=VB)
                dve.wait_ge(moved, n + 1)
                wait(dve, added, n)
                nc.vector.tensor_tensor(ACC[:, bass.ds(b, 2), :], ACC[:, bass.ds(b, 2), :],
                                        psB[s][:, :, 0:C], ALU.add).then_inc(added, 1)

            STEPS = 3 if weigh else 0

            def group(n, s):
                link = Steps(dve, step, n * STEPS)

                def mark_places():
                    wait(dve, summed, n - 1)
                    nc.vector.tensor_tensor(hot[s][:, :, :], gr.iota[:, 0:P].unsqueeze(1).to_broadcast([P, T, P]),
                                            gr.rel[:, at(n, T)].unsqueeze(2).to_broadcast([P, T, P]),
                                            ALU.is_equal).then_inc(hot_ready, 1)

                if not weigh:
                    mark_places()
                dve.wait_ge(landed[s], (n - s) * (8 * T) + 16 * T)
                put(n + 2, s)
                if weigh:
                    nc.vector.tensor_tensor(prod[:, :, :, :],
                                            rows[s][:, :, :].rearrange("p t (a c) -> p t a c", a=2),
                                            weigh.attr[:, at(n, T), :].unsqueeze(3).to_broadcast([P, T, 2, MC]),
                                            ALU.mult).then_inc(rows_used, 1)
                    mark_places()
                    dve.wait_ge(rows_used, n + 1)
                    wait(dve, val_ready, n)
                    link(nc.vector.tensor_tensor(msg[:, :, :], prod[:, :, 0, :], prod[:, :, 1, :], ALU.add))
                    nsc = msg[:, :, OF:MC]
                    link.mark(nc.vector.tensor_tensor(weigh.smax[:, :, :], weigh.smax[:, :, :], nsc, ALU.max))
                    link(nc.vector.scalar_tensor_tensor(sco[:, :, :], nsc, 0.2, nsc, ALU.mult, ALU.max))
                    assert link.n == STEPS
                    nc.vector.tensor_tensor(sco[:, :, :], sco[:, :, :],
                                            weigh.shift[:, :].unsqueeze(1).to_broadcast([P, T, H]),
                                            ALU.subtract).then_inc(scores_ready, 1)
                    dve.wait_ge(weights_ready, n + 1)
                    for hd in range(H):
                        last = nc.vector.tensor_tensor(
                            val[s][:, :, hd * OF:(hd + 1) * OF], msg[:, :, 0:OF],
                            val[s][:, :, H * OF + hd:H * OF + hd + 1].to_broadcast([P, T, OF]), ALU.mult)
                    last.then_inc(val_ready, 1)
                wait(dve, moved, n - 1)
                nc.vector.tensor_scalar(move[s][:, :], gr.diff[:, :], gr.off[:, at(n)], None,
                                        ALU.is_equal).then_inc(move_ready, 1)
                if not (isinstance(n, int) and n < 2):
                    add_sums(n - 2, s)

            def body():
                for s in range(2):
                    put(s, s)
                pairs(dve, G1, group)
                for n in (G1 - 2, G1 - 1):
                    add_sums(n, n % 2)

            when(dve, flag, body)

        @block.scalar
        def _(act):
            def take_window(n, s):
                act.wait_ge(summed, n + 1)
                wait(act, moved, n - 1)
                nc.scalar.activation(wsum[s][:, :], psW[s][:, 0:C], ACT.Copy).then_inc(wsum_ready, 1)

            def group(n, s):
                if weigh:
                    act.wait_ge(scores_ready, n + 1)
                    wait(act, summed, n - 1)
                    nc.scalar.activation(val[s][:, :, H * OF:C], sco[:, :, :], ACT.Exp).then_inc(weights_ready, 1)
                if not (isinstance(n, int) and n < 1):
                    take_window(n - 1, 1 - s)

            def body():
                pairs(act, G1, group)
                take_window(G1 - 1, 1)

            when(act, flag, body)

        @block.tensor
        def _(pe):
            def onto_blocks(n, s):
                pe.wait_ge(wsum_ready, n + 1)
                pe.wait_ge(move_ready, n + 1)
                wait(pe, added, n - 1)
                for half in range(2):
                    last = nc.tensor.matmul(psB[s][:, half, 0:C], move[s][:, half * P:(half + 1) * P], wsum[s][:, :],
                                            start=True, stop=True)
                last.then_inc(moved, 1)

            def group(n, s):
                pe.wait_ge(hot_ready, n + 1)
                if weigh:
                    pe.wait_ge(val_ready, n + 1)
                else:
                    pe.wait_ge(landed[s], (n - s) * (8 * T) + 16 * T)
                wait(pe, wsum_ready, n - 1)
                for t in range(T):
                    last = nc.tensor.matmul(psW[s][:, 0:C], hot[s][:, t, :], val[s][:, t, :],
                                            start=(t == 0), stop=(t == T - 1))
                last.then_inc(summed, 1)
                if not (isinstance(n, int) and n < 1):
                    onto_blocks(n - 1, 1 - s)

            def body():
                pairs(pe, G1, group)
                onto_blocks(G1 - 1, 1)

            when(pe, flag, body)


def stray_edges(nc, prefix, table, row, gr, C, ACC, weigh, flag):
    with ExitStack() as stack:
        m = Mem(nc, stack, prefix)
        stage = m.sb("stage", [P, T], I32)
        rows = m.sb("rows", [P, T, row])
        hot = m.sb("hot", [P, T, W])
        d = m.sb("d", [P, T])
        inside = m.sb("inside", [P, T])
        node = m.sb("node", [P, T])
        psB = m.ps("psB", [P, 2, 512])
        if weigh:
            val = m.sb("val", [P, T, C])
            prod = m.sb("prod", [P, T, 2, MC])
            msg = m.sb("msg", [P, T, MC])
            sco = m.sb("sco", [P, T, H])
        else:
            val = rows
        step = m.sem("step")
        staged = m.sem("staged")
        gathering = m.sem("gathering")
        landed = m.sem("landed")
        scores_ready = m.sem("scores_ready")
        weights_ready = m.sem("weights_ready")
        hot_ready = m.sem("hot_ready")
        summed = m.sem("summed")
        rows_seen = m.sem("rows_seen")
        block = stack.enter_context(nc.Block())
        STEPS = 5 + (3 + H if weigh else 0) + HB * 2

        @block.gpsimd
        def _(pool):
            def body():
                with pool.Fori(0, G1) as g:
                    pool.wait_ge(staged, g + 1)
                    pool.sem_inc(gathering, 1)
                    for t in range(T):
                        pool.indirect_dma_start(
                            out=rows[:, t, :], out_offset=None, in_=table,
                            in_offset=bass.IndirectOffsetOnAxis(ap=stage[:, t:t + 1], axis=0),
                        ).then_inc(landed, 16)

            when(pool, flag, body)

        @block.vector
        def _(dve):
            def body():
                with dve.Fori(0, G1) as g:
                    nc.vector.tensor_scalar(stage[:, :], gr.src[:, at(g, T)], N - 1, 0,
                                            ALU.min, ALU.max).then_inc(staged, 1)
                    link = Steps(dve, step, g * STEPS)
                    rel = gr.rel[:, at(g, T)]
                    link(nc.vector.tensor_scalar(d[:, :], rel, gr.first[:, at(g)], None, ALU.add))
                    link(nc.vector.tensor_scalar(inside[:, :], rel, float(P), None, ALU.is_lt))
                    link(nc.vector.scalar_tensor_tensor(inside[:, :], rel, 0.0, inside[:, :], ALU.is_ge, ALU.mult))
                    link(nc.vector.scalar_tensor_tensor(inside[:, :], d[:, :], 1.0, inside[:, :], ALU.add, ALU.mult))
                    link.mark(nc.vector.tensor_tensor(node[:, :], d[:, :], inside[:, :], ALU.subtract))
                    if weigh:
                        dve.wait_ge(landed, g * (16 * T) + 16 * T)
                        link(nc.vector.tensor_tensor(prod[:, :, :, :],
                                                     rows[:, :, :].rearrange("p t (a c) -> p t a c", a=2),
                                                     weigh.attr[:, at(g, T), :].unsqueeze(3).to_broadcast([P, T, 2, MC]),
                                                     ALU.mult))
                        link(nc.vector.tensor_tensor(msg[:, :, :], prod[:, :, 0, :], prod[:, :, 1, :], ALU.add))
                        nsc = msg[:, :, OF:MC]
                        link(nc.vector.scalar_tensor_tensor(sco[:, :, :], nsc, 0.2, nsc, ALU.mult, ALU.max))
                        nc.vector.tensor_tensor(sco[:, :, :], sco[:, :, :],
                                                weigh.shift[:, :].unsqueeze(1).to_broadcast([P, T, H]),
                                                ALU.subtract).then_inc(scores_ready, 1)
                        dve.wait_ge(weights_ready, g + 1)
                        for hd in range(H):
                            link.mark(nc.vector.tensor_tensor(
                                val[:, :, hd * OF:(hd + 1) * OF], msg[:, :, 0:OF],
                                val[:, :, H * OF + hd:H * OF + hd + 1].to_broadcast([P, T, OF]), ALU.mult))
                    fixed = link.n
                    with dve.Fori(0, HB) as b:
                        link = Steps(dve, step, g * STEPS + b * 2 + fixed)
                        dve.wait_ge(step, link.base)
                        nc.vector.tensor_tensor(hot[:, :, :], gr.iota[:, :].unsqueeze(1).to_broadcast([P, T, W]),
                                                node[:, :].unsqueeze(2).to_broadcast([P, T, W]),
                                                ALU.is_equal).then_inc(hot_ready, 1)
                        dve.wait_ge(hot_ready, g * HB + b + 1)
                        link.mark(nc.vector.tensor_scalar(node[:, :], node[:, :], float(-W), None, ALU.add))
                        dve.wait_ge(summed, g * HB + b + 1)
                        link.mark(nc.vector.tensor_tensor(ACC[:, at(b, 2), :], ACC[:, at(b, 2), :],
                                                          psB[:, :, 0:C], ALU.add))

            when(dve, flag, body)

        if weigh:
            @block.scalar
            def _(act):
                def body():
                    with act.Fori(0, G1) as g:
                        act.wait_ge(scores_ready, g + 1)
                        nc.scalar.activation(val[:, :, H * OF:C], sco[:, :, :], ACT.Exp).then_inc(weights_ready, 1)

                when(act, flag, body)

        @block.tensor
        def _(pe):
            def body():
                with pe.Fori(0, G1) as g:
                    if not weigh:
                        pe.wait_ge(landed, g * (16 * T) + 16 * T)
                        pe.sem_inc(rows_seen, 1)
                    with pe.Fori(0, HB) as b:
                        pe.wait_ge(hot_ready, g * HB + b + 1)
                        for half in range(2):
                            for t in range(T):
                                last = nc.tensor.matmul(psB[:, half, 0:C], hot[:, t, half * P:(half + 1) * P],
                                                        val[:, t, :], start=(t == 0), stop=(t == T - 1))
                        last.then_inc(summed, 1)

            when(pe, flag, body)


def attention_bound(nc, prefix, keep, attr_in, attr, shift, smax):
    with ExitStack() as stack:
        m = Mem(nc, stack, prefix)
        big = m.sb("big", [P, 2 * H + 2])
        all_big = m.sb("all_big", [P, 2 * H + 2])
        t0 = m.sb("t0", [P, 2, H])
        loaded = m.sem("loaded")
        step = m.sem("step")
        big_ready = m.sem("big_ready")
        all_ready = m.sem("all_ready")
        block = stack.enter_context(nc.Block())

        @block.sync
        def _(sp):
            sp.dma_start(attr[:, :, :], attr_in.rearrange("p (e c) -> p e c", c=2)).then_inc(loaded, 16)

        @block.vector
        def _(dve):
            link = Steps(dve, step)
            link(nc.vector.memset(smax[:, :, :], NEG))
            nc.vector.tensor_reduce(big[:, 0:2 * H], keep[:, :, :].rearrange("p n c -> p c n"), AX.X, ALU.max,
                                    apply_absolute_value=True).then_inc(big_ready, 1)
            dve.wait_ge(loaded, 16)
            nc.vector.tensor_reduce(big[:, 2 * H:], attr[:, :, :].rearrange("p e c -> p c e"), AX.X, ALU.max,
                                    apply_absolute_value=True).then_inc(big_ready, 1)
            dve.wait_ge(all_ready, 1)
            link(nc.vector.tensor_tensor(t0[:, :, :], all_big[:, 0:2 * H].rearrange("p (a h) -> p a h", a=2),
                                         all_big[:, 2 * H:].unsqueeze(2).to_broadcast([P, 2, H]), ALU.mult))
            link(nc.vector.tensor_tensor(shift[:, :], t0[:, 0, :], t0[:, 1, :], ALU.add))

        @block.gpsimd
        def _(pool):
            pool.wait_ge(big_ready, 2)
            nc.gpsimd.partition_all_reduce(all_big[:, :], big[:, :], P, RED.max).then_inc(all_ready, 1)


def attention_gap(nc, prefix, gr, shift, smax, gap, again, again_stray):
    with ExitStack() as stack:
        m = Mem(nc, stack, prefix)
        top = m.sb("top", [P, H])
        all_top = m.sb("all_top", [P, H])
        far = m.sb("far", [P, H])
        most = m.sb("most", [P, 1])
        step = m.sem("step")
        top_ready = m.sem("top_ready")
        all_ready = m.sem("all_ready")
        block = stack.enter_context(nc.Block())

        @block.vector
        def _(dve):
            link = Steps(dve, step)
            nc.vector.tensor_reduce(top[:, :], smax[:, :, :].rearrange("p t h -> p h t"), AX.X,
                                    ALU.max).then_inc(top_ready, 1)
            dve.wait_ge(all_ready, 1)
            link(nc.vector.scalar_tensor_tensor(top[:, :], all_top[:, :], 0.2, all_top[:, :], ALU.mult, ALU.max))
            link(nc.vector.tensor_tensor(gap[:, :], top[:, :], shift[:, :], ALU.subtract))
            link(nc.vector.tensor_scalar(far[:, :], gap[:, :], -FAR, None, ALU.is_lt))
            link(nc.vector.tensor_reduce(most[:, :], far[:, :], AX.X, ALU.max))
            link(nc.vector.tensor_copy(again[:, :], most[:, :]))
            link(nc.vector.tensor_tensor(again_stray[:, :], most[:, :], gr.stray[:, :], ALU.mult))
            link(nc.vector.scalar_tensor_tensor(far[:, :], gap[:, :], most[:, 0:1], shift[:, :], ALU.mult, ALU.add))
            link(nc.vector.tensor_copy(shift[:, :], far[:, :]))
            link(nc.vector.tensor_scalar(far[:, :], gap[:, :], most[:, 0:1], None, ALU.mult))
            link(nc.vector.tensor_tensor(gap[:, :], gap[:, :], far[:, :], ALU.subtract))

        @block.gpsimd
        def _(pool):
            pool.wait_ge(top_ready, 1)
            nc.gpsimd.partition_all_reduce(all_top[:, :], top[:, :], P, RED.max).then_inc(all_ready, 1)


def zero_sums(nc, prefix, ACC, flag):
    with ExitStack() as stack:
        block = stack.enter_context(nc.Block())

        @block.vector
        def _(dve):
            when(dve, flag, lambda: nc.vector.memset(ACC[:, :, :], 0.0))


def attention_finish(nc, prefix, X, ACC, gap):
    with ExitStack() as stack:
        m = Mem(nc, stack, prefix)
        eps = m.sb("eps", [P, H])
        rec = m.sb("rec", [P, NB, H])
        step = m.sem("step")
        eps_ready = m.sem("eps_ready")
        block = stack.enter_context(nc.Block())

        @block.vector
        def _(dve):
            link = Steps(dve, step)
            dve.wait_ge(eps_ready, 1)
            link(nc.vector.tensor_scalar(eps[:, :], eps[:, :], 1e-10, None, ALU.mult))
            link(nc.vector.tensor_tensor(rec[:, :, :], ACC[:, :, H * OF:AC],
                                         eps[:, :].unsqueeze(1).to_broadcast([P, NB, H]), ALU.add))
            link(nc.vector.reciprocal(rec[:, :, :], rec[:, :, :]))
            for hd in range(H):
                link.mark(nc.vector.tensor_tensor(ACC[:, :, hd * OF:(hd + 1) * OF], ACC[:, :, hd * OF:(hd + 1) * OF],
                                                  rec[:, :, hd:hd + 1].to_broadcast([P, NB, OF]), ALU.mult))
            dve.wait_ge(step, link.n)
            link(nc.vector.tensor_tensor(X[:, :, :], X[:, :, :], ACC[:, :, 0:D], ALU.add))

        @block.scalar
        def _(act):
            nc.scalar.activation(eps[:, :], gap[:, :], ACT.Exp).then_inc(eps_ready, 1)


def routing_tables(nc, prefix, keep, table_dst, AGG):
    with ExitStack() as stack:
        m = Mem(nc, stack, prefix)
        V = EX0 * H
        top = m.sb("top", [P, H])
        all_top = m.sb("all_top", [P, H])
        t0 = m.sb("t0", [P, NB, H])
        t1 = m.sb("t1", [P, NB, H])
        rows = m.sb("rows", [P, NB, 2 * H])
        step = m.sem("step")
        top_ready = m.sem("top_ready")
        all_ready = m.sem("all_ready")
        rows_ready = m.sem("rows_ready")
        own_ready = m.sem("own_ready")
        weight_ready = m.sem("weight_ready")
        stored = m.sem("stored")
        block = stack.enter_context(nc.Block())
        A = AGG[:, :, :, :].rearrange("p n a c -> p (n a) c")

        @block.vector
        def _(dve):
            link = Steps(dve, step)
            nc.vector.tensor_reduce(top[:, :], keep[:, :, V:V + H].rearrange("p n c -> p c n"), AX.X,
                                    ALU.max).then_inc(top_ready, 1)
            link(nc.vector.tensor_tensor(t1[:, :, :], keep[:, :, V:V + H], keep[:, :, V + H:], ALU.add))
            dve.wait_ge(all_ready, 1)
            link(nc.vector.tensor_tensor(t0[:, :, :], keep[:, :, V + H:],
                                         all_top[:, :].unsqueeze(1).to_broadcast([P, NB, H]), ALU.add))
            nc.vector.tensor_copy(rows[:, :, 0:H], keep[:, :, V + H:]).then_inc(rows_ready, 1)
            nc.vector.scalar_tensor_tensor(rows[:, :, H:], t0[:, :, :], 0.2, t0[:, :, :], ALU.mult,
                                           ALU.max).then_inc(rows_ready, 1)
            dve.wait_ge(rows_ready, 2)
            link(nc.vector.scalar_tensor_tensor(t0[:, :, :], t1[:, :, :], 0.2, t1[:, :, :], ALU.mult, ALU.max))
            nc.vector.tensor_tensor(t0[:, :, :], t0[:, :, :], rows[:, :, H:], ALU.subtract).then_inc(own_ready, 1)
            dve.wait_ge(weight_ready, 1)
            link(nc.vector.tensor_tensor(A[:, :, 0:V].rearrange("p n (h e) -> p n h e", e=EX0),
                                         keep[:, :, 0:V].rearrange("p n (h e) -> p n h e", e=EX0),
                                         A[:, :, V:].unsqueeze(3).to_broadcast([P, NB, H, EX0]), ALU.mult))

        @block.scalar
        def _(act):
            act.wait_ge(own_ready, 1)
            nc.scalar.activation(A[:, :, V:], t0[:, :, :], ACT.Exp).then_inc(weight_ready, 1)

        @block.gpsimd
        def _(pool):
            pool.wait_ge(top_ready, 1)
            nc.gpsimd.partition_all_reduce(all_top[:, :], top[:, :], P, RED.max).then_inc(all_ready, 1)

        @block.sync
        def _(sp):
            sp.wait_ge(rows_ready, 2)
            sp.dma_start(table_dst.rearrange("(n p) c -> p n c", p=P), rows[:, :, :]).then_inc(stored, 16)
            sp.wait_ge(stored, 16)


def routing_with_experts(nc, prefix, table_src, table_dst, src_in, dst_in, gr, AGG, t_hT, t_y, w1, b1, w2, b2):
    with ExitStack() as stack:
        m = Mem(nc, stack, prefix)
        V = EX0 * H
        TH = T // 2
        src = m.sb("src", [P, (G2 + 2) * T], I32)
        dst = m.sb("dst", [P, (G2 + 2) * T], I32)
        ints = m.sb("ints", [P, G2 * T], I32)
        lo = m.sb("lo", [P, G2 * T])
        hi = m.sb("hi", [P, G2 * T])
        stage = [[m.sb(f"stage{s}{e}", [P, T], I32) for e in range(2)] for s in range(2)]
        rows = [m.sb(f"rows{s}", [P, T, V + H]) for s in range(2)]
        rowd = [m.sb(f"rowd{s}", [P, T, 2 * H]) for s in range(2)]
        hot = [m.sb(f"hot{s}", [P, T, W], F32R) for s in range(2)]
        hoth = m.sb("hoth", [P, T, HB])
        sco = m.sb("sco", [P, T, H])
        sc2 = m.sb("sc2", [P, T, H])
        val = m.sb("val", [P, T, SC])
        part = [m.sb(f"part{k}", [P, T, SC], F32R) for k in range(2)]
        wide = [[m.sb(f"wide{s}{k}", [P, TH, HB, SC], F32R) for k in range(2)] for s in range(2)]
        zero = m.sb("zero", [P, HB * SC], F32R)
        hT = m.sb("hT", [P, KD, W])
        hid = [m.sb(f"hid{s}", [P, M0, W]) for s in range(2)]
        y = [m.sb(f"y{s}", [P, 2, D]) for s in range(2)]
        sums = m.ps("sums", [P, 2, 512])
        psH = [m.ps(f"psH{j}", [P, W]) for j in range(M0)]
        psY = [m.ps(f"psY{s}", [P, 2, D]) for s in range(2)]
        loaded = m.sem("loaded")
        step = m.sem("step")
        staged = m.sem("staged")
        gathering = m.sem("gathering")
        landed = [m.sem(f"landed{s}") for s in range(2)]
        rows_used = m.sem("rows_used")
        scores_ready = m.sem("scores_ready")
        weights_ready = m.sem("weights_ready")
        val_ready = m.sem("val_ready")
        high_ready = m.sem("high_ready")
        wide_ready = m.sem("wide_ready")
        summed = m.sem("summed")
        added = m.sem("added")
        zero_ready = m.sem("zero_ready")
        hoth_ready = m.sem("hoth_ready")
        hT_in = m.sem("hT_in")
        hid_made = m.sem("hid_made")
        hid_ready = m.sem("hid_ready")
        y_made = m.sem("y_made")
        y_ready = m.sem("y_ready")
        y_stored = [m.sem(f"y_stored{s}") for s in range(2)]
        block = stack.enter_context(nc.Block())
        UNITS = HB * EX0

        def steps(eng, group, unit, tail):
            for e in range(EX0):
                group(e, e % 2)
                unit(e, e)
            with eng.Fori(1, HB) as i:
                for e in range(EX0):
                    group(i * EX0 + e, e % 2)
                    unit(i * EX0 + e, e)
            group(UNITS, 0)
            tail()
            group(UNITS + 1, 1)
            with eng.Fori(UNITS // 2 + 1, G2 // 2) as j:
                for s in range(2):
                    group(j * 2 + s, s)

        @block.sync
        def _(sp):
            sp.dma_start(src[:, :], src_in).then_inc(loaded, 16)
            sp.dma_start(dst[:, :], dst_in).then_inc(loaded, 16)
            with sp.Fori(0, HB) as i:
                for e in range(EX0):
                    sp.wait_ge(y_ready, i * EX0 + (e + 1))
                    sp.dma_start(t_y[at(i), :, e, :].rearrange("a p c -> (a p) c"),
                                 y[e % 2][:, :, :].rearrange("p q d -> p (q d)")).then_inc(y_stored[e % 2], 16)
            for s in range(2):
                sp.wait_ge(y_stored[s], 16 * (UNITS // 2))

        @block.gpsimd
        def _(pool):
            def gather(n, s):
                pool.wait_ge(staged, n * 2 + 2)
                wait(pool, rows_used, n - 1)
                pool.sem_inc(gathering, 1)
                for t in range(T):
                    for k, (to, table) in enumerate(((rows, table_src), (rowd, table_dst))):
                        pool.indirect_dma_start(
                            out=to[s][:, t, :], out_offset=None, in_=table,
                            in_offset=bass.IndirectOffsetOnAxis(ap=stage[s][k][:, t:t + 1], axis=0),
                        ).then_inc(landed[s], 16)

            pairs(pool, G2, gather)

        @block.vector
        def _(dve):
            nc.vector.memset(zero[:, :].bitcast(F32), 0.0).then_inc(zero_ready, 1)
            dve.wait_ge(loaded, 32)
            link = Steps(dve, step)
            link(nc.vector.tensor_single_scalar(ints[:, :], dst[:, 0:G2 * T], W - 1, ALU.bitwise_and))
            link(nc.vector.tensor_copy(lo[:, :], ints[:, :]))
            link(nc.vector.tensor_single_scalar(ints[:, :], dst[:, 0:G2 * T], 8, ALU.arith_shift_right))
            link(nc.vector.tensor_copy(hi[:, :], ints[:, :]))
            setup = link.n

            def put(n, s):
                for k, of in enumerate((src, dst)):
                    nc.vector.tensor_scalar(stage[s][k][:, :], of[:, at(n, T)], N - 1, 0,
                                            ALU.min, ALU.max).then_inc(staged, 1)

            LINKS = 2

            def group(n, s):
                link = Steps(dve, step, n * LINKS + setup)
                wait(dve, summed, n * 2 - 2)
                for t in range(T):
                    nc.vector.tensor_scalar(hot[s][:, t, :], gr.iota[:, :], lo[:, at(n * T + t)], None,
                                            ALU.is_equal)
                wait(dve, wide_ready, n * 2)
                nc.vector.tensor_tensor(hoth[:, :, :], gr.iota[:, 0:HB].unsqueeze(1).to_broadcast([P, T, HB]),
                                        hi[:, at(n, T)].unsqueeze(2).to_broadcast([P, T, HB]),
                                        ALU.is_equal).then_inc(hoth_ready, 1)
                dve.wait_ge(landed[s], (n - s) * (16 * T) + 32 * T)
                link(nc.vector.tensor_tensor(sco[:, :, :], rows[s][:, :, V:], rowd[s][:, :, 0:H], ALU.add))
                link(nc.vector.scalar_tensor_tensor(sc2[:, :, :], sco[:, :, :], 0.2, sco[:, :, :],
                                                    ALU.mult, ALU.max))
                assert link.n == LINKS
                nc.vector.tensor_tensor(sc2[:, :, :], sc2[:, :, :], rowd[s][:, :, H:],
                                        ALU.subtract).then_inc(scores_ready, 1)
                put(n + 2, s)
                dve.wait_ge(weights_ready, n + 1)
                nc.vector.tensor_tensor(val[:, :, 0:V].rearrange("p t (h e) -> p t h e", e=EX0),
                                        rows[s][:, :, 0:V].rearrange("p t (h e) -> p t h e", e=EX0),
                                        val[:, :, V:].unsqueeze(3).to_broadcast([P, T, H, EX0]),
                                        ALU.mult).then_inc(rows_used, 1)
                dve.wait_ge(high_ready, n + 1)
                nc.vector.tensor_tensor(part[1][:, :, :], val[:, :, :], part[0][:, :, :],
                                        ALU.subtract).then_inc(val_ready, 1)
                dve.wait_ge(val_ready, n + 1)
                dve.wait_ge(hoth_ready, n + 1)
                for half in range(2):
                    wait(dve, summed, n * 2 + half - 1)
                    for k in range(2):
                        last = nc.vector.tensor_tensor(
                            wide[half][k][:, :, :, :],
                            hoth[:, half * TH:(half + 1) * TH, :].unsqueeze(3).to_broadcast([P, TH, HB, SC]),
                            part[k][:, half * TH:(half + 1) * TH, :].unsqueeze(2).to_broadcast([P, TH, HB, SC]),
                            ALU.mult)
                    last.then_inc(wide_ready, 1)

            def take(u, e):
                s = e % 2
                dve.wait_ge(y_made, u + 1)
                wait(dve, y_stored[s], (u - s) * 8)
                nc.vector.tensor_tensor(y[s][:, :, :], psY[s][:, :, :],
                                        b2[:, e, :].unsqueeze(1).to_broadcast([P, 2, D]),
                                        ALU.add).then_inc(y_ready, 1)

            def unit(u, e):
                if not (isinstance(u, int) and u < 2):
                    take(u - 2, (e - 2) % EX0)

            def tail():
                take(UNITS - 2, 2)
                take(UNITS - 1, 3)

            put(0, 0)
            put(1, 1)
            steps(dve, group, unit, tail)
            dve.wait_ge(summed, G2 * 2 + 1)
            for half in range(2):
                nc.vector.tensor_tensor(AGG[:, :, half, :], AGG[:, :, half, :],
                                        sums[:, half, 0:HB * SC].rearrange("p (n c) -> p n c", c=SC),
                                        ALU.add).then_inc(added, 1)
            dve.wait_ge(added, 2)

        @block.scalar
        def _(act):
            def load_hT(i):
                act.dma_start(hT[:, :, :].rearrange("p k c -> p (k c)"),
                              t_hT[at(i), :, :].rearrange("a p c -> (a p) c")).then_inc(hT_in, 16)

            def group(n, s):
                act.wait_ge(scores_ready, n + 1)
                wait(act, val_ready, n)
                nc.scalar.activation(val[:, :, V:], sc2[:, :, :], ACT.Exp).then_inc(weights_ready, 1)
                act.wait_ge(rows_used, n + 1)
                wait(act, wide_ready, n * 2)
                nc.scalar.activation(part[0][:, :, :], val[:, :, :], ACT.Copy).then_inc(high_ready, 1)

            def hidden(u, e):
                wait(act, y_made, u - 1)
                for j in range(M0):
                    act.wait_ge(hid_made, u * M0 + (j + 1))
                    nc.scalar.activation(hid[e % 2][:, j, :], psH[j][:, :], ACT.Gelu,
                                         bias=b1[:, e, j:j + 1]).then_inc(hid_ready, 1)

            def unit(u, e):
                if not (isinstance(u, int) and u < 1):
                    hidden(u - 1, (e - 1) % EX0)
                if e == 0:
                    if isinstance(u, int):
                        load_hT(0)
                    else:
                        load_hT(u // EX0)

            steps(act, group, unit, lambda: hidden(UNITS - 1, EX0 - 1))

        @block.tensor
        def _(pe):
            def group(n, s):
                first = isinstance(n, int) and n == 0
                for half in range(2):
                    pe.wait_ge(wide_ready, n * 2 + (half + 1))
                    for t in range(TH):
                        for k in range(2):
                            for b in range(2):
                                last = nc.tensor.matmul(
                                    sums[:, b, 0:HB * SC], hot[s][:, half * TH + t, b * P:(b + 1) * P],
                                    wide[half][k][:, t, :, :].rearrange("p n c -> p (n c)"),
                                    start=first and half == 0 and t == 0 and k == 0, stop=False)
                    last.then_inc(summed, 1)

            def hidden(u, e):
                pe.wait_ge(hT_in, (u - e) * (16 // EX0) + 16)
                for j in range(M0):
                    wait(pe, hid_ready, u * M0 + (j - M0 + 1))
                    for k in range(KD):
                        last = nc.tensor.matmul(psH[j][:, :], w1[:, e, k, j * P:(j + 1) * P], hT[:, k, :],
                                                start=(k == 0), stop=(k == KD - 1))
                    last.then_inc(hid_made, 1)

            def rows_of(u, e):
                pe.wait_ge(hid_ready, u * M0 + M0)
                wait(pe, y_ready, u - 1)
                for q in range(2):
                    for k in range(M0):
                        last = nc.tensor.matmul(psY[e % 2][:, q, :], hid[e % 2][:, k, q * P:(q + 1) * P],
                                                w2[:, e, k, :], start=(k == 0), stop=(k == M0 - 1))
                last.then_inc(y_made, 1)

            def unit(u, e):
                hidden(u, e)
                if not (isinstance(u, int) and u < 1):
                    rows_of(u - 1, (e - 1) % EX0)

            steps(pe, group, unit, lambda: rows_of(UNITS - 1, EX0 - 1))
            pe.wait_ge(zero_ready, 1)
            for b in range(2):
                last = nc.tensor.matmul(sums[:, b, 0:HB * SC], zero[:, 0:P], zero[:, :], start=False, stop=True)
            last.then_inc(summed, 1)


def add_experts(nc, prefix, X, GT, t_y):
    with ExitStack() as stack:
        m = Mem(nc, stack, prefix)
        y = [m.sb(f"y{s}", [P, EX0, 2, D]) for s in range(3)]
        y_in = [m.sem(f"y_in{s}") for s in range(3)]
        added = m.sem("added")
        block = stack.enter_context(nc.Block())

        def thirds(eng, body):
            for s in range(3):
                body(s, s)
            with eng.Fori(1, HB // 3) as i:
                for s in range(3):
                    body(i * 3 + s, s)
            for n in range(HB - HB % 3, HB):
                body(n, n % 3)

        @block.sync
        def _(sp):
            def pair(n, s):
                wait(sp, added, (n - 2) * (2 * EX0))
                sp.dma_start(y[s][:, :, :, :].rearrange("p e q d -> p (e q d)"),
                             t_y[at(n), :, :, :].rearrange("a p e c -> (a p) (e c)")).then_inc(y_in[s], 16)

            thirds(sp, pair)

        @block.vector
        def _(dve):
            def pair(n, s):
                if isinstance(n, int):
                    dve.wait_ge(y_in[s], (n // 3 + 1) * 16)
                else:
                    dve.wait_ge(y_in[s], (n // 3) * 16 + 16)
                for e in range(EX0):
                    for q in range(2):
                        b = n * 2 + q
                        if e > 0:
                            dve.wait_ge(added, n * (2 * EX0) + (2 * e + q - 1))
                        nc.vector.scalar_tensor_tensor(X[:, at(b), :], y[s][:, e, q, :].unsqueeze(1),
                                                       GT[:, at(b), e], X[:, at(b), :],
                                                       ALU.mult, ALU.add).then_inc(added, 1)

            thirds(dve, pair)


def routing_scores(nc, prefix, AGG, b_gat, gamma, beta, S):
    with ExitStack() as stack:
        m = Mem(nc, stack, prefix)
        V = EX0 * H
        A = AGG[:, :, :, :].rearrange("p n a c -> p (n a) c")
        y = m.sb("y", [P, NB, V])
        sq = m.sb("sq", [P, NB, V])
        rec = m.sb("rec", [P, NB, H])
        t0 = m.sb("t0", [P, NB])
        t1 = m.sb("t1", [P, NB])
        step = m.sem("step")
        var_ready = m.sem("var_ready")
        std_ready = m.sem("std_ready")
        block = stack.enter_context(nc.Block())
        full = [P, NB, V]

        @block.vector
        def _(dve):
            link = Steps(dve, step)
            link(nc.vector.tensor_scalar(rec[:, :, :], A[:, :, V:], 1e-16, None, ALU.add))
            link(nc.vector.reciprocal(rec[:, :, :], rec[:, :, :]))
            link(nc.vector.tensor_tensor(y[:, :, :].rearrange("p n (h e) -> p n h e", e=EX0),
                                         A[:, :, 0:V].rearrange("p n (h e) -> p n h e", e=EX0),
                                         rec[:, :, :].unsqueeze(3).to_broadcast([P, NB, H, EX0]), ALU.mult))
            link(nc.vector.tensor_tensor(y[:, :, :], y[:, :, :], b_gat[:, :].unsqueeze(1).to_broadcast(full), ALU.add))
            link(nc.vector.tensor_reduce(t0[:, :], y[:, :, :], AX.X, ALU.add))
            link(nc.vector.tensor_scalar(t0[:, :], t0[:, :], 1.0 / V, None, ALU.mult))
            link(nc.vector.tensor_tensor(y[:, :, :], y[:, :, :], t0[:, :].unsqueeze(2).to_broadcast(full), ALU.subtract))
            link(nc.vector.tensor_tensor(sq[:, :, :], y[:, :, :], y[:, :, :], ALU.mult))
            link(nc.vector.tensor_reduce(t0[:, :], sq[:, :, :], AX.X, ALU.add))
            nc.vector.tensor_scalar(t0[:, :], t0[:, :], 1.0 / V, LN_EPS, ALU.mult, ALU.add).then_inc(var_ready, 1)
            dve.wait_ge(std_ready, 1)
            link(nc.vector.reciprocal(t1[:, :], t1[:, :]))
            link(nc.vector.tensor_tensor(y[:, :, :], y[:, :, :], t1[:, :].unsqueeze(2).to_broadcast(full), ALU.mult))
            link(nc.vector.tensor_tensor(y[:, :, :], y[:, :, :], gamma[:, :].unsqueeze(1).to_broadcast(full), ALU.mult))
            link(nc.vector.tensor_tensor(y[:, :, :], y[:, :, :], beta[:, :].unsqueeze(1).to_broadcast(full), ALU.add))
            link(nc.vector.tensor_reduce(S[:, :, :], y[:, :, :].rearrange("p n (h e) -> p n e h", e=EX0), AX.X, ALU.add))
            link(nc.vector.tensor_scalar(S[:, :, :], S[:, :, :], 1.0 / H, None, ALU.mult))

        @block.scalar
        def _(act):
            act.wait_ge(var_ready, 1)
            nc.scalar.activation(t1[:, :], t0[:, :], ACT.Sqrt).then_inc(std_ready, 1)


def experts(nc, prefix, X, HT, GT, ex, sizes, weights, biases, out_bias, funcs, out_dram):
    with ExitStack() as stack:
        m = Mem(nc, stack, prefix)
        L = len(sizes)
        hid = [[m.sb(f"hid{l}{s}", [P, sizes[l], W]) for s in range(2)] for l in range(L)]
        psH = [m.ps(f"psH{s}", [P, W]) for s in range(4)]
        psY = [m.ps(f"psY{s}", [P, D]) for s in range(4)]
        PER = ex * sum(sizes)
        assert PER % 4 == 0 and (ex * 2) % 4 == 0
        order = [(l, e - l) for e in range(ex + L) for l in reversed(range(L + 1)) if 0 <= e - l < ex]
        pos, c = {}, 0
        for l, e in order:
            if l < L:
                pos[l, e] = c
                c += sizes[l]
        made = m.sem("made")
        hid_ready = m.sem("hid_ready")
        y_ready = m.sem("y_ready")
        y_added = m.sem("y_added")
        bias_added = m.sem("bias_added")
        stored = m.sem("stored")
        block = stack.enter_context(nc.Block())

        @block.tensor
        def _(pe):
            pe.sem_inc(y_ready, 4)
            with pe.Fori(0, HB) as i:
                for l, e in order:
                    if l > 0:
                        pe.wait_ge(hid_ready, i * PER + (pos[l - 1, e] + sizes[l - 1] + 4))
                    if l < L:
                        for j in range(sizes[l]):
                            c = pos[l, e] + j
                            pe.wait_ge(hid_ready, i * PER + (c + 1))
                            K = KD if l == 0 else sizes[l - 1]
                            for k in range(K):
                                x = HT[:, k, at(i, W)] if l == 0 else hid[l - 1][e % 2][:, k, :]
                                last = nc.tensor.matmul(psH[c % 4][:, :], weights[l][:, e, k, j * P:(j + 1) * P],
                                                        x, start=(k == 0), stop=(k == K - 1))
                            last.then_inc(made, 1)
                    else:
                        for q in range(2):
                            c = 2 * e + q
                            pe.wait_ge(y_added, i * (2 * ex) + (c + 1))
                            for k in range(sizes[-1]):
                                last = nc.tensor.matmul(psY[c % 4][:, :], hid[-1][e % 2][:, k, q * P:(q + 1) * P],
                                                        weights[L][:, e, k, :], start=(k == 0),
                                                        stop=(k == sizes[-1] - 1))
                            last.then_inc(y_ready, 1)

        @block.scalar
        def _(act):
            act.sem_inc(hid_ready, 4)
            with act.Fori(0, HB) as i:
                for l, e in order:
                    if l == L:
                        continue
                    act.wait_ge(y_ready, i * (2 * ex) + (2 * e + 2))
                    for j in range(sizes[l]):
                        c = pos[l, e] + j
                        act.wait_ge(made, i * PER + (c + 1))
                        nc.scalar.activation(hid[l][e % 2][:, j, :], psH[c % 4][:, :], funcs[l],
                                             bias=biases[l][:, e, j:j + 1]).then_inc(hid_ready, 1)

        @block.vector
        def _(dve):
            dve.sem_inc(y_added, 4)
            with dve.Fori(0, HB) as i:
                for e in range(ex):
                    for q in range(2):
                        b = i * 2 + q
                        if e > 0:
                            dve.wait_ge(bias_added, i * (2 * ex) + 2 * (e - 1) + q + 1)
                        nc.vector.scalar_tensor_tensor(X[:, at(b), :], out_bias[:, e:e + 1, :], GT[:, at(b), e],
                                                       X[:, at(b), :], ALU.mult, ALU.add).then_inc(bias_added, 1)
                dve.wait_ge(bias_added, i * (2 * ex) + 2 * ex)
                for e in range(ex):
                    for q in range(2):
                        b = i * 2 + q
                        c = 2 * e + q
                        dve.wait_ge(y_ready, i * (2 * ex) + (c + 5))
                        if e > 0:
                            dve.wait_ge(y_added, i * (2 * ex) + (c + 3))
                        nc.vector.scalar_tensor_tensor(X[:, at(b), :],
                                                       psY[c % 4][:, :].rearrange("p (a d) -> p a d", a=1),
                                                       GT[:, at(b), e], X[:, at(b), :],
                                                       ALU.mult, ALU.add).then_inc(y_added, 1)

        if out_dram is not None:
            @block.sync
            def _(sp):
                with sp.Fori(0, VB // 2) as i:
                    sp.wait_ge(y_added, i * (2 * ex) + (2 * ex + 4))
                    sp.dma_start(out_dram[at(i, W), :].rearrange("(b p) d -> p b d", p=P),
                                 X[:, at(i, 2), :]).then_inc(stored, 16)
                sp.wait_ge(y_added, (VB // 2 + 1) * (2 * ex) + 4)
                sp.dma_start(out_dram[VB * P:N, :], X[0:VR, VB, :]).then_inc(stored, 16)
                sp.wait_ge(stored, 16 * (VB // 2 + 1))


def router(nc, prefix, HT, w1, b1, w2, b2, LG):
    with ExitStack() as stack:
        m = Mem(nc, stack, prefix)
        hid = [m.sb(f"hid{s}", [P, W]) for s in range(2)]
        top = m.sb("top", [P, NB])
        psH = [m.ps(f"psH{s}", [P, W]) for s in range(2)]
        psL = [m.ps(f"psL{s}", [P, 2, EX1]) for s in range(2)]
        made = m.sem("made")
        hid_ready = m.sem("hid_ready")
        logits_ready = m.sem("logits_ready")
        logits_taken = m.sem("logits_taken")
        step = m.sem("step")
        d_ready = m.sem("d_ready")
        exp_ready = m.sem("exp_ready")
        block = stack.enter_context(nc.Block())
        full = [P, NB, EX1]

        def groups(eng, body):
            with eng.Fori(0, HB // 2) as i:
                for s in range(2):
                    body(i * 2 + s, s)
            body(HB - 1, 0)

        @block.tensor
        def _(pe):
            pe.sem_inc(logits_ready, 2)

            def pair(n, s):
                pe.wait_ge(hid_ready, n + 1)
                for k in range(KD):
                    last = nc.tensor.matmul(psH[s][:, :], w1[:, k, :], HT[:, k, at(n, W)],
                                            start=(k == 0), stop=(k == KD - 1))
                last.then_inc(made, 1)
                pe.wait_ge(hid_ready, n + 3)
                pe.wait_ge(logits_taken, n + 1)
                for q in range(2):
                    last = nc.tensor.matmul(psL[s][:, q, :], hid[s][:, q * P:(q + 1) * P], w2[:, :],
                                            start=True, stop=True)
                last.then_inc(logits_ready, 1)

            groups(pe, pair)

        @block.scalar
        def _(act):
            act.sem_inc(hid_ready, 2)

            def pair(n, s):
                act.wait_ge(made, n + 1)
                act.wait_ge(logits_ready, n + 1)
                nc.scalar.activation(hid[s][:, :], psH[s][:, :], ACT.Relu, bias=b1[:, 0:1]).then_inc(hid_ready, 1)

            groups(act, pair)
            act.wait_ge(d_ready, 1)
            nc.scalar.activation(LG[:, :, :], LG[:, :, :], ACT.Exp).then_inc(exp_ready, 1)

        @block.vector
        def _(dve):
            dve.sem_inc(logits_taken, 2)

            def pair(n, s):
                dve.wait_ge(logits_ready, n + 3)
                nc.vector.tensor_tensor(LG[:, at(n, 2), :], psL[s][:, :, :],
                                        b2[:, :].unsqueeze(1).to_broadcast([P, 2, EX1]),
                                        ALU.add).then_inc(logits_taken, 1)

            groups(dve, pair)
            dve.wait_ge(logits_taken, HB + 2)
            link = Steps(dve, step)
            link(nc.vector.tensor_reduce(top[:, :], LG[:, :, :], AX.X, ALU.max))
            nc.vector.tensor_tensor(LG[:, :, :], LG[:, :, :], top[:, :].unsqueeze(2).to_broadcast(full),
                                    ALU.subtract).then_inc(d_ready, 1)
            dve.wait_ge(exp_ready, 1)
            link(nc.vector.tensor_reduce(top[:, :], LG[:, :, :], AX.X, ALU.add))
            link(nc.vector.reciprocal(top[:, :], top[:, :]))
            link(nc.vector.tensor_tensor(LG[:, :, :], LG[:, :, :], top[:, :].unsqueeze(2).to_broadcast(full),
                                         ALU.mult))


def normalize(nc, prefix, X, rstd, nmr, ACC, table):
    with ExitStack() as stack:
        m = Mem(nc, stack, prefix)
        ready = m.sem("ready")
        stored = m.sem("stored")
        block = stack.enter_context(nc.Block())

        @block.scalar
        def _(act):
            with act.Fori(0, NB) as n:
                nc.scalar.activation(ACC[:, at(n), :], X[:, at(n), :], ACT.Identity, bias=nmr[:, at(n)],
                                     scale=rstd[:, at(n)]).then_inc(ready, 1)

        @block.sync
        def _(sp):
            with sp.Fori(0, HB) as i:
                sp.wait_ge(ready, i * 2 + 2)
                sp.dma_start(table[at(i, W), :].rearrange("(b p) d -> p b d", p=P),
                             ACC[:, at(i, 2), :]).then_inc(stored, 16)
            sp.wait_ge(stored, 16 * HB)


def batch_normalized(nc, prefix, X, ACC, HT, ident, w, b, bn_w, bn_b):
    with ExitStack() as stack:
        m = Mem(nc, stack, prefix)
        rows = [m.sb(f"rows{s}", [P, D]) for s in range(2)]
        rT = [m.sb(f"rT{s}", [P, KD, P]) for s in range(2)]
        FS = 512
        NF = -(-N // FS)
        st = m.sb("st", [P, KD, NF, 6])
        mv = m.sb("mv", [P, KD, 2])
        sc = m.sb("sc", [P, KD])
        sh = m.sb("sh", [P, KD])
        psT = [m.ps(f"psT{s}", [P, KD, P]) for s in range(2)]
        psH = [m.ps(f"psH{s}", [P, KD, P]) for s in range(2)]
        rows_ready = m.sem("rows_ready")
        turned = m.sem("turned")
        rT_ready = m.sem("rT_ready")
        made = m.sem("made")
        h_ready = m.sem("h_ready")
        step = m.sem("step")
        var_ready = m.sem("var_ready")
        std_ready = m.sem("std_ready")
        scale_ready = m.sem("scale_ready")
        out_rows = m.sem("out_rows")
        out_turned = m.sem("out_turned")
        added = m.sem("added")
        block = stack.enter_context(nc.Block())

        @block.scalar
        def _(act):
            act.sem_inc(h_ready, 2)
            with act.Fori(0, HB) as i:
                for s in range(2):
                    n = i * 2 + s
                    act.wait_ge(turned, n + 1)
                    nc.scalar.activation(rows[s][:, :].rearrange("p (a d) -> p a d", a=1), ACC[:, at(n), :],
                                         ACT.Copy).then_inc(rows_ready, 1)
                for s in range(2):
                    n = i * 2 + s
                    act.wait_ge(made, n + 3)
                    for j in range(KD):
                        last = nc.scalar.activation(HT[:, j, at(n, P)], psH[s][:, j, :], ACT.Identity,
                                                    bias=b[:, j:j + 1])
                    last.then_inc(h_ready, 1)
            act.wait_ge(var_ready, 1)
            nc.scalar.activation(sc[:, :], sc[:, :], ACT.Sqrt).then_inc(std_ready, 1)
            act.wait_ge(scale_ready, 1)
            with act.Fori(0, HB) as i:
                for s in range(2):
                    n = i * 2 + s
                    act.wait_ge(out_turned, n + 1)
                    for j in range(KD):
                        last = nc.scalar.activation(rT[s][:, j, :], HT[:, j, at(n, P)], ACT.Identity,
                                                    bias=sh[:, j:j + 1], scale=sc[:, j:j + 1])
                    last.then_inc(out_rows, 1)

        @block.tensor
        def _(pe):
            pe.sem_inc(turned, 2)
            pe.sem_inc(made, 2)
            with pe.Fori(0, HB) as i:
                for s in range(2):
                    n = i * 2 + s
                    pe.wait_ge(rows_ready, n + 1)
                    pe.wait_ge(rT_ready, n + 1)
                    for k in range(KD):
                        last = nc.tensor.transpose(psT[s][:, k, :], rows[s][:, k * P:(k + 1) * P], ident[:, :])
                    last.then_inc(turned, 1)
                for s in range(2):
                    n = i * 2 + s
                    pe.wait_ge(rT_ready, n + 3)
                    pe.wait_ge(h_ready, n + 1)
                    for j in range(KD):
                        for k in range(KD):
                            last = nc.tensor.matmul(psH[s][:, j, :], w[:, k, j * P:(j + 1) * P], rT[s][:, k, :],
                                                    start=(k == 0), stop=(k == KD - 1))
                    last.then_inc(made, 1)
            pe.wait_ge(made, NB + 2)
            pe.sem_inc(out_turned, 2)
            with pe.Fori(0, HB) as i:
                for s in range(2):
                    n = i * 2 + s
                    pe.wait_ge(out_rows, n + 1)
                    pe.wait_ge(added, n + 1)
                    for j in range(KD):
                        last = nc.tensor.transpose(psT[s][:, j, :], rT[s][:, j, :], ident[:, :])
                    last.then_inc(out_turned, 1)

        @block.vector
        def _(dve):
            dve.sem_inc(rT_ready, 2)
            with dve.Fori(0, HB) as i:
                for s in range(2):
                    n = i * 2 + s
                    dve.wait_ge(turned, n + 3)
                    dve.wait_ge(made, n + 1)
                    nc.vector.tensor_copy(rT[s][:, :, :], psT[s][:, :, :]).then_inc(rT_ready, 1)
            dve.wait_ge(h_ready, NB + 2)
            link = Steps(dve, step)
            for j in range(KD):
                for f in range(NF):
                    link.mark(nc.vector.bn_stats(st[:, j, f, :], HT[:, j, f * FS:min(N, (f + 1) * FS)]))
            dve.wait_ge(step, link.n)
            for j in range(KD):
                link(nc.vector.bn_aggr(mv[:, j, :], st[:, j, :, :].rearrange("p f c -> p (f c)")))
            nc.vector.tensor_scalar(sc[:, :], mv[:, :, 1], LN_EPS, None, ALU.add).then_inc(var_ready, 1)
            dve.wait_ge(std_ready, 1)
            link(nc.vector.reciprocal(sc[:, :], sc[:, :]))
            link(nc.vector.tensor_tensor(sc[:, :], sc[:, :], bn_w[:, :], ALU.mult))
            link(nc.vector.tensor_tensor(sh[:, :], mv[:, :, 0], sc[:, :], ALU.mult))
            nc.vector.tensor_tensor(sh[:, :], bn_b[:, :], sh[:, :], ALU.subtract).then_inc(scale_ready, 1)
            dve.sem_inc(added, 2)
            with dve.Fori(0, HB) as i:
                for s in range(2):
                    n = i * 2 + s
                    dve.wait_ge(out_turned, n + 3)
                    nc.vector.tensor_tensor(X[:, at(n), :], X[:, at(n), :],
                                            psT[s][:, :, :].rearrange("p k c -> p (k c)").unsqueeze(1),
                                            ALU.add).then_inc(added, 1)


def load(nc, prefix, pairs):
    with ExitStack() as stack:
        m = Mem(nc, stack, prefix)
        loaded = m.sem("loaded")
        block = stack.enter_context(nc.Block())

        @block.sync
        def _(sp):
            for to, of in pairs:
                sp.dma_start(to, of).then_inc(loaded, 16)
            sp.wait_ge(loaded, 16 * len(pairs))


def constants(nc, prefix, ident, ACC, tri, ex):
    with ExitStack() as stack:
        m = Mem(nc, stack, prefix)
        zeroed = m.sem("zeroed")
        ident_done = m.sem("ident_done")
        tri_zeroed = m.sem("tri_zeroed")
        block = stack.enter_context(nc.Block())

        @block.gpsimd
        def _(pool):
            nc.gpsimd.memset(ident[:, :], 0.0).then_inc(zeroed, 1)
            pool.wait_ge(zeroed, 1)
            nc.gpsimd.affine_select(out=ident[:, :], in_=ident[:, :], compare_op=ALU.not_equal, fill=1.0,
                                    base=0, pattern=[[-1, P]], channel_multiplier=1).then_inc(ident_done, 1)

        @block.vector
        def _(dve):
            nc.vector.memset(ACC[:, :, :], 0.0)
            nc.vector.memset(tri[:, :, :], 0.0).then_inc(tri_zeroed, 1)
            dve.wait_ge(tri_zeroed, 1)
            for i in range(1, ex):
                nc.vector.memset(tri[:, i, 0:i], 1.0)


def score_columns(nc, prefix, wf, attn, wproj, wgat, att, wg):
    with ExitStack() as stack:
        m = Mem(nc, stack, prefix)
        V = EX0 * H
        prod = m.sb("prod", [P, KD, 2, V])
        psA = m.ps("psA", [P, 2, KD, H])
        made = m.sem("made")
        step = m.sem("step")
        block = stack.enter_context(nc.Block())

        @block.tensor
        def _(pe):
            for a in range(2):
                for k in range(KD):
                    last = nc.tensor.matmul(psA[:, a, k, :], wf[:, a, k * P:(k + 1) * P], attn[:, :],
                                            start=True, stop=True)
            last.then_inc(made, 1)

        @block.vector
        def _(dve):
            link = Steps(dve, step)
            for a in range(2):
                link.mark(nc.vector.tensor_tensor(prod[:, :, a, :], wgat[:, :, :],
                                                  att[:, a, :].unsqueeze(1).to_broadcast([P, KD, V]), ALU.mult))
            dve.wait_ge(step, 2)
            nc.vector.tensor_copy(wg[:, :, 0:V], wgat[:, :, :])
            for k in range(KD):
                nc.vector.tensor_reduce(wg[:, k, V:].rearrange("p (a h) -> p a h", a=2),
                                        prod[:, k, :, :].rearrange("p a (h e) -> p a h e", e=EX0), AX.X, ALU.add)
            dve.wait_ge(made, 1)
            for a in range(2):
                nc.vector.tensor_copy(wproj[:, :, a * MC + OF:(a + 1) * MC], psA[:, a, :, :])


def gnn_ffn(nc, x_in, src1, dst1, first1, attr, w_msg, w_rows, attn_t, w_gat, att, b_gat, gamma, beta,
            e0_w1, e0_b1, e0_w2, e0_b2, src2, dst2, w_gin, b_gin, bn_w, bn_b, r_w1, r_b1, r_w2, r_b2,
            e1_w1, e1_b1, e1_w2, e1_b2, e1_w3, e1_b3, out):
    V = EX0 * H
    t_msg = nc.dram_tensor("t_msg", [NB * P, 2 * MC], F32).ap()
    t_src = nc.dram_tensor("t_src", [NB * P, V + H], F32).ap()
    t_dst = nc.dram_tensor("t_dst", [NB * P, 2 * H], F32).ap()
    t_hT = nc.dram_tensor("t_hT", [HB, P, KD * W], F32).ap()
    t_y = nc.dram_tensor("t_y", [HB, P, EX0, 2 * D], F32).ap()
    t_row = nc.dram_tensor("t_row", [NB * P, D], F32).ap()
    with ExitStack() as whole:
        g = Mem(nc, whole, "all")
        X = g.sb("X", [P, NB, D])
        rstd = g.sb("rstd", [P, NB])
        nmr = g.sb("nmr", [P, NB])
        ident = g.sb("ident", [P, P])
        tri = g.sb("tri", [P, EX1, EX1])
        wg = g.sb("wg", [P, KD, V + 2 * H])
        gr = Graph(g)

        with ExitStack() as layer:
            a = Mem(nc, layer, "l0g")
            ACC = a.sb("ACC", [P, NB, AC])
            wproj = a.sb("wproj", [P, KD, 2 * MC])
            keep = a.sb("keep", [P, NB, 2 * H])
            shift = a.sb("shift", [P, H])
            smax = a.sb("smax", [P, T, H])
            gap = a.sb("gap", [P, H])
            again = a.sb("again", [P, 1], I32)
            again_stray = a.sb("again_stray", [P, 1], I32)
            factors = a.sb("factors", [P, G1 * T, 2])
            with ExitStack() as first:
                f = Mem(nc, first, "prep")
                wf = f.sb("wf", [OF, 2, D])
                attn = f.sb("attn", [OF, H])
                wgat = f.sb("wgat", [P, KD, V])
                att_b = f.sb("att", [P, 2, V])
                read_graph(nc, "graph", gr, src1, dst1, first1)
                constants(nc, "const", ident, ACC, tri, EX1)
                load(nc, "load0", [
                    (X[:, :, :], x_in), (wproj[:, :, :], w_msg), (wf[:, :, :], w_rows), (attn[:, :], attn_t),
                    (wgat[:, :, :], w_gat), (att_b[:, :, :], att.partition_broadcast(P)),
                ])
                score_columns(nc, "scols", wf, attn, wproj, wgat, att_b, wg)
            layernorm_stats(nc, "ln0", X, rstd, nmr)
            normalize_project(nc, "proj0", X, rstd, nmr, ident, wproj, 2 * MC, t_msg, 2 * MC, keep, 2, OF, None)
            attention_bound(nc, "bound", keep, attr, factors, shift, smax)
            weigh = Weigh(factors, shift, smax)
            sorted_graph(nc, "att", t_msg, 2 * MC, gr, AC, ACC, weigh)
            stray_edges(nc, "attst", t_msg, 2 * MC, gr, AC, ACC, weigh, gr.stray)
            attention_gap(nc, "gap", gr, shift, smax, gap, again, again_stray)
            zero_sums(nc, "zsums", ACC, again)
            sorted_graph(nc, "atta", t_msg, 2 * MC, gr, AC, ACC, weigh, again)
            stray_edges(nc, "attsta", t_msg, 2 * MC, gr, AC, ACC, weigh, again_stray)
            attention_finish(nc, "attfin", X, ACC, gap)

        with ExitStack() as layer:
            a = Mem(nc, layer, "l0f")
            S = a.sb("S", [P, NB, EX0])
            GT = a.sb("GT", [P, NB, EX0])
            layernorm_stats(nc, "ln1", X, rstd, nmr)
            with ExitStack() as part:
                q = Mem(nc, part, "rout")
                AGG = q.sb("AGG", [P, HB, 2, SC])
                small = [q.sb(f"small{k}", [P, V]) for k in range(3)]
                w1 = q.sb("w1", [P, EX0, KD, F0])
                w2 = q.sb("w2", [P, EX0, M0, D])
                b1 = q.sb("b1", [P, EX0, M0])
                b2 = q.sb("b2", [P, EX0, D])
                with ExitStack() as projection:
                    keep = Mem(nc, projection, "rkeep").sb("keep", [P, NB, V + 2 * H])
                    load(nc, "load1", [(small[k][:, :], v.partition_broadcast(P))
                                       for k, v in enumerate((b_gat, gamma, beta))] + [
                        (w1[:, :, :, :], e0_w1), (w2[:, :, :, :], e0_w2), (b1[:, :, :], e0_b1),
                        (b2[:, :, :], e0_b2.partition_broadcast(P))])
                    normalize_project(nc, "proj1", X, rstd, nmr, ident, wg, V + 2 * H, t_src, V + H, keep, 1, 0,
                                      t_hT)
                    routing_tables(nc, "rtab", keep, t_dst, AGG)
                routing_with_experts(nc, "rgraph", t_src, t_dst, src2, dst2, gr, AGG, t_hT, t_y, w1, b1, w2, b2)
                routing_scores(nc, "rscore", AGG, *small, S)
                gates(nc, "gate0", S, GT, EX0, tri)
            add_experts(nc, "addex", X, GT, t_y)

        with ExitStack() as layer:
            a = Mem(nc, layer, "l1g")
            ACC = a.sb("ACC", [P, NB, D])
            layernorm_stats(nc, "ln2", X, rstd, nmr)
            normalize(nc, "norm", X, rstd, nmr, ACC, t_row)
            sorted_graph(nc, "gin", t_row, D, gr, D, ACC, None)
            stray_edges(nc, "ginst", t_row, D, gr, D, ACC, None, gr.stray)
            HT = a.sb("HT", [P, KD, NB * P])
            wgin = a.sb("w", [P, KD, D])
            vec = [a.sb(f"vec{k}", [P, KD]) for k in range(3)]
            load(nc, "load3", [(wgin[:, :, :], w_gin)] + [
                (vec[k][:, :], v) for k, v in enumerate((b_gin, bn_w, bn_b))])
            batch_normalized(nc, "bn", X, ACC, HT, ident, wgin, *vec)

        with ExitStack() as layer:
            a = Mem(nc, layer, "l1f")
            HT = a.sb("HT", [P, KD, NB * P])
            GT = a.sb("GT", [P, NB, EX1])
            S = a.sb("S", [P, NB, EX1])
            layernorm_stats(nc, "ln3", X, rstd, nmr)
            transpose_normalized(nc, "turn", X, rstd, nmr, ident, HT)
            rw1 = a.sb("rw1", [P, KD, P])
            rb1 = a.sb("rb1", [P, 1])
            rw2 = a.sb("rw2", [P, EX1])
            rb2 = a.sb("rb2", [P, EX1])
            w1 = a.sb("w1", [P, EX1, KD, D])
            w2 = a.sb("w2", [P, EX1, KD, D])
            w3 = a.sb("w3", [P, EX1, KD, D])
            b1 = a.sb("b1", [P, EX1, KD])
            b2 = a.sb("b2", [P, EX1, KD])
            b3 = a.sb("b3", [P, EX1, D])
            load(nc, "load4", [
                (rw1[:, :, :], r_w1), (rb1[:, :], r_b1), (rw2[:, :], r_w2), (rb2[:, :], r_b2.partition_broadcast(P)),
                (w1[:, :, :, :], e1_w1), (w2[:, :, :, :], e1_w2), (w3[:, :, :, :], e1_w3),
                (b1[:, :, :], e1_b1), (b2[:, :, :], e1_b2), (b3[:, :, :], e1_b3.partition_broadcast(P))])
            router(nc, "router", HT, rw1, rb1, rw2, rb2, S)
            gates(nc, "gate1", S, GT, EX1, tri)
            experts(nc, "ex1", X, HT, GT, EX1, [KD, KD], [w1, w2, w3], [b1, b2], b3, [ACT.Relu] * 2, out)


def transpose_normalized(nc, prefix, X, rstd, nmr, ident, HT):
    with ExitStack() as stack:
        m = Mem(nc, stack, prefix)
        h = [m.sb(f"h{s}", [P, D]) for s in range(2)]
        psT = [m.ps(f"psT{s}", [P, KD, P]) for s in range(2)]
        h_ready = m.sem("h_ready")
        h_turned = m.sem("h_turned")
        HT_ready = m.sem("HT_ready")
        block = stack.enter_context(nc.Block())

        @block.scalar
        def _(act):
            with act.Fori(0, HB) as i:
                for s in range(2):
                    n = i * 2 + s
                    act.wait_ge(h_turned, n + 1)
                    nc.scalar.activation(h[s][:, :], X[:, at(n), :], ACT.Identity, bias=nmr[:, at(n)],
                                         scale=rstd[:, at(n)]).then_inc(h_ready, 1)

        @block.tensor
        def _(pe):
            pe.sem_inc(h_turned, 2)
            with pe.Fori(0, HB) as i:
                for s in range(2):
                    n = i * 2 + s
                    pe.wait_ge(h_ready, n + 1)
                    pe.wait_ge(HT_ready, n + 1)
                    for k in range(KD):
                        last = nc.tensor.transpose(psT[s][:, k, :], h[s][:, k * P:(k + 1) * P], ident[:, :])
                    last.then_inc(h_turned, 1)

        @block.vector
        def _(dve):
            dve.sem_inc(HT_ready, 2)
            with dve.Fori(0, HB) as i:
                for s in range(2):
                    n = i * 2 + s
                    dve.wait_ge(h_turned, n + 3)
                    nc.vector.tensor_copy(HT[:, :, at(n, P)], psT[s][:, :, :]).then_inc(HT_ready, 1)


def layouts(i, np):
    def blocks(a):
        a = np.concatenate([a, np.zeros((NB * P - N, a.shape[1]), a.dtype)])
        return a.reshape(NB, P, -1).transpose(1, 0, 2)

    def edges(a, groups, pad, extra=0):
        tail = np.repeat(a[-1:] if pad is None else np.full_like(a[-1:], pad), groups * GE - len(a), axis=0)
        a = np.concatenate([a, tail]).reshape((groups, P, T) + a.shape[1:])
        a = np.moveaxis(a, 0, 1).reshape((P, -1))
        return np.concatenate([a, np.zeros((P, extra * T), a.dtype)], axis=1)

    def slices(a):
        a = a.reshape(a.shape[:-2] + (-1, P, a.shape[-1]))
        return np.moveaxis(a, -2, 0)

    def cols(a):
        return np.moveaxis(a.reshape(a.shape[:-1] + (-1, P)), -1, 0)

    src, dst = i["src"], i["dst"]
    wf, wr = i["L0_gnn_W_forward"], i["L0_gnn_W_reverse"]
    gap = np.zeros((D, H), wf.dtype)
    ei = i["L0_ffn_edge_index"]
    firsts = np.concatenate([dst, dst[-1:].repeat(G1 * GE - E1)])[::GE]
    return {
        "x_in": blocks(i["x"]), "src1": edges(src, G1, None, 2), "dst1": edges(dst, G1, -1),
        "first1": firsts, "attr": edges(i["edge_attr_2"], G1, None),
        "w_msg": slices(np.concatenate([wf.T, gap, wr.T, gap], axis=1)),
        "w_rows": np.stack([wf, wr]).transpose(1, 0, 2), "attn_t": i["L0_gnn_attn_forward"][0].T,
        "w_gat": slices(i["L0_ffn_W_gat"]),
        "att": np.stack([i["L0_ffn_att_src"].reshape(-1), i["L0_ffn_att_dst"].reshape(-1)]),
        "b_gat": i["L0_ffn_b_gat"], "gamma": i["L0_ffn_ln_gamma"], "beta": i["L0_ffn_ln_beta"],
        "e0_w1": slices(i["L0_ffn_W1"]), "e0_b1": cols(i["L0_ffn_b1"]),
        "e0_w2": slices(i["L0_ffn_W2"]), "e0_b2": i["L0_ffn_b2"],
        "src2": edges(ei[0], G2, None, 2), "dst2": edges(ei[1], G2, -1, 2),
        "w_gin": slices(i["L1_gnn_W"].T), "b_gin": cols(i["L1_gnn_b"]),
        "bn_w": cols(i["L1_gnn_bn_w"]), "bn_b": cols(i["L1_gnn_bn_b"]),
        "r_w1": slices(i["L1_ffn_router_w1"]), "r_b1": cols(i["L1_ffn_router_b1"]),
        "r_w2": i["L1_ffn_router_w2"], "r_b2": i["L1_ffn_router_b2"],
        "e1_w1": slices(i["L1_ffn_expert_w1"]), "e1_b1": cols(i["L1_ffn_expert_b1"]),
        "e1_w2": slices(i["L1_ffn_expert_w2"]), "e1_b2": cols(i["L1_ffn_expert_b2"]),
        "e1_w3": slices(i["L1_ffn_expert_w3"]), "e1_b3": i["L1_ffn_expert_b3"],
    }


def kernel(**inputs):
    import numpy as np
    import concourse.bacc as bacc
    from concourse.bass_utils import run_bass_kernel_spmd

    nc = bacc.Bacc("TRN2", target_bir_lowering=False, num_devices=1)
    arrays = {k: np.ascontiguousarray(v) for k, v in
              layouts({k: np.asarray(v) for k, v in inputs.items()}, np).items()}
    args = {k: nc.dram_tensor(k, v.shape, mybir.dt.from_np(v.dtype), kind="ExternalInput").ap()
            for k, v in arrays.items()}
    out = nc.dram_tensor("out", (N, D), F32, kind="ExternalOutput").ap()
    gnn_ffn(nc, out=out, **args)
    return run_bass_kernel_spmd(nc, [arrays], core_ids=[0]).results[0]["out"]
```

```python
import collections

import concourse.bass as bass
from concourse import mybir
from contextlib import ExitStack

F32 = mybir.dt.float32
I32 = mybir.dt.int32
F32R = mybir.dt.float32r
ALU = mybir.AluOpType
ACT = mybir.ActivationFunctionType
AX = mybir.AxisListType
RED = bass.bass_isa.ReduceOp

P = 128
N = 6250
D = 256
KD = D // P
NB = 50
VB = N // P
VR = N - VB * P
T = 8
GE = P * T
E1 = 106250
G1 = 104
E2 = 131072
G2 = E2 // GE
H = 4
OF = 64
MC = OF + H
AC = H * OF + H
W = 2 * P
EX0 = 4
HB = NB // 2
SC = EX0 * H + H
F0 = 512
M0 = F0 // P
EX1 = 6
LN_EPS = 1e-5
NEG = -3.0e38
PASSES = ((0, 0), (0, 1), (1, 0))
FAR = 40.0


class Steps:

    def __init__(self, eng, sem, base=0):
        self.eng, self.sem, self.base, self.n = eng, sem, base, 0

    def __call__(self, ins):
        self.mark(ins)
        self.done()

    def done(self):
        self.eng.wait_ge(self.sem, self.base + self.n)

    def mark(self, ins):
        ins.then_inc(self.sem, 1)
        self.n += 1


def at(i, k=1):
    return bass.ds(i * k, k)


class Mem:

    order = {}

    def __init__(self, nc, stack, prefix):
        self.nc, self.stack, self.prefix = nc, stack, prefix
        self.sems, self.nums = [], []
        self.waiting = Mem.order.setdefault(id(nc), collections.deque(nc.free_semaphores))
        stack.callback(self.free_sems)

    def free_sems(self):
        if self.sems:
            self.nc.clear_and_free_semaphores(self.sems)
            self.waiting.extend(self.nums)

    def sb(self, name, shape, dt=F32):
        return self.stack.enter_context(self.nc.sbuf_tensor(f"{self.prefix}_{name}", shape, dt))

    def ps(self, name, shape):
        return self.stack.enter_context(self.nc.psum_tensor(f"{self.prefix}_{name}", shape, F32))

    def sem(self, name):
        self.nums.append(self.waiting.popleft())
        self.sems.append(self.nc.alloc_semaphore(f"{self.prefix}_{name}", self.nums[-1]))
        return self.sems[-1]


def layernorm_stats(nc, prefix, X, rstd, nmr, loads=(), splits=()):
    with ExitStack() as stack:
        m = Mem(nc, stack, prefix)
        st = m.sb("st", [P, NB, 6])
        t0 = m.sb("t0", [P, NB])
        t1 = m.sb("t1", [P, NB])
        stats_in = m.sem("stats_in")
        step = m.sem("step")
        var_ready = m.sem("var_ready")
        std_ready = m.sem("std_ready")
        loaded = m.sem("loaded")
        high_ready = m.sem("high_ready")
        block = stack.enter_context(nc.Block())

        @block.sync
        def _(sp):
            for to, of in loads:
                sp.dma_start(to, of).then_inc(loaded, 16)
            if loads:
                sp.wait_ge(loaded, 16 * len(loads))

        @block.vector
        def _(dve):
            EACH = 10
            with dve.Fori(0, NB // EACH) as i:
                for k in range(EACH):
                    n = i * EACH + k
                    last = nc.vector.bn_stats(st[:, at(n), :], X[:, at(n), :])
                last.then_inc(stats_in, 1)
            dve.wait_ge(stats_in, NB // EACH)
            link = Steps(dve, step)
            link(nc.vector.tensor_tensor(t0[:, :], st[:, :, 1], st[:, :, 4], ALU.subtract))
            link(nc.vector.tensor_tensor(t0[:, :], t0[:, :], t0[:, :], ALU.mult))
            link(nc.vector.tensor_tensor(t1[:, :], st[:, :, 2], st[:, :, 5], ALU.add))
            link(nc.vector.scalar_tensor_tensor(t0[:, :], t0[:, :], D / 4.0, t1[:, :], ALU.mult, ALU.add))
            nc.vector.tensor_scalar(t0[:, :], t0[:, :], 1.0 / D, LN_EPS, ALU.mult, ALU.add).then_inc(var_ready, 1)
            dve.wait_ge(std_ready, 1)
            link(nc.vector.reciprocal(rstd[:, :], t1[:, :]))
            link(nc.vector.tensor_tensor(t0[:, :], st[:, :, 1], st[:, :, 4], ALU.add))
            link(nc.vector.scalar_tensor_tensor(nmr[:, :], t0[:, :], -0.5, rstd[:, :], ALU.mult, ALU.mult))
            for n, (whole, high, low) in enumerate(splits):
                dve.wait_ge(high_ready, n + 1)
                nc.vector.tensor_tensor(low, whole, high, ALU.subtract)

        @block.scalar
        def _(act):
            act.wait_ge(var_ready, 1)
            nc.scalar.activation(t1[:, :], t0[:, :], ACT.Sqrt).then_inc(std_ready, 1)
            if splits:
                act.wait_ge(loaded, 16 * len(loads))
            for whole, high, _ in splits:
                nc.scalar.activation(high, whole, ACT.Copy).then_inc(high_ready, 1)


def normalize_project(nc, prefix, X, rstd, nmr, ident, wproj, out, tcol, table, t_hT, plus=None):
    with ExitStack() as stack:
        m = Mem(nc, stack, prefix)
        ncol = wproj.shape[-1]
        h = [m.sb(f"h{s}", [P, D]) for s in range(4)]
        hT = [m.sb(f"hT{s}", [P, KD, W]) for s in range(4)]
        psT = [m.ps(f"psT{s}", [P, KD, P]) for s in range(4)]
        psO = [m.ps(f"psO{s}", [P, ncol]) for s in range(4)]
        h_ready = m.sem("h_ready")
        h_turned = m.sem("h_turned")
        hT_ready = m.sem("hT_ready")
        projected = m.sem("projected")
        out_ready = m.sem("out_ready")
        hT_stored = [m.sem(f"hT_stored{s}") for s in range(4)]
        stored = m.sem("stored")
        block = stack.enter_context(nc.Block())
        Q = 8

        def blocks(eng, body):
            for k in range(Q):
                body(k, k)
            with eng.Fori(1, NB // Q) as i:
                for k in range(Q):
                    body(i * Q + k, k)
            for n in range(NB - NB % Q, NB):
                body(n, n % Q)

        @block.scalar
        def _(act):
            def rows(n, k):
                wait(act, h_turned, n - 3)
                nc.scalar.activation(h[k % 4][:, :], X[:, at(n), :], ACT.Identity, bias=nmr[:, at(n)],
                                     scale=rstd[:, at(n)]).then_inc(h_ready, 1)

            blocks(act, rows)

        @block.tensor
        def _(pe):
            def product(n, k):
                pe.wait_ge(hT_ready, n + 1)
                wait(pe, out_ready, n - 3)
                for j in range(KD):
                    last = nc.tensor.matmul(psO[k % 4][:, :], hT[k // 2][:, j, (k % 2) * P:(k % 2 + 1) * P],
                                            wproj[:, j, :], start=(j == 0), stop=(j == KD - 1))
                last.then_inc(projected, 1)

            def turn(n, k):
                pe.wait_ge(h_ready, n + 1)
                wait(pe, hT_ready, n - 3)
                for j in range(KD):
                    last = nc.tensor.transpose(psT[k % 4][:, j, :], h[k % 4][:, j * P:(j + 1) * P], ident[:, :])
                last.then_inc(h_turned, 1)
                if not (isinstance(n, int) and n < 1):
                    product(n - 1, (k - 1) % Q)

            blocks(pe, turn)
            product(NB - 1, (NB - 1) % Q)

        @block.vector
        def _(dve):
            def take(n, k):
                dve.wait_ge(projected, n + 1)
                if plus is not None:
                    to, b = plus
                    nc.vector.tensor_tensor(to[:, at(n), :], psO[k % 4][:, :].unsqueeze(1),
                                            b[:, :].unsqueeze(1), ALU.add)
                nc.vector.tensor_copy(out[:, at(n), :], psO[k % 4][:, :].unsqueeze(1)).then_inc(out_ready, 1)

            def turned(n, k):
                dve.wait_ge(h_turned, n + 1)
                wait(dve, projected, n - 7)
                if t_hT is not None and not (isinstance(n, int) and n < Q):
                    dve.wait_ge(hT_stored[k // 2], (n - k) * (16 // Q))
                nc.vector.tensor_copy(hT[k // 2][:, :, (k % 2) * P:(k % 2 + 1) * P],
                                      psT[k % 4][:, :, :]).then_inc(hT_ready, 1)
                if not (isinstance(n, int) and n < 1):
                    take(n - 1, (k - 1) % Q)

            blocks(dve, turned)
            take(NB - 1, (NB - 1) % Q)

        @block.sync
        def _(sp):
            def rows(n, k):
                sp.wait_ge(out_ready, n + 1)
                sp.dma_start(table[bass.ds((n - 1) * P, W), :].rearrange("(b p) c -> p b c", p=P),
                             out[:, bass.ds(n - 1, 2), 0:tcol]).then_inc(stored, 16)

            def store(n, k):
                if k % 2 == 0:
                    return
                if t_hT is not None:
                    sp.wait_ge(hT_ready, n + 1)
                    pair = n // 2 if isinstance(n, int) else (n - k) // 2 + k // 2
                    sp.dma_start(t_hT[at(pair), :, :].rearrange("a p (k c) -> (a p) k c", k=KD),
                                 hT[k // 2][:, :, :]).then_inc(hT_stored[k // 2], 16)
                rows(n, k)

            blocks(sp, store)
            sp.wait_ge(stored, 16 * HB)
            if t_hT is not None:
                for s in range(4):
                    sp.wait_ge(hT_stored[s], 16 * ((HB + 3 - s) // 4))


def gates(nc, prefix, S, GT, ex, tri):
    with ExitStack() as stack:
        m = Mem(nc, stack, prefix)
        cmp = m.sb("cmp", [P, NB, ex, ex])
        eq = m.sb("eq", [P, NB, ex, ex])
        rank = m.sb("rank", [P, NB, ex])
        top = m.sb("top", [P, NB])
        d = m.sb("d", [P, NB, ex])
        step = m.sem("step")
        d_ready = m.sem("d_ready")
        exp_ready = m.sem("exp_ready")
        block = stack.enter_context(nc.Block())
        wide = [P, NB, ex, ex]

        @block.vector
        def _(dve):
            link = Steps(dve, step)
            other = S[:, :, :].unsqueeze(2).to_broadcast(wide)
            own = S[:, :, :].unsqueeze(3).to_broadcast(wide)
            link(nc.vector.tensor_reduce(top[:, :], S[:, :, :], AX.X, ALU.max))
            nc.vector.tensor_tensor(d[:, :, :], S[:, :, :], top[:, :].unsqueeze(2).to_broadcast([P, NB, ex]),
                                    ALU.subtract).then_inc(d_ready, 1)
            link(nc.vector.tensor_tensor(cmp[:, :, :, :], other, own, ALU.is_gt))
            link(nc.vector.tensor_tensor(eq[:, :, :, :], other, own, ALU.is_equal))
            link(nc.vector.tensor_tensor(eq[:, :, :, :], eq[:, :, :, :],
                                         tri[:, 0:ex, 0:ex].unsqueeze(1).to_broadcast(wide), ALU.mult))
            link(nc.vector.tensor_tensor(cmp[:, :, :, :], cmp[:, :, :, :], eq[:, :, :, :], ALU.add))
            link(nc.vector.tensor_reduce(rank[:, :, :], cmp[:, :, :, :], AX.X, ALU.add))
            dve.wait_ge(exp_ready, 1)
            link(nc.vector.scalar_tensor_tensor(GT[:, :, :], rank[:, :, :], 1.5, d[:, :, :], ALU.is_lt, ALU.mult))
            link(nc.vector.tensor_reduce(top[:, :], GT[:, :, :], AX.X, ALU.add))
            link(nc.vector.reciprocal(top[:, :], top[:, :]))
            link(nc.vector.tensor_tensor(GT[:, :, :], GT[:, :, :],
                                         top[:, :].unsqueeze(2).to_broadcast([P, NB, ex]), ALU.mult))

        @block.scalar
        def _(act):
            act.wait_ge(d_ready, 1)
            nc.scalar.activation(d[:, :, :], d[:, :, :], ACT.Exp).then_inc(exp_ready, 1)


def wait(eng, sem, n):
    if not (isinstance(n, int) and n <= 0):
        eng.wait_ge(sem, n)


def when(eng, flag, body):
    if flag is None:
        body()
    else:
        set_ = eng.value_load(flag[0:1, 0:1], min_val=0, max_val=1)
        with eng.If(set_ > 0):
            body()


def pairs(eng, count, body):
    for s in range(2):
        body(s, s)
    with eng.Fori(1, count // 2) as i:
        for s in range(2):
            body(i * 2 + s, s)


class Graph:

    def __init__(self, m):
        self.src = m.sb("src", [P, (G1 + 2) * T], I32)
        self.rel = m.sb("rel", [P, G1 * T])
        self.first = m.sb("first", [P, G1])
        self.base = m.sb("base", [P, G1], I32)
        self.off = m.sb("off", [P, G1])
        self.stray = m.sb("stray", [P, 1], I32)
        self.iota = m.sb("iota", [P, W])
        self.diff = m.sb("diff", [P, W])


def prepare(nc, prefix, gr, src_in, dst_in, first_in, ident, ACC, tri, ex, loads):
    with ExitStack() as stack:
        m = Mem(nc, stack, prefix)
        dst = m.sb("dst", [P, G1 * T], I32)
        first = m.sb("first", [P, G1], I32)
        basef = m.sb("basef", [P, G1])
        iotai = m.sb("iotai", [P, W], I32)
        diffi = m.sb("diffi", [P, W], I32)
        out0 = m.sb("out0", [P, G1 * T])
        out1 = m.sb("out1", [P, G1 * T])
        some = m.sb("some", [P, 1])
        any_ = m.sb("any", [P, 1])
        loaded = m.sem("loaded")
        iota_done = m.sem("iota_done")
        step = m.sem("step")
        some_ready = m.sem("some_ready")
        any_ready = m.sem("any_ready")
        inputs_in = m.sem("inputs_in")
        zeroed = m.sem("zeroed")
        ident_done = m.sem("ident_done")
        tri_zeroed = m.sem("tri_zeroed")
        block = stack.enter_context(nc.Block())

        @block.sync
        def _(sp):
            sp.dma_start(dst[:, :], dst_in).then_inc(loaded, 16)
            sp.dma_start(first[:, :], first_in.partition_broadcast(P)).then_inc(loaded, 16)
            sp.dma_start(gr.src[:, :], src_in).then_inc(loaded, 16)
            for to, of in loads:
                sp.dma_start(to, of).then_inc(inputs_in, 16)
            sp.wait_ge(inputs_in, 16 * len(loads))

        @block.gpsimd
        def _(pool):
            nc.gpsimd.iota(iotai[:, :], pattern=[[1, W]], base=0, channel_multiplier=0).then_inc(iota_done, 1)
            nc.gpsimd.iota(diffi[:, :], pattern=[[1, W]], base=0, channel_multiplier=-1).then_inc(iota_done, 1)
            nc.gpsimd.memset(ident[:, :], 0.0).then_inc(zeroed, 1)
            pool.wait_ge(zeroed, 1)
            nc.gpsimd.affine_select(out=ident[:, :], in_=ident[:, :], compare_op=ALU.not_equal, fill=1.0,
                                    base=0, pattern=[[-1, P]], channel_multiplier=1).then_inc(ident_done, 1)
            pool.wait_ge(some_ready, 1)
            nc.gpsimd.partition_all_reduce(any_[:, :], some[:, :], P, RED.max).then_inc(any_ready, 1)

        @block.vector
        def _(dve):
            dve.wait_ge(loaded, 48)
            dve.wait_ge(iota_done, 2)
            link = Steps(dve, step)
            link.mark(nc.vector.tensor_copy(gr.iota[:, :], iotai[:, :]))
            link.mark(nc.vector.tensor_copy(gr.diff[:, :], diffi[:, :]))
            link.mark(nc.vector.tensor_copy(gr.first[:, :], first[:, :]))
            link(nc.vector.tensor_single_scalar(gr.base[:, :], first[:, :], 7, ALU.arith_shift_right))
            link(nc.vector.tensor_scalar(gr.base[:, :], gr.base[:, :], VB, 0, ALU.min, ALU.max))
            link(nc.vector.tensor_scalar(basef[:, :], gr.base[:, :], float(P), None, ALU.mult))
            link(nc.vector.tensor_tensor(gr.off[:, :], gr.first[:, :], basef[:, :], ALU.subtract))
            link(nc.vector.tensor_tensor(gr.rel[:, :].rearrange("p (g t) -> p g t", t=T),
                                         dst[:, :].rearrange("p (g t) -> p g t", t=T),
                                         gr.first[:, :].unsqueeze(2).to_broadcast([P, G1, T]), ALU.subtract))
            link(nc.vector.tensor_scalar(out0[:, :], gr.rel[:, :], 0.0, None, ALU.is_lt))
            link(nc.vector.scalar_tensor_tensor(out1[:, :], gr.rel[:, :], float(P), out0[:, :], ALU.is_ge, ALU.add))
            link(nc.vector.scalar_tensor_tensor(out0[:, :], dst[:, :], 0.0, out1[:, :], ALU.is_ge, ALU.mult))
            nc.vector.tensor_reduce(some[:, :], out0[:, :], AX.X, ALU.max).then_inc(some_ready, 1)
            dve.wait_ge(any_ready, 1)
            link(nc.vector.tensor_copy(gr.stray[:, :], any_[:, :]))
            nc.vector.memset(ACC[:, :, :], 0.0)
            nc.vector.memset(tri[:, :, :], 0.0).then_inc(tri_zeroed, 1)
            dve.wait_ge(tri_zeroed, 1)
            for i in range(1, ex):
                nc.vector.memset(tri[:, i, 0:i], 1.0)


class Weigh:

    def __init__(self, attr, shift, smax):
        self.attr, self.shift, self.smax = attr, shift, smax


def sorted_graph(nc, prefix, table, row, gr, C, ACC, weigh, flag=None):
    with ExitStack() as stack:
        m = Mem(nc, stack, prefix)
        stage = [m.sb(f"stage{s}", [P, T], I32) for s in range(2)]
        rows = [m.sb(f"rows{s}", [P, T, row]) for s in range(2)]
        hot = [m.sb(f"hot{s}", [P, T, P]) for s in range(2)]
        move = [m.sb(f"move{s}", [P, W]) for s in range(2)]
        wsum = [m.sb(f"wsum{s}", [P, C]) for s in range(2)]
        psW = [m.ps(f"psW{s}", [P, 512]) for s in range(2)]
        psB = [m.ps(f"psB{s}", [P, 2, 512]) for s in range(2)]
        if weigh:
            val = [m.sb(f"val{s}", [P, T, C]) for s in range(2)]
            prod = m.sb("prod", [P, T, 2, MC])
            msg = m.sb("msg", [P, T, MC])
            sco = m.sb("sco", [P, T, H])
        else:
            val = rows
        step = m.sem("step")
        src_staged = m.sem("src_staged")
        gathering = m.sem("gathering")
        landed = [m.sem(f"landed{s}") for s in range(2)]
        rows_used = m.sem("rows_used")
        hot_ready = m.sem("hot_ready")
        move_ready = m.sem("move_ready")
        scores_ready = m.sem("scores_ready")
        weights_ready = m.sem("weights_ready")
        val_ready = m.sem("val_ready")
        summed = m.sem("summed")
        wsum_ready = m.sem("wsum_ready")
        moved = m.sem("moved")
        added = m.sem("added")
        block = stack.enter_context(nc.Block())

        @block.gpsimd
        def _(pool):
            def gather(n, s):
                pool.wait_ge(src_staged, n + 1)
                wait(pool, rows_used if weigh else summed, n - 1)
                pool.sem_inc(gathering, 1)
                for t in range(T):
                    pool.indirect_dma_start(
                        out=rows[s][:, t, :], out_offset=None, in_=table,
                        in_offset=bass.IndirectOffsetOnAxis(ap=stage[s][:, t:t + 1], axis=0),
                    ).then_inc(landed[s], 16)

            when(pool, flag, lambda: pairs(pool, G1, gather))

        @block.vector
        def _(dve):
            def put(n, s):
                nc.vector.tensor_scalar(stage[s][:, :], gr.src[:, at(n, T)], N - 1, 0,
                                        ALU.min, ALU.max).then_inc(src_staged, 1)

            def add_sums(n, s):
                b = dve.value_load(gr.base[0:1, at(n)], min_val=0, max_val=VB)
                dve.wait_ge(moved, n + 1)
                wait(dve, added, n)
                nc.vector.tensor_tensor(ACC[:, bass.ds(b, 2), :], ACC[:, bass.ds(b, 2), :],
                                        psB[s][:, :, 0:C], ALU.add).then_inc(added, 1)

            STEPS = 3 if weigh else 0

            def group(n, s):
                link = Steps(dve, step, n * STEPS)

                def mark_places():
                    wait(dve, summed, n - 1)
                    nc.vector.tensor_tensor(hot[s][:, :, :], gr.iota[:, 0:P].unsqueeze(1).to_broadcast([P, T, P]),
                                            gr.rel[:, at(n, T)].unsqueeze(2).to_broadcast([P, T, P]),
                                            ALU.is_equal).then_inc(hot_ready, 1)

                if not weigh:
                    mark_places()
                dve.wait_ge(landed[s], (n - s) * (8 * T) + 16 * T)
                put(n + 2, s)
                if weigh:
                    nc.vector.tensor_tensor(prod[:, :, :, :],
                                            rows[s][:, :, :].rearrange("p t (a c) -> p t a c", a=2),
                                            weigh.attr[:, at(n, T), :].unsqueeze(3).to_broadcast([P, T, 2, MC]),
                                            ALU.mult).then_inc(rows_used, 1)
                    mark_places()
                    dve.wait_ge(rows_used, n + 1)
                    wait(dve, val_ready, n)
                    link(nc.vector.tensor_tensor(msg[:, :, :], prod[:, :, 0, :], prod[:, :, 1, :], ALU.add))
                    nsc = msg[:, :, OF:MC]
                    link.mark(nc.vector.tensor_tensor(weigh.smax[:, :, :], weigh.smax[:, :, :], nsc, ALU.max))
                    link(nc.vector.scalar_tensor_tensor(sco[:, :, :], nsc, 0.2, nsc, ALU.mult, ALU.max))
                    assert link.n == STEPS
                    nc.vector.tensor_tensor(sco[:, :, :], sco[:, :, :],
                                            weigh.shift[:, :].unsqueeze(1).to_broadcast([P, T, H]),
                                            ALU.subtract).then_inc(scores_ready, 1)
                    dve.wait_ge(weights_ready, n + 1)
                    for hd in range(H):
                        last = nc.vector.tensor_tensor(
                            val[s][:, :, hd * OF:(hd + 1) * OF], msg[:, :, 0:OF],
                            val[s][:, :, H * OF + hd:H * OF + hd + 1].to_broadcast([P, T, OF]), ALU.mult)
                    last.then_inc(val_ready, 1)
                wait(dve, moved, n - 1)
                nc.vector.tensor_scalar(move[s][:, :], gr.diff[:, :], gr.off[:, at(n)], None,
                                        ALU.is_equal).then_inc(move_ready, 1)
                if not (isinstance(n, int) and n < 2):
                    add_sums(n - 2, s)

            def body():
                for s in range(2):
                    put(s, s)
                pairs(dve, G1, group)
                for n in (G1 - 2, G1 - 1):
                    add_sums(n, n % 2)

            when(dve, flag, body)

        @block.scalar
        def _(act):
            def take_window(n, s):
                act.wait_ge(summed, n + 1)
                wait(act, moved, n - 1)
                nc.scalar.activation(wsum[s][:, :], psW[s][:, 0:C], ACT.Copy).then_inc(wsum_ready, 1)

            def group(n, s):
                if weigh:
                    act.wait_ge(scores_ready, n + 1)
                    wait(act, summed, n - 1)
                    nc.scalar.activation(val[s][:, :, H * OF:C], sco[:, :, :], ACT.Exp).then_inc(weights_ready, 1)
                if not (isinstance(n, int) and n < 1):
                    take_window(n - 1, 1 - s)

            def body():
                pairs(act, G1, group)
                take_window(G1 - 1, 1)

            when(act, flag, body)

        @block.tensor
        def _(pe):
            def onto_blocks(n, s):
                pe.wait_ge(wsum_ready, n + 1)
                pe.wait_ge(move_ready, n + 1)
                wait(pe, added, n - 1)
                for half in range(2):
                    last = nc.tensor.matmul(psB[s][:, half, 0:C], move[s][:, half * P:(half + 1) * P], wsum[s][:, :],
                                            start=True, stop=True)
                last.then_inc(moved, 1)

            def group(n, s):
                pe.wait_ge(hot_ready, n + 1)
                if weigh:
                    pe.wait_ge(val_ready, n + 1)
                else:
                    pe.wait_ge(landed[s], (n - s) * (8 * T) + 16 * T)
                wait(pe, wsum_ready, n - 1)
                for t in range(T):
                    last = nc.tensor.matmul(psW[s][:, 0:C], hot[s][:, t, :], val[s][:, t, :],
                                            start=(t == 0), stop=(t == T - 1))
                last.then_inc(summed, 1)
                if not (isinstance(n, int) and n < 1):
                    onto_blocks(n - 1, 1 - s)

            def body():
                pairs(pe, G1, group)
                onto_blocks(G1 - 1, 1)

            when(pe, flag, body)


def stray_edges(nc, prefix, table, row, gr, C, ACC, weigh, flag):
    with ExitStack() as stack:
        m = Mem(nc, stack, prefix)
        stage = m.sb("stage", [P, T], I32)
        rows = m.sb("rows", [P, T, row])
        hot = m.sb("hot", [P, T, W])
        d = m.sb("d", [P, T])
        inside = m.sb("inside", [P, T])
        node = m.sb("node", [P, T])
        psB = m.ps("psB", [P, 2, 512])
        if weigh:
            val = m.sb("val", [P, T, C])
            prod = m.sb("prod", [P, T, 2, MC])
            msg = m.sb("msg", [P, T, MC])
            sco = m.sb("sco", [P, T, H])
        else:
            val = rows
        step = m.sem("step")
        staged = m.sem("staged")
        gathering = m.sem("gathering")
        landed = m.sem("landed")
        scores_ready = m.sem("scores_ready")
        weights_ready = m.sem("weights_ready")
        hot_ready = m.sem("hot_ready")
        summed = m.sem("summed")
        rows_seen = m.sem("rows_seen")
        block = stack.enter_context(nc.Block())
        STEPS = 5 + (3 + H if weigh else 0) + HB * 2

        @block.gpsimd
        def _(pool):
            def body():
                with pool.Fori(0, G1) as g:
                    pool.wait_ge(staged, g + 1)
                    pool.sem_inc(gathering, 1)
                    for t in range(T):
                        pool.indirect_dma_start(
                            out=rows[:, t, :], out_offset=None, in_=table,
                            in_offset=bass.IndirectOffsetOnAxis(ap=stage[:, t:t + 1], axis=0),
                        ).then_inc(landed, 16)

            when(pool, flag, body)

        @block.vector
        def _(dve):
            def body():
                with dve.Fori(0, G1) as g:
                    nc.vector.tensor_scalar(stage[:, :], gr.src[:, at(g, T)], N - 1, 0,
                                            ALU.min, ALU.max).then_inc(staged, 1)
                    link = Steps(dve, step, g * STEPS)
                    rel = gr.rel[:, at(g, T)]
                    link(nc.vector.tensor_scalar(d[:, :], rel, gr.first[:, at(g)], None, ALU.add))
                    link(nc.vector.tensor_scalar(inside[:, :], rel, float(P), None, ALU.is_lt))
                    link(nc.vector.scalar_tensor_tensor(inside[:, :], rel, 0.0, inside[:, :], ALU.is_ge, ALU.mult))
                    link(nc.vector.scalar_tensor_tensor(inside[:, :], d[:, :], 1.0, inside[:, :], ALU.add, ALU.mult))
                    link.mark(nc.vector.tensor_tensor(node[:, :], d[:, :], inside[:, :], ALU.subtract))
                    if weigh:
                        dve.wait_ge(landed, g * (16 * T) + 16 * T)
                        link(nc.vector.tensor_tensor(prod[:, :, :, :],
                                                     rows[:, :, :].rearrange("p t (a c) -> p t a c", a=2),
                                                     weigh.attr[:, at(g, T), :].unsqueeze(3).to_broadcast([P, T, 2, MC]),
                                                     ALU.mult))
                        link(nc.vector.tensor_tensor(msg[:, :, :], prod[:, :, 0, :], prod[:, :, 1, :], ALU.add))
                        nsc = msg[:, :, OF:MC]
                        link(nc.vector.scalar_tensor_tensor(sco[:, :, :], nsc, 0.2, nsc, ALU.mult, ALU.max))
                        nc.vector.tensor_tensor(sco[:, :, :], sco[:, :, :],
                                                weigh.shift[:, :].unsqueeze(1).to_broadcast([P, T, H]),
                                                ALU.subtract).then_inc(scores_ready, 1)
                        dve.wait_ge(weights_ready, g + 1)
                        for hd in range(H):
                            link.mark(nc.vector.tensor_tensor(
                                val[:, :, hd * OF:(hd + 1) * OF], msg[:, :, 0:OF],
                                val[:, :, H * OF + hd:H * OF + hd + 1].to_broadcast([P, T, OF]), ALU.mult))
                    fixed = link.n
                    with dve.Fori(0, HB) as b:
                        link = Steps(dve, step, g * STEPS + b * 2 + fixed)
                        dve.wait_ge(step, link.base)
                        nc.vector.tensor_tensor(hot[:, :, :], gr.iota[:, :].unsqueeze(1).to_broadcast([P, T, W]),
                                                node[:, :].unsqueeze(2).to_broadcast([P, T, W]),
                                                ALU.is_equal).then_inc(hot_ready, 1)
                        dve.wait_ge(hot_ready, g * HB + b + 1)
                        link.mark(nc.vector.tensor_scalar(node[:, :], node[:, :], float(-W), None, ALU.add))
                        dve.wait_ge(summed, g * HB + b + 1)
                        link.mark(nc.vector.tensor_tensor(ACC[:, at(b, 2), :], ACC[:, at(b, 2), :],
                                                          psB[:, :, 0:C], ALU.add))

            when(dve, flag, body)

        if weigh:
            @block.scalar
            def _(act):
                def body():
                    with act.Fori(0, G1) as g:
                        act.wait_ge(scores_ready, g + 1)
                        nc.scalar.activation(val[:, :, H * OF:C], sco[:, :, :], ACT.Exp).then_inc(weights_ready, 1)

                when(act, flag, body)

        @block.tensor
        def _(pe):
            def body():
                with pe.Fori(0, G1) as g:
                    if not weigh:
                        pe.wait_ge(landed, g * (16 * T) + 16 * T)
                        pe.sem_inc(rows_seen, 1)
                    with pe.Fori(0, HB) as b:
                        pe.wait_ge(hot_ready, g * HB + b + 1)
                        for half in range(2):
                            for t in range(T):
                                last = nc.tensor.matmul(psB[:, half, 0:C], hot[:, t, half * P:(half + 1) * P],
                                                        val[:, t, :], start=(t == 0), stop=(t == T - 1))
                        last.then_inc(summed, 1)

            when(pe, flag, body)


def attention_bound(nc, prefix, msgs, attr_in, attr, shift, smax):
    with ExitStack() as stack:
        m = Mem(nc, stack, prefix)
        big = m.sb("big", [P, 2 * H + 2])
        all_big = m.sb("all_big", [P, 2 * H + 2])
        t0 = m.sb("t0", [P, 2, H])
        loaded = m.sem("loaded")
        step = m.sem("step")
        big_ready = m.sem("big_ready")
        all_ready = m.sem("all_ready")
        block = stack.enter_context(nc.Block())

        @block.sync
        def _(sp):
            sp.dma_start(attr[:, :, :], attr_in.rearrange("p (e c) -> p e c", c=2)).then_inc(loaded, 16)

        @block.vector
        def _(dve):
            link = Steps(dve, step)
            link(nc.vector.memset(smax[:, :, :], NEG))
            for a in range(2):
                nc.vector.tensor_reduce(big[:, a * H:(a + 1) * H],
                                        msgs[:, :, a * MC + OF:(a + 1) * MC].rearrange("p n c -> p c n"), AX.X,
                                        ALU.max, apply_absolute_value=True).then_inc(big_ready, 1)
            dve.wait_ge(loaded, 16)
            nc.vector.tensor_reduce(big[:, 2 * H:], attr[:, :, :].rearrange("p e c -> p c e"), AX.X, ALU.max,
                                    apply_absolute_value=True).then_inc(big_ready, 1)
            dve.wait_ge(all_ready, 1)
            link(nc.vector.tensor_tensor(t0[:, :, :], all_big[:, 0:2 * H].rearrange("p (a h) -> p a h", a=2),
                                         all_big[:, 2 * H:].unsqueeze(2).to_broadcast([P, 2, H]), ALU.mult))
            link(nc.vector.tensor_tensor(shift[:, :], t0[:, 0, :], t0[:, 1, :], ALU.add))

        @block.gpsimd
        def _(pool):
            pool.wait_ge(big_ready, 3)
            nc.gpsimd.partition_all_reduce(all_big[:, :], big[:, :], P, RED.max).then_inc(all_ready, 1)


def attention_gap(nc, prefix, gr, shift, smax, gap, again, again_stray):
    with ExitStack() as stack:
        m = Mem(nc, stack, prefix)
        top = m.sb("top", [P, H])
        all_top = m.sb("all_top", [P, H])
        far = m.sb("far", [P, H])
        most = m.sb("most", [P, 1])
        step = m.sem("step")
        top_ready = m.sem("top_ready")
        all_ready = m.sem("all_ready")
        block = stack.enter_context(nc.Block())

        @block.vector
        def _(dve):
            link = Steps(dve, step)
            nc.vector.tensor_reduce(top[:, :], smax[:, :, :].rearrange("p t h -> p h t"), AX.X,
                                    ALU.max).then_inc(top_ready, 1)
            dve.wait_ge(all_ready, 1)
            link(nc.vector.scalar_tensor_tensor(top[:, :], all_top[:, :], 0.2, all_top[:, :], ALU.mult, ALU.max))
            link(nc.vector.tensor_tensor(gap[:, :], top[:, :], shift[:, :], ALU.subtract))
            link(nc.vector.tensor_scalar(far[:, :], gap[:, :], -FAR, None, ALU.is_lt))
            link(nc.vector.tensor_reduce(most[:, :], far[:, :], AX.X, ALU.max))
            link(nc.vector.tensor_copy(again[:, :], most[:, :]))
            link(nc.vector.tensor_tensor(again_stray[:, :], most[:, :], gr.stray[:, :], ALU.mult))
            link(nc.vector.scalar_tensor_tensor(far[:, :], gap[:, :], most[:, 0:1], shift[:, :], ALU.mult, ALU.add))
            link(nc.vector.tensor_copy(shift[:, :], far[:, :]))
            link(nc.vector.tensor_scalar(far[:, :], gap[:, :], most[:, 0:1], None, ALU.mult))
            link(nc.vector.tensor_tensor(gap[:, :], gap[:, :], far[:, :], ALU.subtract))

        @block.gpsimd
        def _(pool):
            pool.wait_ge(top_ready, 1)
            nc.gpsimd.partition_all_reduce(all_top[:, :], top[:, :], P, RED.max).then_inc(all_ready, 1)


def zero_sums(nc, prefix, ACC, flag):
    with ExitStack() as stack:
        block = stack.enter_context(nc.Block())

        @block.vector
        def _(dve):
            when(dve, flag, lambda: nc.vector.memset(ACC[:, :, :], 0.0))


def attention_finish(nc, prefix, X, ACC, gap):
    with ExitStack() as stack:
        m = Mem(nc, stack, prefix)
        eps = m.sb("eps", [P, H])
        rec = m.sb("rec", [P, NB, H])
        step = m.sem("step")
        eps_ready = m.sem("eps_ready")
        block = stack.enter_context(nc.Block())

        @block.vector
        def _(dve):
            link = Steps(dve, step)
            dve.wait_ge(eps_ready, 1)
            link(nc.vector.tensor_scalar(eps[:, :], eps[:, :], 1e-10, None, ALU.mult))
            link(nc.vector.tensor_tensor(rec[:, :, :], ACC[:, :, H * OF:AC],
                                         eps[:, :].unsqueeze(1).to_broadcast([P, NB, H]), ALU.add))
            link(nc.vector.reciprocal(rec[:, :, :], rec[:, :, :]))
            for hd in range(H):
                link.mark(nc.vector.tensor_tensor(ACC[:, :, hd * OF:(hd + 1) * OF], ACC[:, :, hd * OF:(hd + 1) * OF],
                                                  rec[:, :, hd:hd + 1].to_broadcast([P, NB, OF]), ALU.mult))
            dve.wait_ge(step, link.n)
            link(nc.vector.tensor_tensor(X[:, :, :], X[:, :, :], ACC[:, :, 0:D], ALU.add))

        @block.scalar
        def _(act):
            nc.scalar.activation(eps[:, :], gap[:, :], ACT.Exp).then_inc(eps_ready, 1)


def source_range(nc, prefix, keep, best, wide_range):
    with ExitStack() as stack:
        m = Mem(nc, stack, prefix)
        V = EX0 * H
        ends = m.sb("ends", [P, 2, H])
        all_ends = m.sb("all_ends", [P, 2, H])
        minus = m.sb("minus", [P, NB, H])
        far = m.sb("far", [P, H])
        most = m.sb("most", [P, 1])
        step = m.sem("step")
        ends_ready = m.sem("ends_ready")
        all_ready = m.sem("all_ready")
        block = stack.enter_context(nc.Block())

        @block.vector
        def _(dve):
            link = Steps(dve, step)
            a_src = keep[:, :, V:V + H]
            link(nc.vector.tensor_scalar(minus[:, :, :], a_src, -1.0, None, ALU.mult))
            nc.vector.tensor_reduce(ends[:, 0, :], a_src.rearrange("p n c -> p c n"), AX.X,
                                    ALU.max).then_inc(ends_ready, 1)
            nc.vector.tensor_reduce(ends[:, 1, :], minus[:, :, :].rearrange("p n c -> p c n"), AX.X,
                                    ALU.max).then_inc(ends_ready, 1)
            dve.wait_ge(all_ready, 1)
            link(nc.vector.tensor_tensor(far[:, :], all_ends[:, 0, :], all_ends[:, 1, :], ALU.add))
            link(nc.vector.tensor_scalar(far[:, :], far[:, :], FAR, None, ALU.is_gt))
            link(nc.vector.tensor_reduce(most[:, :], far[:, :], AX.X, ALU.max))
            link(nc.vector.tensor_copy(wide_range[:, :], most[:, :]))
            link(nc.vector.tensor_copy(best[:, :, :], all_ends[:, 0, :].unsqueeze(1).to_broadcast([P, NB, H])))

        @block.gpsimd
        def _(pool):
            pool.wait_ge(ends_ready, 2)
            nc.gpsimd.partition_all_reduce(all_ends[:, :, :].rearrange("p a h -> p (a h)"),
                                           ends[:, :, :].rearrange("p a h -> p (a h)"), P,
                                           RED.max).then_inc(all_ready, 1)


def segment_max(nc, prefix, keep, best, table_src, t_edge, src_in, dst_in, flag):
    with ExitStack() as stack:
        m = Mem(nc, stack, prefix)
        V = EX0 * H
        src = m.sb("src", [P, (G2 + 2) * T], I32)
        dst = m.sb("dst", [P, (G2 + 2) * T], I32)
        pidi = m.sb("pidi", [P, 1], I32)
        pid = m.sb("pid", [P, 1])
        stage = m.sb("stage", [P, T], I32)
        rows = m.sb("rows", [P, T, V + H])
        mine = m.sb("mine", [P, T, H + 1])
        line = m.sb("line", [P, GE, H + 1])
        apart = m.sb("apart", [P, GE])
        cand = m.sb("cand", [P, GE, H])
        top = m.sb("top", [P, 1, H])
        loaded = m.sem("loaded")
        pid_done = m.sem("pid_done")
        staged = m.sem("staged")
        pool_turn = m.sem("pool_turn")
        landed = m.sem("landed")
        mine_ready = m.sem("mine_ready")
        mine_out = m.sem("mine_out")
        line_in = m.sem("line_in")
        step = m.sem("step")
        block = stack.enter_context(nc.Block())
        BIG = 3.0e38
        ONCE = 2
        EACH = 6
        PER = 3 + NB * EACH

        @block.sync
        def _(sp):
            def body():
                sp.dma_start(src[:, :], src_in).then_inc(loaded, 16)
                sp.dma_start(dst[:, :], dst_in).then_inc(loaded, 16)
                with sp.Fori(0, G2) as g:
                    sp.wait_ge(mine_ready, g + 1)
                    sp.dma_start(t_edge.rearrange("(p c) -> p c", p=P),
                                 mine[:, :, :].rearrange("p t c -> p (t c)")).then_inc(mine_out, 16)
                    sp.wait_ge(mine_out, g * 16 + 16)
                    sp.dma_start(line[:, :, :].rearrange("p e c -> p (e c)"),
                                 t_edge.partition_broadcast(P)).then_inc(line_in, 16)

            when(sp, flag, body)

        @block.gpsimd
        def _(pool):
            def body():
                nc.gpsimd.iota(pidi[:, :], pattern=[[0, 1]], base=0, channel_multiplier=1).then_inc(pid_done, 1)
                with pool.Fori(0, G2) as g:
                    pool.wait_ge(staged, g + 1)
                    pool.sem_inc(pool_turn, 1)
                    for t in range(T):
                        pool.indirect_dma_start(
                            out=rows[:, t, :], out_offset=None, in_=table_src,
                            in_offset=bass.IndirectOffsetOnAxis(ap=stage[:, t:t + 1], axis=0),
                        ).then_inc(landed, 16)

            when(pool, flag, body)

        @block.vector
        def _(dve):
            def body():
                link = Steps(dve, step)
                dve.wait_ge(loaded, 32)
                dve.wait_ge(pid_done, 1)
                link(nc.vector.tensor_copy(pid[:, :], pidi[:, :]))
                link(nc.vector.tensor_copy(best[:, 0:NB - 1, :], keep[:, 0:NB - 1, V:V + H]))
                assert link.n == ONCE
                with dve.Fori(0, G2) as g:
                    nc.vector.tensor_scalar(stage[:, :], src[:, at(g, T)], N - 1, 0,
                                            ALU.min, ALU.max).then_inc(staged, 1)
                    link = Steps(dve, step, g * PER + ONCE)
                    dve.wait_ge(landed, g * (16 * T) + 16 * T)
                    link(nc.vector.tensor_copy(mine[:, :, 0:H], rows[:, :, V:]))
                    link(nc.vector.tensor_copy(mine[:, :, H], dst[:, at(g, T)]))
                    nc.vector.tensor_copy(top[:, 0, 0:1], pid[:, :]).then_inc(mine_ready, 1)
                    dve.wait_ge(line_in, g * 16 + 16)
                    link.mark(nc.vector.tensor_copy(apart[:, 0:1], pid[:, :]))
                    with dve.Fori(0, NB) as b:
                        link = Steps(dve, step, g * PER + b * EACH + (ONCE + 3))
                        dve.wait_ge(step, link.base)
                        link(nc.vector.tensor_scalar(apart[:, :], line[:, :, H], pid[:, 0:1], BIG,
                                                     ALU.is_equal, ALU.mult))
                        link(nc.vector.tensor_scalar(apart[:, :], apart[:, :], -BIG, None, ALU.add))
                        link(nc.vector.tensor_scalar(line[:, :, H], line[:, :, H], -float(P), None, ALU.add))
                        link(nc.vector.tensor_tensor(cand[:, :, :], line[:, :, 0:H],
                                                     apart[:, :].unsqueeze(2).to_broadcast([P, GE, H]), ALU.add))
                        link(nc.vector.tensor_reduce(top[:, 0, :], cand[:, :, :].rearrange("p e h -> p h e"), AX.X,
                                                     ALU.max))
                        link.mark(nc.vector.tensor_tensor(best[:, at(b), :], best[:, at(b), :], top[:, :, :], ALU.max))
                        assert link.n == EACH

            when(dve, flag, body)


def routing_tables(nc, prefix, keep, best, table_dst, tab, AGG):
    with ExitStack() as stack:
        m = Mem(nc, stack, prefix)
        V = EX0 * H
        t0 = m.sb("t0", [P, NB, H])
        t1 = m.sb("t1", [P, NB, H])
        rows = m.sb("rows", [P, NB, 2 * H])
        step = m.sem("step")
        rows_ready = m.sem("rows_ready")
        own_ready = m.sem("own_ready")
        weight_ready = m.sem("weight_ready")
        stored = m.sem("stored")
        high_ready = m.sem("high_ready")
        block = stack.enter_context(nc.Block())
        by_half = rows[:, :, :].rearrange("p (i a) c -> p a i c", a=2)
        A = AGG[:, :, :, :].rearrange("p n a c -> p (n a) c")

        @block.vector
        def _(dve):
            link = Steps(dve, step)
            link(nc.vector.tensor_tensor(t1[:, :, :], keep[:, :, V:V + H], keep[:, :, V + H:], ALU.add))
            link(nc.vector.tensor_tensor(t0[:, :, :], keep[:, :, V + H:], best[:, :, :], ALU.add))
            nc.vector.tensor_copy(rows[:, :, 0:H], keep[:, :, V + H:]).then_inc(rows_ready, 1)
            nc.vector.scalar_tensor_tensor(rows[:, :, H:], t0[:, :, :], 0.2, t0[:, :, :], ALU.mult,
                                           ALU.max).then_inc(rows_ready, 1)
            dve.wait_ge(rows_ready, 2)
            dve.wait_ge(high_ready, 1)
            nc.vector.tensor_tensor(tab[1][:, :, :, :], by_half, tab[0][:, :, :, :], ALU.subtract)
            link(nc.vector.scalar_tensor_tensor(t0[:, :, :], t1[:, :, :], 0.2, t1[:, :, :], ALU.mult, ALU.max))
            nc.vector.tensor_tensor(t0[:, :, :], t0[:, :, :], rows[:, :, H:], ALU.subtract).then_inc(own_ready, 1)
            dve.wait_ge(weight_ready, 1)
            link(nc.vector.tensor_tensor(A[:, :, 0:V].rearrange("p n (h e) -> p n h e", e=EX0),
                                         keep[:, :, 0:V].rearrange("p n (h e) -> p n h e", e=EX0),
                                         A[:, :, V:].unsqueeze(3).to_broadcast([P, NB, H, EX0]), ALU.mult))

        @block.scalar
        def _(act):
            act.wait_ge(rows_ready, 2)
            nc.scalar.activation(tab[0][:, :, :, :], by_half, ACT.Copy).then_inc(high_ready, 1)
            act.wait_ge(own_ready, 1)
            nc.scalar.activation(A[:, :, V:], t0[:, :, :], ACT.Exp).then_inc(weight_ready, 1)

        @block.sync
        def _(sp):
            sp.wait_ge(rows_ready, 2)
            sp.dma_start(table_dst.rearrange("(n p) c -> p n c", p=P), rows[:, :, :]).then_inc(stored, 16)
            sp.wait_ge(stored, 16)


def routing_with_experts(nc, prefix, table_src, table_dst, tab, src_in, dst_in, gr, ident, AGG, t_hT, t_y,
                         w1, b1, w2, b2):
    with ExitStack() as stack:
        m = Mem(nc, stack, prefix)
        V = EX0 * H
        NC = 4
        TC = T // NC
        PICK = 1
        PT = 2
        LANDED = 16 * (2 * T - PT)
        src = m.sb("src", [P, (G2 + 2) * T], I32)
        dst = m.sb("dst", [P, (G2 + 2) * T], I32)
        ints = m.sb("ints", [P, (G2 + 1) * T], I32)
        lo = m.sb("lo", [P, (G2 + 1) * T])
        hi = m.sb("hi", [P, G2 * T])
        stage = [[m.sb(f"stage{s}{e}", [P, T], I32) for e in range(2)] for s in range(2)]
        rows = [m.sb(f"rows{s}", [P, T, V + H]) for s in range(2)]
        rowd = [m.sb(f"rowd{s}", [P, T, 2 * H]) for s in range(2)]
        hot_first = [m.sb(f"hot_first{k}", [P, PT, W], F32R) for k in range(4)]
        hot = [m.sb(f"hot{s}", [P, T - PT, W], F32R) for s in range(2)]
        identr = m.sb("identr", [P, P], F32R)
        hotT = m.sb("hotT", [P, PT, 2, P], F32R)
        chosen = m.sb("chosen", [P, PT, HB, 2 * H])
        hoth = m.sb("hoth", [P, T, HB])
        sco = m.sb("sco", [P, T, H])
        sc2 = m.sb("sc2", [P, T, H])
        val = m.sb("val", [P, T, SC])
        part = [m.sb(f"part{k}", [P, T, SC], F32R) for k in range(2)]
        wide = [[m.sb(f"wide{s}{k}", [P, TC, HB, SC], F32R) for k in range(2)] for s in range(2)]
        zero = m.sb("zero", [P, HB * SC], F32R)
        raw = m.sb("raw", [P, KD, W])
        hT = [m.sb(f"hT{k}", [P, KD, W], F32R) for k in range(2)]
        hid = [m.sb(f"hid{s}", [P, M0, W]) for s in range(2)]
        y = [m.sb(f"y{s}", [P, 2, D]) for s in range(2)]
        sums = m.ps("sums", [P, 2, 512])
        psH = [m.ps(f"psH{j}", [P, 2, W]) for j in range(M0 // 2)]
        psY = [m.ps(f"psY{s}", [P, 2, D]) for s in range(2)]
        psT = m.ps("psT", [P, PT, 2, P])
        psG = m.ps("psG", [P, PT, HB, 2 * H])
        loaded = m.sem("loaded")
        step = m.sem("step")
        staged = m.sem("staged")
        gathering = m.sem("gathering")
        landed = [m.sem(f"landed{s}") for s in range(2)]
        rows_used = m.sem("rows_used")
        scores_ready = m.sem("scores_ready")
        weights_ready = m.sem("weights_ready")
        val_ready = m.sem("val_ready")
        high_ready = m.sem("high_ready")
        wide_ready = m.sem("wide_ready")
        summed = m.sem("summed")
        added = m.sem("added")
        zero_ready = m.sem("zero_ready")
        first_ready = m.sem("first_ready")
        first_turned = m.sem("first_turned")
        hotT_ready = m.sem("hotT_ready")
        picked = m.sem("picked")
        psG_used = m.sem("psG_used")
        rowd_chosen = m.sem("rowd_chosen")
        hoth_ready = m.sem("hoth_ready")
        raw_in = m.sem("raw_in")
        raw_high = m.sem("raw_high")
        hT_ready = m.sem("hT_ready")
        hid_made = m.sem("hid_made")
        hid_ready = m.sem("hid_ready")
        y_made = m.sem("y_made")
        y_ready = m.sem("y_ready")
        y_stored = [m.sem(f"y_stored{s}") for s in range(2)]
        block = stack.enter_context(nc.Block())
        UNITS = HB * EX0

        SLOW = (G2 - UNITS) // EX0
        FAST = HB - SLOW
        assert UNITS + SLOW * EX0 == G2

        def steps(eng, group, unit, second, tail):
            for e in range(EX0):
                group(e, e)
                unit(e, e)
                second(e, e)
            with eng.Fori(1, FAST) as i:
                for e in range(EX0):
                    group(i * EX0 + e, e)
                    unit(i * EX0 + e, e)
                    second(i * EX0 + e, e)
            with eng.Fori(0, SLOW) as j:
                for e in range(EX0):
                    group(j * (2 * EX0) + (FAST * EX0 + 2 * e), 2 * e % 4)
                    unit(j * EX0 + (FAST * EX0 + e), e)
                    group(j * (2 * EX0) + (FAST * EX0 + 2 * e + 1), (2 * e + 1) % 4)
                    second(j * EX0 + (FAST * EX0 + e), e)
            tail()

        @block.sync
        def _(sp):
            sp.dma_start(src[:, :], src_in).then_inc(loaded, 16)
            sp.dma_start(dst[:, :], dst_in).then_inc(loaded, 16)
            with sp.Fori(0, HB) as i:
                for e in range(EX0):
                    sp.wait_ge(y_ready, i * EX0 + (e + 1))
                    sp.dma_start(t_y[at(i), :, e, :].rearrange("a p c -> (a p) c"),
                                 y[e % 2][:, :, :].rearrange("p q d -> p (q d)")).then_inc(y_stored[e % 2], 16)
            for s in range(2):
                sp.wait_ge(y_stored[s], 16 * (UNITS // 2))

        @block.gpsimd
        def _(pool):
            def gather(n, s):
                pool.wait_ge(staged, n * 2 + 2)
                wait(pool, rows_used, n - 1)
                pool.sem_inc(gathering, 1)
                for t in range(T):
                    for k, (to, table) in enumerate(((rows, table_src), (rowd, table_dst))):
                        if k == 1 and t < PT:
                            continue
                        pool.indirect_dma_start(
                            out=to[s][:, t, :], out_offset=None, in_=table,
                            in_offset=bass.IndirectOffsetOnAxis(ap=stage[s][k][:, t:t + 1], axis=0),
                        ).then_inc(landed[s], 16)

            pairs(pool, G2, gather)

        @block.vector
        def _(dve):
            nc.vector.memset(zero[:, :].bitcast(F32), 0.0).then_inc(zero_ready, 1)
            dve.wait_ge(loaded, 32)
            link = Steps(dve, step)
            link(nc.vector.tensor_single_scalar(ints[:, :], dst[:, 0:(G2 + 1) * T], W - 1, ALU.bitwise_and))
            link(nc.vector.tensor_copy(lo[:, :], ints[:, :]))
            link(nc.vector.tensor_single_scalar(ints[:, :], dst[:, 0:(G2 + 1) * T], 8, ALU.arith_shift_right))
            link(nc.vector.tensor_copy(hi[:, :], ints[:, 0:G2 * T]))
            link(nc.vector.tensor_copy(identr[:, :], ident[:, :]))
            setup = link.n

            def put(n, s):
                for k, (of, end) in enumerate(((src, N - 1), (dst, NB * P - 1))):
                    nc.vector.tensor_scalar(stage[s][k][:, :], of[:, at(n, T)], end, 0,
                                            ALU.min, ALU.max).then_inc(staged, 1)

            LINKS = 3

            def mark_first(n, k, t):
                nc.vector.tensor_scalar(hot_first[k][:, t, :], gr.iota[:, :], lo[:, at(n * T + t)],
                                        None, ALU.is_equal).then_inc(first_ready, 1)

            def mark_later(n, s, t):
                nc.vector.tensor_scalar(hot[s][:, t - PT, :], gr.iota[:, :], lo[:, at(n * T + t)], None,
                                        ALU.is_equal)

            def group(n, k):
                s = k % 2
                link = Steps(dve, step, n * LINKS + setup)
                wait(dve, wide_ready, n * NC)
                nc.vector.tensor_tensor(hoth[:, :, :], gr.iota[:, 0:HB].unsqueeze(1).to_broadcast([P, T, HB]),
                                        hi[:, at(n, T)].unsqueeze(2).to_broadcast([P, T, HB]),
                                        ALU.is_equal).then_inc(hoth_ready, 1)
                wait(dve, summed, n * NC - NC)
                mark_later(n, s, 2)
                dve.wait_ge(hoth_ready, n + 1)
                dve.wait_ge(picked, n + 1)
                nc.vector.tensor_tensor(chosen[:, :, :, :], psG[:, :, :, :],
                                        hoth[:, 0:PT, :].unsqueeze(3).to_broadcast([P, PT, HB, 2 * H]),
                                        ALU.mult).then_inc(psG_used, 1)
                mark_later(n, s, 3)
                dve.wait_ge(psG_used, n + 1)
                nc.vector.tensor_reduce(rowd[s][:, 0:PT, :], chosen[:, :, :, :].rearrange("p t i c -> p t c i"),
                                        AX.X, ALU.add).then_inc(rowd_chosen, 1)
                mark_later(n, s, 4)
                dve.wait_ge(rowd_chosen, n + 1)
                dve.wait_ge(landed[s], (n - s) * (LANDED // 2) + LANDED)
                link.mark(nc.vector.tensor_tensor(sco[:, :, :], rows[s][:, :, V:], rowd[s][:, :, 0:H], ALU.add))
                mark_later(n, s, 5)
                link.done()
                link.mark(nc.vector.scalar_tensor_tensor(sc2[:, :, :], sco[:, :, :], 0.2, sco[:, :, :],
                                                         ALU.mult, ALU.max))
                mark_later(n, s, 6)
                link.done()
                link.mark(nc.vector.tensor_tensor(sc2[:, :, :], sc2[:, :, :], rowd[s][:, :, H:], ALU.subtract))
                mark_later(n, s, 7)
                link.done()
                assert link.n == LINKS and T == 8 and PT == 2
                nc.vector.tensor_scalar(sc2[:, :, :], sc2[:, :, :], 0.0, None, ALU.min).then_inc(scores_ready, 1)
                put(n + 2, s)
                mark_first(n + 1, (k + 1) % 4, 0)
                dve.wait_ge(weights_ready, n + 1)
                nc.vector.tensor_tensor(val[:, :, 0:V].rearrange("p t (h e) -> p t h e", e=EX0),
                                        rows[s][:, :, 0:V].rearrange("p t (h e) -> p t h e", e=EX0),
                                        val[:, :, V:].unsqueeze(3).to_broadcast([P, T, H, EX0]),
                                        ALU.mult).then_inc(rows_used, 1)
                mark_first(n + 1, (k + 1) % 4, 1)
                dve.wait_ge(high_ready, n + 1)
                nc.vector.tensor_tensor(part[1][:, :, :], val[:, :, :], part[0][:, :, :],
                                        ALU.subtract).then_inc(val_ready, 1)
                dve.wait_ge(val_ready, n + 1)
                for c in range(NC):
                    wait(dve, summed, n * NC + c - 1)
                    tiles = slice(c * TC, (c + 1) * TC)
                    for p in range(2):
                        last = nc.vector.tensor_tensor(
                            wide[c % 2][p][:, :, :, :],
                            hoth[:, tiles, :].unsqueeze(3).to_broadcast([P, TC, HB, SC]),
                            part[p][:, tiles, :].unsqueeze(2).to_broadcast([P, TC, HB, SC]), ALU.mult)
                    last.then_inc(wide_ready, 1)

            def take(u, e):
                s = e % 2
                dve.wait_ge(y_made, u + 1)
                wait(dve, y_stored[s], (u - s) * 8)
                nc.vector.tensor_tensor(y[s][:, :, :], psY[s][:, :, :],
                                        b2[:, e, :].unsqueeze(1).to_broadcast([P, 2, D]),
                                        ALU.add).then_inc(y_ready, 1)

            def unit(u, e):
                if e == 0:
                    i = u // EX0
                    dve.wait_ge(raw_high, i + 1)
                    nc.vector.tensor_tensor(hT[1][:, :, :], raw[:, :, :], hT[0][:, :, :],
                                            ALU.subtract).then_inc(hT_ready, 1)
                if not (isinstance(u, int) and u < 2):
                    take(u - 2, (e - 2) % EX0)

            def tail():
                take(UNITS - 2, 2)
                take(UNITS - 1, 3)

            put(0, 0)
            put(1, 1)
            for t in range(PT):
                mark_first(0, 0, t)
            steps(dve, group, unit, lambda u, e: None, tail)
            dve.wait_ge(summed, G2 * NC + 1)
            for half in range(2):
                nc.vector.tensor_tensor(AGG[:, :, half, :], AGG[:, :, half, :],
                                        sums[:, half, 0:HB * SC].rearrange("p (n c) -> p n c", c=SC),
                                        ALU.add).then_inc(added, 1)
            dve.wait_ge(added, 2)

        @block.scalar
        def _(act):
            def load_raw(i):
                wait(act, hT_ready, i)
                act.dma_start(raw[:, :, :].rearrange("p k c -> p (k c)"),
                              t_hT[at(i), :, :].rearrange("a p c -> (a p) c")).then_inc(raw_in, 16)

            def turn_first(n):
                act.wait_ge(first_turned, n + 1)
                wait(act, picked, n)
                nc.scalar.activation(hotT[:, :, :, :], psT[:, :, :, :], ACT.Copy).then_inc(hotT_ready, 1)

            def group(n, k):
                act.wait_ge(scores_ready, n + 1)
                wait(act, val_ready, n)
                nc.scalar.activation(val[:, :, V:], sc2[:, :, :], ACT.Exp).then_inc(weights_ready, 1)
                act.wait_ge(rows_used, n + 1)
                wait(act, wide_ready, n * NC)
                nc.scalar.activation(part[0][:, :, :], val[:, :, :], ACT.Copy).then_inc(high_ready, 1)
                turn_first(n + 1)

            def hidden(u, e):
                wait(act, y_made, u - 1)
                for j in range(M0):
                    if j % 2 == 0:
                        act.wait_ge(hid_made, u * M0 + (j + 2))
                    nc.scalar.activation(hid[e % 2][:, j, :], psH[j // 2][:, j % 2, :], ACT.Gelu,
                                         bias=b1[:, e, j:j + 1]).then_inc(hid_ready, 1)

            def unit(u, e):
                i = u // EX0
                if e == 0:
                    load_raw(i)
                if not (isinstance(u, int) and u < 1):
                    hidden(u - 1, (e - 1) % EX0)
                if e == 0:
                    act.wait_ge(raw_in, i * 16 + 16)
                    nc.scalar.activation(hT[0][:, :, :], raw[:, :, :], ACT.Copy).then_inc(raw_high, 1)

            turn_first(0)
            steps(act, group, unit, lambda u, e: None, lambda: hidden(UNITS - 1, EX0 - 1))

        @block.tensor
        def _(pe):
            def turn_first(n, k):
                pe.wait_ge(first_ready, n * PT + PT)
                wait(pe, hotT_ready, n)
                for t in range(PT):
                    for b in range(2):
                        last = nc.tensor.matmul(psT[:, t, b, :], hot_first[k][:, t, b * P:(b + 1) * P], identr[:, :],
                                                start=True, stop=True)
                last.then_inc(first_turned, 1)

            def pick_first(n):
                pe.wait_ge(hotT_ready, n + 1)
                wait(pe, psG_used, n)
                for t in range(PT):
                    for b in range(2):
                        for part_ in range(2):
                            last = nc.tensor.matmul(psG[:, t, :, :].rearrange("p i c -> p (i c)"), hotT[:, t, b, :],
                                                    tab[part_][:, b, :, :].rearrange("p i c -> p (i c)"),
                                                    start=b == 0 and part_ == 0, stop=b == 1 and part_ == 1)
                last.then_inc(picked, 1)

            def group(n, k):
                first = isinstance(n, int) and n == 0
                turn_first(n + 1, (k + 1) % 4)
                for c in range(NC):
                    pe.wait_ge(wide_ready, n * NC + (c + 1))
                    for t in range(c * TC, (c + 1) * TC):
                        place = hot_first[k][:, t, :] if t < PT else hot[k % 2][:, t - PT, :]
                        for p in range(2):
                            for b in range(2):
                                last = nc.tensor.matmul(
                                    sums[:, b, 0:HB * SC], place[:, b * P:(b + 1) * P],
                                    wide[c % 2][p][:, t - c * TC, :, :].rearrange("p n c -> p (n c)"),
                                    start=first and t == 0 and p == 0, stop=False)
                    last.then_inc(summed, 1)
                    if c == PICK:
                        pick_first(n + 1)

            def hidden(u, e):
                pe.wait_ge(hT_ready, u // EX0 + 1)
                for j in range(M0):
                    if j % 2 == 0:
                        wait(pe, hid_ready, u * M0 + (j - 2))
                    for k in range(KD):
                        for a, b in PASSES:
                            last = nc.tensor.matmul(psH[j // 2][:, j % 2, :], w1[a][:, e, k, j * P:(j + 1) * P],
                                                    hT[b][:, k, :], start=k == 0 and (a, b) == PASSES[0],
                                                    stop=k == KD - 1 and (a, b) == PASSES[-1])
                    last.then_inc(hid_made, 1)

            def rows_of(u, e):
                pe.wait_ge(hid_ready, u * M0 + M0)
                wait(pe, y_ready, u - 1)
                for q in range(2):
                    for k in range(M0):
                        last = nc.tensor.matmul(psY[e % 2][:, q, :], hid[e % 2][:, k, q * P:(q + 1) * P],
                                                w2[:, e, k, :], start=(k == 0), stop=(k == M0 - 1))
                last.then_inc(y_made, 1)

            def second(u, e):
                if not (isinstance(u, int) and u < 1):
                    rows_of(u - 1, (e - 1) % EX0)

            turn_first(0, 0)
            pick_first(0)
            steps(pe, group, hidden, second, lambda: rows_of(UNITS - 1, EX0 - 1))
            pe.wait_ge(zero_ready, 1)
            for b in range(2):
                last = nc.tensor.matmul(sums[:, b, 0:HB * SC], zero[:, 0:P], zero[:, :], start=False, stop=True)
            last.then_inc(summed, 1)


def add_experts(nc, prefix, X, GT, t_y):
    with ExitStack() as stack:
        m = Mem(nc, stack, prefix)
        y = [m.sb(f"y{s}", [P, EX0, 2, D]) for s in range(3)]
        y_in = [m.sem(f"y_in{s}") for s in range(3)]
        added = m.sem("added")
        block = stack.enter_context(nc.Block())

        def thirds(eng, body):
            for s in range(3):
                body(s, s)
            with eng.Fori(1, HB // 3) as i:
                for s in range(3):
                    body(i * 3 + s, s)
            for n in range(HB - HB % 3, HB):
                body(n, n % 3)

        @block.sync
        def _(sp):
            def pair(n, s):
                wait(sp, added, (n - 2) * (2 * EX0))
                sp.dma_start(y[s][:, :, :, :].rearrange("p e q d -> p (e q d)"),
                             t_y[at(n), :, :, :].rearrange("a p e c -> (a p) (e c)")).then_inc(y_in[s], 16)

            thirds(sp, pair)

        @block.vector
        def _(dve):
            def pair(n, s):
                if isinstance(n, int):
                    dve.wait_ge(y_in[s], (n // 3 + 1) * 16)
                else:
                    dve.wait_ge(y_in[s], (n // 3) * 16 + 16)
                for e in range(EX0):
                    for q in range(2):
                        b = n * 2 + q
                        if e > 0:
                            dve.wait_ge(added, n * (2 * EX0) + (2 * e + q - 1))
                        nc.vector.scalar_tensor_tensor(X[:, at(b), :], y[s][:, e, q, :].unsqueeze(1),
                                                       GT[:, at(b), e], X[:, at(b), :],
                                                       ALU.mult, ALU.add).then_inc(added, 1)

            thirds(dve, pair)


def routing_scores(nc, prefix, AGG, b_gat, gamma, beta, S):
    with ExitStack() as stack:
        m = Mem(nc, stack, prefix)
        V = EX0 * H
        A = AGG[:, :, :, :].rearrange("p n a c -> p (n a) c")
        y = m.sb("y", [P, NB, V])
        sq = m.sb("sq", [P, NB, V])
        rec = m.sb("rec", [P, NB, H])
        t0 = m.sb("t0", [P, NB])
        t1 = m.sb("t1", [P, NB])
        step = m.sem("step")
        var_ready = m.sem("var_ready")
        std_ready = m.sem("std_ready")
        block = stack.enter_context(nc.Block())
        full = [P, NB, V]

        @block.vector
        def _(dve):
            link = Steps(dve, step)
            link(nc.vector.tensor_scalar(rec[:, :, :], A[:, :, V:], 1e-16, None, ALU.add))
            link(nc.vector.reciprocal(rec[:, :, :], rec[:, :, :]))
            link(nc.vector.tensor_tensor(y[:, :, :].rearrange("p n (h e) -> p n h e", e=EX0),
                                         A[:, :, 0:V].rearrange("p n (h e) -> p n h e", e=EX0),
                                         rec[:, :, :].unsqueeze(3).to_broadcast([P, NB, H, EX0]), ALU.mult))
            link(nc.vector.tensor_tensor(y[:, :, :], y[:, :, :], b_gat[:, :].unsqueeze(1).to_broadcast(full), ALU.add))
            link(nc.vector.tensor_reduce(t0[:, :], y[:, :, :], AX.X, ALU.add))
            link(nc.vector.tensor_scalar(t0[:, :], t0[:, :], 1.0 / V, None, ALU.mult))
            link(nc.vector.tensor_tensor(y[:, :, :], y[:, :, :], t0[:, :].unsqueeze(2).to_broadcast(full), ALU.subtract))
            link(nc.vector.tensor_tensor(sq[:, :, :], y[:, :, :], y[:, :, :], ALU.mult))
            link(nc.vector.tensor_reduce(t0[:, :], sq[:, :, :], AX.X, ALU.add))
            nc.vector.tensor_scalar(t0[:, :], t0[:, :], 1.0 / V, LN_EPS, ALU.mult, ALU.add).then_inc(var_ready, 1)
            dve.wait_ge(std_ready, 1)
            link(nc.vector.reciprocal(t1[:, :], t1[:, :]))
            link(nc.vector.tensor_tensor(y[:, :, :], y[:, :, :], t1[:, :].unsqueeze(2).to_broadcast(full), ALU.mult))
            link(nc.vector.tensor_tensor(y[:, :, :], y[:, :, :], gamma[:, :].unsqueeze(1).to_broadcast(full), ALU.mult))
            link(nc.vector.tensor_tensor(y[:, :, :], y[:, :, :], beta[:, :].unsqueeze(1).to_broadcast(full), ALU.add))
            link(nc.vector.tensor_reduce(S[:, :, :], y[:, :, :].rearrange("p n (h e) -> p n e h", e=EX0), AX.X, ALU.add))
            link(nc.vector.tensor_scalar(S[:, :, :], S[:, :, :], 1.0 / H, None, ALU.mult))

        @block.scalar
        def _(act):
            act.wait_ge(var_ready, 1)
            nc.scalar.activation(t1[:, :], t0[:, :], ACT.Sqrt).then_inc(std_ready, 1)


def experts(nc, prefix, X, t_hT, GT, weights, biases, out_bias, out_dram):
    with ExitStack() as stack:
        m = Mem(nc, stack, prefix)
        L = 2
        raw = m.sb("raw", [P, KD, W])
        hT = [[m.sb(f"hT{s}{k}", [P, KD, W], F32R) for k in range(2)] for s in range(2)]
        full = [[m.sb(f"full{l}{s}", [P, KD, W]) for s in range(2)] for l in range(L)]
        hid = [[[m.sb(f"hid{l}{s}{k}", [P, KD, W], F32R) for k in range(2)] for s in range(2)] for l in range(L)]
        psH = [[m.ps(f"psH{l}{s}", [P, KD, W]) for s in range(2)] for l in range(L)]
        psY = [m.ps(f"psY{s}", [P, 2, D]) for s in range(2)]
        raw_in = m.sem("raw_in")
        raw_high = m.sem("raw_high")
        hT_ready = m.sem("hT_ready")
        made = [m.sem(f"made{l}") for l in range(L)]
        full_ready = [m.sem(f"full_ready{l}") for l in range(L)]
        high_ready = [m.sem(f"high_ready{l}") for l in range(L)]
        hid_ready = [m.sem(f"hid_ready{l}") for l in range(L)]
        y_made = m.sem("y_made")
        added = m.sem("added")
        stored = m.sem("stored")
        block = stack.enter_context(nc.Block())
        AHEAD = 3

        def units(eng, body, tail):
            def pair(i, s):
                for e in range(EX1):
                    body(i, s, e)

            pair(0, 0)
            with eng.Fori(0, (HB - 3) // 2) as j:
                pair(j * 2 + 1, 1)
                pair(j * 2 + 2, 0)
            pair(HB - 2, 1)
            pair(HB - 1, 0)
            tail()

        def before(i, e, k, stage):
            if e >= k:
                stage(i, e - k)
            elif not isinstance(i, int) or i > 0:
                stage(i - 1, e - k + EX1)

        @block.tensor
        def _(pe):
            def hidden(l, s=None):
                def stage(i, e):
                    u = i * EX1 + e
                    if l == 0:
                        pe.wait_ge(hT_ready, i + 1)
                    else:
                        pe.wait_ge(hid_ready[l - 1], u + 1)
                    wait(pe, full_ready[l], u * KD - KD)
                    for j in range(KD):
                        for k in range(KD):
                            for a, b in PASSES:
                                x = hT[s][b] if l == 0 else hid[l - 1][e % 2][b]
                                last = nc.tensor.matmul(psH[l][e % 2][:, j, :],
                                                        weights[l][a][:, e, k, j * P:(j + 1) * P], x[:, k, :],
                                                        start=k == 0 and (a, b) == PASSES[0],
                                                        stop=k == KD - 1 and (a, b) == PASSES[-1])
                    last.then_inc(made[l], 1)
                return stage

            def rows(i, e):
                u = i * EX1 + e
                pe.wait_ge(hid_ready[1], u + 1)
                wait(pe, added, u * 4 - 4)
                for q in range(2):
                    for k in range(KD):
                        for a, b in PASSES:
                            last = nc.tensor.matmul(psY[e % 2][:, q, :], hid[1][e % 2][b][:, k, q * P:(q + 1) * P],
                                                    weights[2][a][:, e, k, :],
                                                    start=k == 0 and (a, b) == PASSES[0],
                                                    stop=k == KD - 1 and (a, b) == PASSES[-1])
                last.then_inc(y_made, 1)

            def unit(i, s, e):
                before(i, e, 4, rows)
                before(i, e, 2, hidden(1))
                hidden(0, s)(i, e)

            def tail():
                for e in (EX1 - 2, EX1 - 1):
                    rows(HB - 1, e - 2)
                    hidden(1)(HB - 1, e)
                rows(HB - 1, EX1 - 2)
                rows(HB - 1, EX1 - 1)

            units(pe, unit, tail)

        @block.scalar
        def _(act):
            def take(l):
                def stage(i, e):
                    u = i * EX1 + e
                    act.wait_ge(made[l], u + 1)
                    wait(act, hid_ready[l], u - 1)
                    for j in range(KD):
                        nc.scalar.activation(full[l][e % 2][:, j, :], psH[l][e % 2][:, j, :], ACT.Relu,
                                             bias=biases[l][:, e, j:j + 1]).then_inc(full_ready[l], 1)
                    act.wait_ge(full_ready[l], u * KD + KD)
                    wait(act, made[1] if l == 0 else y_made, u - 1)
                    nc.scalar.activation(hid[l][e % 2][0][:, :, :], full[l][e % 2][:, :, :],
                                         ACT.Copy).then_inc(high_ready[l], 1)
                return stage

            def split_pair(i, s):
                if not (isinstance(i, int) and i < 2):
                    act.wait_ge(made[0], i * EX1 - EX1)
                act.wait_ge(raw_in, i * 16 + 16)
                nc.scalar.activation(hT[s][0][:, :, :], raw[:, :, :], ACT.Copy).then_inc(raw_high, 1)

            def unit(i, s, e):
                if e == AHEAD and not (isinstance(i, int) and i == HB - 1):
                    split_pair(i + 1, 1 - s)
                before(i, e, 2, take(1))
                take(0)(i, e)

            def tail():
                take(1)(HB - 1, EX1 - 2)
                take(1)(HB - 1, EX1 - 1)

            split_pair(0, 0)
            units(act, unit, tail)

        @block.vector
        def _(dve):
            def low(l):
                def stage(i, e):
                    u = i * EX1 + e
                    dve.wait_ge(high_ready[l], u + 1)
                    nc.vector.tensor_tensor(hid[l][e % 2][1][:, :, :], full[l][e % 2][:, :, :],
                                            hid[l][e % 2][0][:, :, :], ALU.subtract).then_inc(hid_ready[l], 1)
                return stage

            def add(i, e):
                u = i * EX1 + e
                for k in range(4):
                    q = k % 2
                    b = i * 2 + q
                    if k == 2:
                        dve.wait_ge(y_made, u + 1)
                    wait(dve, added, u * 4 + (k - 1))
                    what = out_bias[:, e:e + 1, :] if k < 2 else psY[e % 2][:, q:q + 1, :]
                    nc.vector.scalar_tensor_tensor(X[:, at(b), :], what, GT[:, at(b), e], X[:, at(b), :],
                                                   ALU.mult, ALU.add).then_inc(added, 1)

            def split_pair(i, s):
                dve.wait_ge(raw_high, i + 1)
                nc.vector.tensor_tensor(hT[s][1][:, :, :], raw[:, :, :], hT[s][0][:, :, :],
                                        ALU.subtract).then_inc(hT_ready, 1)

            def unit(i, s, e):
                if e == AHEAD and not (isinstance(i, int) and i == HB - 1):
                    split_pair(i + 1, 1 - s)
                before(i, e, 2, low(1))
                low(0)(i, e)
                before(i, e, 4, add)

            def tail():
                for e in (EX1 - 2, EX1 - 1):
                    low(1)(HB - 1, e)
                    add(HB - 1, e - 2)
                add(HB - 1, EX1 - 2)
                add(HB - 1, EX1 - 1)

            split_pair(0, 0)
            units(dve, unit, tail)

        @block.sync
        def _(sp):
            def load_pair(i):
                wait(sp, hT_ready, i)
                sp.dma_start(raw[:, :, :].rearrange("p k c -> p (k c)"),
                             t_hT[at(i), :, :].rearrange("a p c -> (a p) c")).then_inc(raw_in, 16)

            def store_pair(i):
                sp.wait_ge(added, i * (4 * EX1) + 4 * EX1)
                sp.dma_start(out_dram[at(i, W), :].rearrange("(b p) d -> p b d", p=P),
                             X[:, at(i, 2), :]).then_inc(stored, 16)

            load_pair(0)
            load_pair(1)
            with sp.Fori(2, HB) as i:
                load_pair(i)
                store_pair(i - 2)
            store_pair(HB - 2)
            sp.wait_ge(added, HB * (4 * EX1))
            sp.dma_start(out_dram[VB * P:N, :], X[0:VR, VB, :]).then_inc(stored, 16)
            sp.wait_ge(stored, 16 * HB)


def turn_and_route(nc, prefix, X, rstd, nmr, ident, t_hT, w1, b1, w2, b2, LG):
    with ExitStack() as stack:
        m = Mem(nc, stack, prefix)
        h = [[m.sb(f"h{s}{q}", [P, D]) for q in range(2)] for s in range(2)]
        HT = [m.sb(f"HT{s}", [P, KD, W]) for s in range(2)]
        hid = [m.sb(f"hid{s}", [P, W]) for s in range(2)]
        top = m.sb("top", [P, NB])
        psT = [m.ps(f"psT{s}", [P, KD, P]) for s in range(2)]
        psH = [m.ps(f"psH{s}", [P, W]) for s in range(2)]
        psL = [m.ps(f"psL{s}", [P, 2, EX1]) for s in range(2)]
        stored = [m.sem(f"stored{s}") for s in range(2)]
        h_ready = m.sem("h_ready")
        h_turned = m.sem("h_turned")
        HT_ready = m.sem("HT_ready")
        made = m.sem("made")
        hid_ready = m.sem("hid_ready")
        logits_ready = m.sem("logits_ready")
        logits_taken = m.sem("logits_taken")
        step = m.sem("step")
        d_ready = m.sem("d_ready")
        exp_ready = m.sem("exp_ready")
        block = stack.enter_context(nc.Block())
        full = [P, NB, EX1]

        def groups(eng, body):
            pairs(eng, HB - 1, body)
            body(HB - 1, 0)

        def after(n, k):
            return not isinstance(n, int) or n >= k

        @block.scalar
        def _(act):
            def hidden(n, s):
                act.wait_ge(made, n + 1)
                act.wait_ge(logits_ready, n + 1)
                nc.scalar.activation(hid[s][:, :], psH[s][:, :], ACT.Relu, bias=b1[:, 0:1]).then_inc(hid_ready, 1)

            def pair(n, s):
                for q in range(2):
                    b = n * 2 + q
                    wait(act, h_turned, b - 3)
                    nc.scalar.activation(h[s][q][:, :], X[:, at(b), :], ACT.Identity, bias=nmr[:, at(b)],
                                         scale=rstd[:, at(b)]).then_inc(h_ready, 1)
                if after(n, 2):
                    hidden(n - 2, s)

            groups(act, pair)
            hidden(HB - 2, 1)
            hidden(HB - 1, 0)
            act.wait_ge(d_ready, 1)
            nc.scalar.activation(LG[:, :, :], LG[:, :, :], ACT.Exp).then_inc(exp_ready, 1)

        @block.tensor
        def _(pe):
            pe.sem_inc(logits_ready, 2)

            def hidden(n, s):
                pe.wait_ge(HT_ready, n * 2 + 2)
                wait(pe, hid_ready, n - 1)
                for k in range(KD):
                    last = nc.tensor.matmul(psH[s][:, :], w1[:, k, :], HT[s][:, k, :],
                                            start=(k == 0), stop=(k == KD - 1))
                last.then_inc(made, 1)

            def logits(n, s):
                pe.wait_ge(hid_ready, n + 1)
                pe.wait_ge(logits_taken, n + 1)
                for q in range(2):
                    last = nc.tensor.matmul(psL[s][:, q, :], hid[s][:, q * P:(q + 1) * P], w2[:, :],
                                            start=True, stop=True)
                last.then_inc(logits_ready, 1)

            def pair(n, s):
                for q in range(2):
                    b = n * 2 + q
                    pe.wait_ge(h_ready, b + 1)
                    wait(pe, HT_ready, b - 1)
                    for k in range(KD):
                        last = nc.tensor.transpose(psT[q][:, k, :], h[s][q][:, k * P:(k + 1) * P], ident[:, :])
                    last.then_inc(h_turned, 1)
                if after(n, 1):
                    hidden(n - 1, 1 - s)
                if after(n, 2):
                    logits(n - 2, s)

            groups(pe, pair)
            hidden(HB - 1, 0)
            logits(HB - 2, 1)
            logits(HB - 1, 0)

        @block.vector
        def _(dve):
            def take(n, s):
                dve.wait_ge(logits_ready, n + 3)
                nc.vector.tensor_tensor(LG[:, at(n, 2), :], psL[s][:, :, :],
                                        b2[:, :].unsqueeze(1).to_broadcast([P, 2, EX1]),
                                        ALU.add).then_inc(logits_taken, 1)

            def pair(n, s):
                for q in range(2):
                    b = n * 2 + q
                    dve.wait_ge(h_turned, b + 1)
                    if q == 0:
                        wait(dve, made, n - 1)
                        wait(dve, stored[s], (n - s) * 8)
                    nc.vector.tensor_copy(HT[s][:, :, q * P:(q + 1) * P], psT[q][:, :, :]).then_inc(HT_ready, 1)
                if after(n, 2):
                    take(n - 2, s)

            dve.sem_inc(logits_taken, 2)
            groups(dve, pair)
            take(HB - 2, 1)
            take(HB - 1, 0)
            dve.wait_ge(logits_taken, HB + 2)
            link = Steps(dve, step)
            link(nc.vector.tensor_reduce(top[:, :], LG[:, :, :], AX.X, ALU.max))
            nc.vector.tensor_tensor(LG[:, :, :], LG[:, :, :], top[:, :].unsqueeze(2).to_broadcast(full),
                                    ALU.subtract).then_inc(d_ready, 1)
            dve.wait_ge(exp_ready, 1)
            link(nc.vector.tensor_reduce(top[:, :], LG[:, :, :], AX.X, ALU.add))
            link(nc.vector.reciprocal(top[:, :], top[:, :]))
            link(nc.vector.tensor_tensor(LG[:, :, :], LG[:, :, :], top[:, :].unsqueeze(2).to_broadcast(full),
                                         ALU.mult))

        @block.sync
        def _(sp):
            def pair(n, s):
                sp.wait_ge(HT_ready, n * 2 + 2)
                sp.dma_start(t_hT[at(n), :, :].rearrange("a p (k c) -> (a p) k c", k=KD),
                             HT[s][:, :, :]).then_inc(stored[s], 16)

            groups(sp, pair)
            for s in range(2):
                sp.wait_ge(stored[s], 16 * ((HB + 1 - s) // 2))


def batch_normalized(nc, prefix, X, ACC, gr, bn_w, bn_b):
    with ExitStack() as stack:
        m = Mem(nc, stack, prefix)
        LP = HB - 1
        assert VB == 2 * LP
        ones = m.sb("ones", [P, P])
        valid = m.sb("valid", [P, P])
        sq = [m.sb(f"sq{s}", [P, 2, D]) for s in range(2)]
        mean = m.sb("mean", [P, D])
        zero = m.sb("zero", [P, 2 * D])
        scale = m.sb("scale", [P, D])
        var = m.sb("var", [P, D])
        psS = m.ps("psS", [P, 2, D])
        psV = m.ps("psV", [P, 2, D])
        psSL = m.ps("psSL", [P, D])
        psVL = m.ps("psVL", [P, D])
        consts_ready = m.sem("consts_ready")
        summed = m.sem("summed")
        x_shifted = m.sem("x_shifted")
        step = m.sem("step")
        d_ready = m.sem("d_ready")
        sq_ready = m.sem("sq_ready")
        sq_summed = m.sem("sq_summed")
        var_ready = m.sem("var_ready")
        std_ready = m.sem("std_ready")
        scaled = m.sem("scaled")
        block = stack.enter_context(nc.Block())

        def groups(eng, body):
            pairs(eng, HB - 1, body)
            body(HB - 1, 0)

        def column_sums(n, to, last_to, pair, used):
            if isinstance(n, int) and n == LP:
                nc.tensor.matmul(last_to[:, :], valid[:, :], pair[:, 0, :], start=True, stop=True).then_inc(used, 1)
            else:
                nc.tensor.matmul(to[:, :, :].rearrange("p a d -> p (a d)"), ones[:, :],
                                 pair.rearrange("p a d -> p (a d)"), start=isinstance(n, int) and n == 0,
                                 stop=False).then_inc(used, 1)

        @block.tensor
        def _(pe):
            pe.wait_ge(consts_ready, 3)

            def end(to, used):
                nc.tensor.matmul(to[:, :, :].rearrange("p a d -> p (a d)"), ones[:, :], zero[:, :],
                                 start=False, stop=True).then_inc(used, 1)

            groups(pe, lambda n, s: column_sums(n, psS, psSL, ACC[:, at(n, 2), :], summed))
            end(psS, summed)

            def squares(n, s):
                pe.wait_ge(sq_ready, n + 1)
                column_sums(n, psV, psVL, sq[s][:, :, :], sq_summed)

            groups(pe, squares)
            end(psV, sq_summed)

        @block.scalar
        def _(act):
            def square(n, s):
                act.wait_ge(d_ready, n + 1)
                wait(act, sq_summed, n - 1)
                nc.scalar.activation(sq[s][:, :, :], ACC[:, at(n, 2), :], ACT.Square).then_inc(sq_ready, 1)

            groups(act, square)
            act.wait_ge(var_ready, 1)
            nc.scalar.activation(var[:, :], var[:, :], ACT.Sqrt).then_inc(std_ready, 1)

        @block.vector
        def _(dve):
            nc.vector.memset(ones[:, :], 1.0).then_inc(consts_ready, 1)
            nc.vector.memset(zero[:, :], 0.0).then_inc(consts_ready, 1)
            nc.vector.tensor_scalar(valid[:, :], gr.diff[:, 0:1].to_broadcast([P, P]), -float(VR), None,
                                    ALU.is_gt).then_inc(consts_ready, 1)
            full = [P, NB, D]
            nc.vector.tensor_tensor(X[:, :, :], X[:, :, :], bn_b[:, :].unsqueeze(1).to_broadcast(full),
                                    ALU.add).then_inc(x_shifted, 1)

            def average(link, to, ps, psl, plus):
                link(nc.vector.tensor_copy(to[:, :], ps[:, 0, :]))
                link(nc.vector.tensor_tensor(to[:, :], to[:, :], ps[:, 1, :], ALU.add))
                link(nc.vector.tensor_tensor(to[:, :], to[:, :], psl[:, :], ALU.add))
                link(nc.vector.tensor_scalar(to[:, :], to[:, :], 1.0 / N, plus, ALU.mult, ALU.add))

            dve.wait_ge(summed, HB + 1)
            link = Steps(dve, step)
            average(link, mean, psS, psSL, 0.0)
            pair_of = mean[:, :].unsqueeze(1).to_broadcast([P, 2, D])

            def center(n, s):
                nc.vector.tensor_tensor(ACC[:, at(n, 2), :], ACC[:, at(n, 2), :], pair_of,
                                        ALU.subtract).then_inc(d_ready, 1)

            groups(dve, center)
            dve.wait_ge(sq_summed, HB + 1)
            average(link, var, psV, psVL, LN_EPS)
            dve.sem_inc(var_ready, 1)
            dve.wait_ge(std_ready, 1)
            link(nc.vector.reciprocal(scale[:, :], var[:, :]))
            link(nc.vector.tensor_tensor(scale[:, :], scale[:, :], bn_w[:, :], ALU.mult))
            scale_of = scale[:, :].unsqueeze(1).to_broadcast([P, 2, D])
            dve.wait_ge(x_shifted, 1)

            def add(n, s):
                dve.wait_ge(scaled, n + 1)
                nc.vector.tensor_tensor(X[:, at(n, 2), :], X[:, at(n, 2), :], ACC[:, at(n, 2), :], ALU.add)

            def scale_pair(n, s):
                nc.vector.tensor_tensor(ACC[:, at(n, 2), :], ACC[:, at(n, 2), :], scale_of,
                                        ALU.mult).then_inc(scaled, 1)
                if not (isinstance(n, int) and n < 1):
                    add(n - 1, 1 - s)

            dve.wait_ge(d_ready, HB)
            groups(dve, scale_pair)
            add(HB - 1, 0)


def score_columns(nc, prefix, wf, attn, wproj, wgat, att, wg):
    with ExitStack() as stack:
        m = Mem(nc, stack, prefix)
        V = EX0 * H
        prod = m.sb("prod", [P, KD, 2, V])
        psA = m.ps("psA", [P, 2, KD, H])
        made = m.sem("made")
        step = m.sem("step")
        block = stack.enter_context(nc.Block())

        @block.tensor
        def _(pe):
            for a in range(2):
                for k in range(KD):
                    last = nc.tensor.matmul(psA[:, a, k, :], wf[:, a, k * P:(k + 1) * P], attn[:, :],
                                            start=True, stop=True)
            last.then_inc(made, 1)

        @block.vector
        def _(dve):
            link = Steps(dve, step)
            for a in range(2):
                link.mark(nc.vector.tensor_tensor(prod[:, :, a, :], wgat[:, :, :],
                                                  att[:, a, :].unsqueeze(1).to_broadcast([P, KD, V]), ALU.mult))
            dve.wait_ge(step, 2)
            nc.vector.tensor_copy(wg[:, :, 0:V], wgat[:, :, :])
            for k in range(KD):
                nc.vector.tensor_reduce(wg[:, k, V:].rearrange("p (a h) -> p a h", a=2),
                                        prod[:, k, :, :].rearrange("p a (h e) -> p a h e", e=EX0), AX.X, ALU.add)
            dve.wait_ge(made, 1)
            for a in range(2):
                nc.vector.tensor_copy(wproj[:, :, a * MC + OF:(a + 1) * MC], psA[:, a, :, :])


def gnn_ffn(nc, x_in, src1, dst1, first1, attr, w_msg, w_rows, attn_t, w_gat, att, b_gat, gamma, beta,
            e0_w1, e0_b1, e0_w2, e0_b2, src2, dst2, w_gin, b_gin, bn_w, bn_b, r_w1, r_b1, r_w2, r_b2,
            e1_w1, e1_b1, e1_w2, e1_b2, e1_w3, e1_b3, out):
    V = EX0 * H
    t_msg = nc.dram_tensor("t_msg", [NB * P, 2 * MC], F32).ap()
    t_src = nc.dram_tensor("t_src", [NB * P, V + H], F32).ap()
    t_dst = nc.dram_tensor("t_dst", [NB * P, 2 * H], F32).ap()
    t_hT = nc.dram_tensor("t_hT", [HB, P, KD * W], F32).ap()
    t_y = nc.dram_tensor("t_y", [HB, P, EX0, 2 * D], F32).ap()
    t_edge = nc.dram_tensor("t_edge", [GE * (H + 1)], F32).ap()
    t_row = nc.dram_tensor("t_row", [NB * P, D], F32).ap()
    with ExitStack() as whole:
        g = Mem(nc, whole, "all")
        X = g.sb("X", [P, NB, D])
        rstd = g.sb("rstd", [P, NB])
        nmr = g.sb("nmr", [P, NB])
        ident = g.sb("ident", [P, P])
        tri = g.sb("tri", [P, EX1, EX1])
        wg = g.sb("wg", [P, KD, V + 2 * H])
        gr = Graph(g)

        with ExitStack() as layer:
            a = Mem(nc, layer, "l0g")
            ACC = a.sb("ACC", [P, NB, AC])
            wproj = a.sb("wproj", [P, KD, 2 * MC])
            shift = a.sb("shift", [P, H])
            smax = a.sb("smax", [P, T, H])
            gap = a.sb("gap", [P, H])
            again = a.sb("again", [P, 1], I32)
            again_stray = a.sb("again_stray", [P, 1], I32)
            factors = a.sb("factors", [P, G1 * T, 2])
            with ExitStack() as first:
                f = Mem(nc, first, "prep")
                wf = f.sb("wf", [OF, 2, D])
                attn = f.sb("attn", [OF, H])
                wgat = f.sb("wgat", [P, KD, V])
                att_b = f.sb("att", [P, 2, V])
                prepare(nc, "prep0", gr, src1, dst1, first1, ident, ACC, tri, EX1, [
                    (X[:, :, :], x_in), (wproj[:, :, :], w_msg), (wf[:, :, :], w_rows), (attn[:, :], attn_t),
                    (wgat[:, :, :], w_gat), (att_b[:, :, :], att.partition_broadcast(P)),
                ])
                score_columns(nc, "scols", wf, attn, wproj, wgat, att_b, wg)
            layernorm_stats(nc, "ln0", X, rstd, nmr)
            with ExitStack() as projection:
                msgs = Mem(nc, projection, "msgs").sb("rows", [P, NB, 2 * MC])
                normalize_project(nc, "proj0", X, rstd, nmr, ident, wproj, msgs, 2 * MC, t_msg, None)
                attention_bound(nc, "bound", msgs, attr, factors, shift, smax)
            weigh = Weigh(factors, shift, smax)
            sorted_graph(nc, "att", t_msg, 2 * MC, gr, AC, ACC, weigh)
            stray_edges(nc, "attst", t_msg, 2 * MC, gr, AC, ACC, weigh, gr.stray)
            attention_gap(nc, "gap", gr, shift, smax, gap, again, again_stray)
            zero_sums(nc, "zsums", ACC, again)
            sorted_graph(nc, "atta", t_msg, 2 * MC, gr, AC, ACC, weigh, again)
            stray_edges(nc, "attsta", t_msg, 2 * MC, gr, AC, ACC, weigh, again_stray)
            attention_finish(nc, "attfin", X, ACC, gap)

        with ExitStack() as layer:
            a = Mem(nc, layer, "l0f")
            S = a.sb("S", [P, NB, EX0])
            GT = a.sb("GT", [P, NB, EX0])
            with ExitStack() as part:
                q = Mem(nc, part, "rout")
                AGG = q.sb("AGG", [P, HB, 2, SC])
                small = [q.sb(f"small{k}", [P, V]) for k in range(3)]
                tab = [q.sb(f"tab{k}", [P, 2, HB, 2 * H], F32R) for k in range(2)]
                w1 = [q.sb(f"w1{k}", [P, EX0, KD, F0], F32R) for k in range(2)]
                w2 = q.sb("w2", [P, EX0, M0, D])
                b1 = q.sb("b1", [P, EX0, M0])
                b2 = q.sb("b2", [P, EX0, D])
                with ExitStack() as projection:
                    r = Mem(nc, projection, "rkeep")
                    keep = r.sb("keep", [P, NB, V + 2 * H])
                    best = r.sb("best", [P, NB, H])
                    wide_range = r.sb("wide_range", [P, 1], I32)
                    whole = r.sb("whole", [P, EX0, KD, F0])
                    layernorm_stats(nc, "ln1", X, rstd, nmr, [
                        (small[k][:, :], v.partition_broadcast(P)) for k, v in enumerate((b_gat, gamma, beta))] + [
                        (whole[:, :, :, :], e0_w1), (w2[:, :, :, :], e0_w2), (b1[:, :, :], e0_b1),
                        (b2[:, :, :], e0_b2.partition_broadcast(P))],
                        [tuple(t[:, :, :, :] for t in (whole, *w1))])
                    normalize_project(nc, "proj1", X, rstd, nmr, ident, wg, keep, V + H, t_src, t_hT)
                    source_range(nc, "srange", keep, best, wide_range)
                    segment_max(nc, "segmax", keep, best, t_src, t_edge, src2, dst2, wide_range)
                    routing_tables(nc, "rtab", keep, best, t_dst, tab, AGG)
                routing_with_experts(nc, "rgraph", t_src, t_dst, tab, src2, dst2, gr, ident, AGG, t_hT, t_y,
                                     w1, b1, w2, b2)
                routing_scores(nc, "rscore", AGG, *small, S)
                gates(nc, "gate0", S, GT, EX0, tri)
            add_experts(nc, "addex", X, GT, t_y)

        with ExitStack() as layer:
            a = Mem(nc, layer, "l1g")
            ACC = a.sb("ACC", [P, NB, D])
            wgin = a.sb("w", [P, KD, D])
            b, bnw, bnb = (a.sb(name, [P, D]) for name in ("b", "bn_w", "bn_b"))
            layernorm_stats(nc, "ln2", X, rstd, nmr, [(wgin[:, :, :], w_gin)] + [
                (to[:, :], of.partition_broadcast(P)) for to, of in ((b, b_gin), (bnw, bn_w), (bnb, bn_b))])
            with ExitStack() as projection:
                Z = Mem(nc, projection, "z").sb("rows", [P, NB, D])
                normalize_project(nc, "proj2", X, rstd, nmr, ident, wgin, Z, D, t_row, None, (ACC, b))
            sorted_graph(nc, "gin", t_row, D, gr, D, ACC, None)
            stray_edges(nc, "ginst", t_row, D, gr, D, ACC, None, gr.stray)
            batch_normalized(nc, "bn", X, ACC, gr, bnw, bnb)

        with ExitStack() as layer:
            a = Mem(nc, layer, "l1f")
            GT = a.sb("GT", [P, NB, EX1])
            S = a.sb("S", [P, NB, EX1])
            weights = [[a.sb(f"w{l}{k}", [P, EX1, KD, D], F32R) for k in range(2)] for l in range(3)]
            b1 = a.sb("b1", [P, EX1, KD])
            b2 = a.sb("b2", [P, EX1, KD])
            b3 = a.sb("b3", [P, EX1, D])
            with ExitStack() as routing:
                r = Mem(nc, routing, "l1r")
                rw1 = r.sb("rw1", [P, KD, P])
                rb1 = r.sb("rb1", [P, 1])
                rw2 = r.sb("rw2", [P, EX1])
                rb2 = r.sb("rb2", [P, EX1])
                whole = [r.sb(f"whole{l}", [P, EX1, KD, D]) for l in range(3)]
                layernorm_stats(nc, "ln3", X, rstd, nmr, [
                    (rw1[:, :, :], r_w1), (rb1[:, :], r_b1), (rw2[:, :], r_w2),
                    (rb2[:, :], r_b2.partition_broadcast(P)),
                    (whole[0][:, :, :, :], e1_w1), (whole[1][:, :, :, :], e1_w2), (whole[2][:, :, :, :], e1_w3),
                    (b1[:, :, :], e1_b1), (b2[:, :, :], e1_b2), (b3[:, :, :], e1_b3.partition_broadcast(P))],
                    [tuple(t[:, :, :, :] for t in (whole[l], *weights[l])) for l in range(3)])
                turn_and_route(nc, "route", X, rstd, nmr, ident, t_hT, rw1, rb1, rw2, rb2, S)
            gates(nc, "gate1", S, GT, EX1, tri)
            experts(nc, "ex1", X, t_hT, GT, weights, [b1, b2], b3, out)


def layouts(i, np):
    def blocks(a):
        a = np.concatenate([a, np.zeros((NB * P - N, a.shape[1]), a.dtype)])
        return a.reshape(NB, P, -1).transpose(1, 0, 2)

    def edges(a, groups, pad, extra=0):
        tail = np.repeat(a[-1:] if pad is None else np.full_like(a[-1:], pad), groups * GE - len(a), axis=0)
        a = np.concatenate([a, tail]).reshape((groups, P, T) + a.shape[1:])
        a = np.moveaxis(a, 0, 1).reshape((P, -1))
        return np.concatenate([a, np.zeros((P, extra * T), a.dtype)], axis=1)

    def slices(a):
        a = a.reshape(a.shape[:-2] + (-1, P, a.shape[-1]))
        return np.moveaxis(a, -2, 0)

    def cols(a):
        return np.moveaxis(a.reshape(a.shape[:-1] + (-1, P)), -1, 0)

    src, dst = i["src"], i["dst"]
    wf, wr = i["L0_gnn_W_forward"], i["L0_gnn_W_reverse"]
    gap = np.zeros((D, H), wf.dtype)
    ei = i["L0_ffn_edge_index"]
    firsts = np.concatenate([dst, dst[-1:].repeat(G1 * GE - E1)])[::GE]
    return {
        "x_in": blocks(i["x"]), "src1": edges(src, G1, None, 2), "dst1": edges(dst, G1, -1),
        "first1": firsts, "attr": edges(i["edge_attr_2"], G1, None),
        "w_msg": slices(np.concatenate([wf.T, gap, wr.T, gap], axis=1)),
        "w_rows": np.stack([wf, wr]).transpose(1, 0, 2), "attn_t": i["L0_gnn_attn_forward"][0].T,
        "w_gat": slices(i["L0_ffn_W_gat"]),
        "att": np.stack([i["L0_ffn_att_src"].reshape(-1), i["L0_ffn_att_dst"].reshape(-1)]),
        "b_gat": i["L0_ffn_b_gat"], "gamma": i["L0_ffn_ln_gamma"], "beta": i["L0_ffn_ln_beta"],
        "e0_w1": slices(i["L0_ffn_W1"]), "e0_b1": cols(i["L0_ffn_b1"]),
        "e0_w2": slices(i["L0_ffn_W2"]), "e0_b2": i["L0_ffn_b2"],
        "src2": edges(ei[0], G2, None, 2), "dst2": edges(ei[1], G2, -1, 2),
        "w_gin": slices(i["L1_gnn_W"].T), "b_gin": i["L1_gnn_b"],
        "bn_w": i["L1_gnn_bn_w"], "bn_b": i["L1_gnn_bn_b"],
        "r_w1": slices(i["L1_ffn_router_w1"]), "r_b1": cols(i["L1_ffn_router_b1"]),
        "r_w2": i["L1_ffn_router_w2"], "r_b2": i["L1_ffn_router_b2"],
        "e1_w1": slices(i["L1_ffn_expert_w1"]), "e1_b1": cols(i["L1_ffn_expert_b1"]),
        "e1_w2": slices(i["L1_ffn_expert_w2"]), "e1_b2": cols(i["L1_ffn_expert_b2"]),
        "e1_w3": slices(i["L1_ffn_expert_w3"]), "e1_b3": i["L1_ffn_expert_b3"],
    }


def kernel(**inputs):
    import numpy as np
    import concourse.bacc as bacc
    from concourse.bass_utils import run_bass_kernel_spmd

    nc = bacc.Bacc("TRN2", target_bir_lowering=False, num_devices=1)
    arrays = {k: np.ascontiguousarray(v) for k, v in
              layouts({k: np.asarray(v) for k, v in inputs.items()}, np).items()}
    args = {k: nc.dram_tensor(k, v.shape, mybir.dt.from_np(v.dtype), kind="ExternalInput").ap()
            for k, v in arrays.items()}
    out = nc.dram_tensor("out", (N, D), F32, kind="ExternalOutput").ap()
    gnn_ffn(nc, out=out, **args)
    return run_bass_kernel_spmd(nc, [arrays], core_ids=[0]).results[0]["out"]
```
